# Optimizing a Trainium2 kernel written in Bass

```python
import numpy as np
import jax
import jax.numpy as jnp

def _softmax(x, axis=-1):
    return jax.nn.softmax(x, axis=axis)

def _gelu(x):
    return jax.nn.gelu(x, approximate=True)

def _silu(x):
    return jax.nn.silu(x)

def _sigmoid(x):
    return jax.nn.sigmoid(x)

def _layernorm(x, axis=-1, eps=1e-05):
    m = jnp.mean(x, axis=axis, keepdims=True)
    v = jnp.var(x, axis=axis, keepdims=True)
    return (x - m) / jnp.sqrt(v + eps)

def _scatter_add(tgt, idx, src, axis=0):
    return tgt.at[idx].add(src)

def _segment_sum(src, seg, n):
    return jax.ops.segment_sum(src, seg, n)
kernel_name = 'mk_sandwich_d2_jaxref_r4_659715'

def setup_inputs(seed: int=0):
    np.random.seed(seed)
    _w = jnp.asarray

    def _L0_attn_setup():
        import jax, jax.numpy as jnp
        import numpy as np
        B, T, C = (4, 512, 256)
        N_HEAD = 16
        HEAD = C // N_HEAD
        key = jax.random.key(seed)
        k1, k2, k3 = jax.random.split(key, 3)
        x = jax.random.normal(k1, (B, T, C), dtype=jnp.float32)
        w_attn = jax.random.normal(k2, (C, 3 * C), dtype=jnp.float32) * (1.0 / np.sqrt(C))
        w_proj = jax.random.normal(k3, (C, C), dtype=jnp.float32) * (1.0 / np.sqrt(C))
        return {'x': x, 'w_attn': w_attn, 'w_proj': w_proj}
    _L0_attn_in = _L0_attn_setup()

    def _L0_ffn_setup():
        import jax, jax.numpy as jnp
        import numpy as np
        E, K, H, F = (64, 6, 256, 128)
        SHARED_F = 512
        B, S = (1, 512)
        T = B * S
        CAP = 2 * ((T * K + E - 1) // E)
        key = jax.random.key(seed)
        ks = jax.random.split(key, 6)
        s = 0.05
        return {'hidden_states': jax.random.normal(ks[0], (B, S, H), jnp.float32), 'router_weight': jax.random.normal(ks[1], (E, H), jnp.float32) * s, 'expert_bias': jnp.zeros((E,), jnp.float32), 'w1': jax.random.normal(ks[2], (E, H, F), jnp.float32) * s, 'w2': jax.random.normal(ks[3], (E, F, H), jnp.float32) * s, 'sw1': jax.random.normal(ks[4], (SHARED_F, H), jnp.float32) * s, 'sw2': jax.random.normal(ks[5], (H, SHARED_F), jnp.float32) * s}
    _L0_ffn_in = _L0_ffn_setup()

    def _L1_attn_setup():
        import jax, jax.numpy as jnp
        import numpy as np
        EPS_FEAT = 1.0 + 0.0001
        EPS_DEN = 1e-06

        def _linear_attention(x, W_qkv, b_qkv, W_out, b_out, num_heads=16):
            B, L, D = x.shape
            H = num_heads
            E = D // H
            qkv = x @ W_qkv + b_qkv
            q, k, v = jnp.split(qkv, 3, axis=-1)
            q = q.reshape(B, L, H, E)
            k = k.reshape(B, L, H, E)
            v = v.reshape(B, L, H, E)
            q = jax.nn.elu(q * E ** (-0.5)) + EPS_FEAT
            k = jax.nn.elu(k) + EPS_FEAT
            qL = jnp.moveaxis(q, 1, 0)
            kL = jnp.moveaxis(k, 1, 0)
            vL = jnp.moveaxis(v, 1, 0)
            kv0 = jnp.zeros((B, H, E, E), dtype=x.dtype)
            ks0 = jnp.zeros((B, H, E), dtype=x.dtype)

            def step(carry, qkv_t):
                kv_s, k_s = carry
                q_t, k_t, v_t = qkv_t
                kv_s = kv_s + jnp.einsum('bhe,bhf->bhef', k_t, v_t)
                k_s = k_s + k_t
                num = jnp.einsum('bhe,bhef->bhf', q_t, kv_s)
                den = jnp.einsum('bhe,bhe->bh', q_t, k_s)[..., None] + EPS_DEN
                return ((kv_s, k_s), num / den)
            _, out = jax.lax.scan(step, (kv0, ks0), (qL, kL, vL))
            out = jnp.moveaxis(out, 0, 1).reshape(B, L, D)
            return out @ W_out + b_out
        key = jax.random.key(seed)
        k1, k2, k3 = jax.random.split(key, 3)
        B, L, D = (4, 1024, 256)
        x = jax.random.normal(k1, (B, L, D), dtype=jnp.float32)
        W_qkv = jax.random.normal(k2, (D, 3 * D), dtype=jnp.float32) / np.sqrt(D)
        b_qkv = jnp.zeros((3 * D,), dtype=jnp.float32)
        W_out = jax.random.normal(k3, (D, D), dtype=jnp.float32) / np.sqrt(D)
        b_out = jnp.zeros((D,), dtype=jnp.float32)
        return {'x': x, 'W_qkv': W_qkv, 'b_qkv': b_qkv, 'W_out': W_out, 'b_out': b_out}
    _L1_attn_in = _L1_attn_setup()

    def _L1_ffn_setup():
        import jax, jax.numpy as jnp
        import numpy as np
        K = 4
        ROUTED_SCALING = 1.0
        NORM_TOPK = True

        def _gate(hidden_states, router_w, router_bias):
            logits = jnp.einsum('bsh,he->bse', hidden_states, router_w).astype(jnp.float32)
            scores = jax.nn.softmax(logits, axis=-1)
            corrected = scores + router_bias
            _, top_k_indices = jax.lax.top_k(corrected, K)
            top_k_weights = jnp.take_along_axis(scores, top_k_indices, axis=-1)
            if NORM_TOPK:
                top_k_weights = top_k_weights / (top_k_weights.sum(-1, keepdims=True) + 1e-20)
            top_k_weights = top_k_weights * ROUTED_SCALING
            return (top_k_weights.astype(hidden_states.dtype), top_k_indices)
        key = jax.random.key(seed)
        ks = jax.random.split(key, 9)
        B, S, H, E, I, IS = (2, 256, 256, 8, 128, 512)
        sc = 0.02
        return {'hidden_states': jax.random.normal(ks[0], (B, S, H), jnp.float32), 'router_w': jax.random.normal(ks[1], (H, E), jnp.float32) * sc, 'router_bias': jnp.zeros((), jnp.float32), 'gate_w': jax.random.normal(ks[2], (E, H, I), jnp.float32) * sc, 'up_w': jax.random.normal(ks[3], (E, H, I), jnp.float32) * sc, 'down_w': jax.random.normal(ks[4], (E, I, H), jnp.float32) * sc, 's_gate_w': jax.random.normal(ks[5], (H, IS), jnp.float32) * sc, 's_up_w': jax.random.normal(ks[6], (H, IS), jnp.float32) * sc, 's_down_w': jax.random.normal(ks[7], (IS, H), jnp.float32) * sc}
    _L1_ffn_in = _L1_ffn_setup()
    _d = {'L0_attn_x': _L0_attn_in['x'], 'L0_attn_w_attn': _L0_attn_in['w_attn'], 'L0_attn_w_proj': _L0_attn_in['w_proj'], 'L0_ffn_router_weight': _L0_ffn_in['router_weight'], 'L0_ffn_expert_bias': _L0_ffn_in['expert_bias'], 'L0_ffn_w1': _L0_ffn_in['w1'], 'L0_ffn_w2': _L0_ffn_in['w2'], 'L0_ffn_sw1': _L0_ffn_in['sw1'], 'L0_ffn_sw2': _L0_ffn_in['sw2'], 'L1_attn_W_qkv': _L1_attn_in['W_qkv'], 'L1_attn_b_qkv': _L1_attn_in['b_qkv'], 'L1_attn_W_out': _L1_attn_in['W_out'], 'L1_attn_b_out': _L1_attn_in['b_out'], 'L1_ffn_router_w': _L1_ffn_in['router_w'], 'L1_ffn_router_bias': _L1_ffn_in['router_bias'], 'L1_ffn_gate_w': _L1_ffn_in['gate_w'], 'L1_ffn_up_w': _L1_ffn_in['up_w'], 'L1_ffn_down_w': _L1_ffn_in['down_w'], 'L1_ffn_s_gate_w': _L1_ffn_in['s_gate_w'], 'L1_ffn_s_up_w': _L1_ffn_in['s_up_w'], 'L1_ffn_s_down_w': _L1_ffn_in['s_down_w']}
    _x0 = _d['L0_attn_x']
    _d['L0_attn_x'] = jax.random.normal(jax.random.fold_in(jax.random.key(seed), 1), (8, 1024, 256), dtype=_x0.dtype)
    del _x0
    return _d

def reference(L0_attn_x, L0_attn_w_attn, L0_attn_w_proj, L0_ffn_router_weight, L0_ffn_expert_bias, L0_ffn_w1, L0_ffn_w2, L0_ffn_sw1, L0_ffn_sw2, L1_attn_W_qkv, L1_attn_b_qkv, L1_attn_W_out, L1_attn_b_out, L1_ffn_router_w, L1_ffn_router_bias, L1_ffn_gate_w, L1_ffn_up_w, L1_ffn_down_w, L1_ffn_s_gate_w, L1_ffn_s_up_w, L1_ffn_s_down_w):

    def _L0_attn_ref(x, w_attn, w_proj):
        import jax, jax.numpy as jnp
        import numpy as np
        B, T, C = (4, 512, 256)
        N_HEAD = 16
        HEAD = C // N_HEAD
        b, t, c = x.shape
        qkv = x @ w_attn
        q, k, v = jnp.split(qkv, 3, axis=-1)
        q = q.reshape(b, t, N_HEAD, HEAD).transpose(0, 2, 1, 3)
        k = k.reshape(b, t, N_HEAD, HEAD).transpose(0, 2, 1, 3)
        v = v.reshape(b, t, N_HEAD, HEAD).transpose(0, 2, 1, 3)
        scale = 1.0 / np.sqrt(HEAD).astype(np.float32)
        attn = jnp.einsum('bhqd,bhkd->bhqk', q, k) * scale
        causal = jnp.tril(jnp.ones((t, t), dtype=bool))
        attn = jnp.where(causal[None, None], attn, -jnp.inf)
        sm = jax.nn.softmax(attn, axis=-1)
        out = jnp.einsum('bhqk,bhkd->bhqd', sm, v)
        out = out.transpose(0, 2, 1, 3).reshape(b, t, c)
        return out @ w_proj

    def _L0_ffn_ref(hidden_states, router_weight, expert_bias, w1, w2, sw1, sw2):
        import jax, jax.numpy as jnp
        import numpy as np
        E, K, H, F = (64, 6, 256, 128)
        SHARED_F = 512
        B, S = (1, 512)
        T = B * S
        CAP = 2 * ((T * K + E - 1) // E)
        b, s, h = hidden_states.shape
        x = hidden_states.reshape(-1, h)
        t = x.shape[0]
        logits = x @ router_weight.T
        scores = jax.nn.sigmoid(logits)
        _, top_idx = jax.lax.top_k(scores + expert_bias[None, :], K)
        top_scores = jnp.take_along_axis(scores, top_idx, axis=1)
        probs = top_scores / (jnp.sum(top_scores, axis=-1, keepdims=True) + 1e-20)
        flat_e = top_idx.reshape(-1)
        order = jnp.argsort(flat_e)
        sorted_e = flat_e[order]
        token_of = order // K
        counts = jnp.bincount(flat_e, length=E)
        offsets = jnp.cumsum(counts) - counts
        pos = jnp.arange(t * K) - offsets[sorted_e]
        valid = pos < CAP
        slot = jnp.where(valid, sorted_e * CAP + pos, E * CAP)
        xs = jnp.zeros((E * CAP + 1, h), x.dtype).at[slot].set(x[token_of])
        xs = xs[:-1].reshape(E, CAP, h)
        hmid = jax.nn.gelu(jnp.einsum('ech,ehf->ecf', xs, w1), approximate=True)
        y = jnp.einsum('ecf,efh->ech', hmid, w2).reshape(E * CAP, h)
        pair_w = jnp.where(valid, probs.reshape(-1)[order], 0.0)
        y_pair = y[jnp.minimum(slot, E * CAP - 1)] * pair_w[:, None]
        out = jnp.zeros((t, h), x.dtype).at[token_of].add(y_pair)
        shared = jax.nn.gelu(x @ sw1.T, approximate=True) @ sw2.T
        return (out + shared).reshape(b, s, h)

    def _L1_attn_ref(x, W_qkv, b_qkv, W_out, b_out):
        import jax, jax.numpy as jnp
        import numpy as np
        EPS_FEAT = 1.0 + 0.0001
        EPS_DEN = 1e-06

        def _linear_attention(x, W_qkv, b_qkv, W_out, b_out, num_heads=16):
            B, L, D = x.shape
            H = num_heads
            E = D // H
            qkv = x @ W_qkv + b_qkv
            q, k, v = jnp.split(qkv, 3, axis=-1)
            q = q.reshape(B, L, H, E)
            k = k.reshape(B, L, H, E)
            v = v.reshape(B, L, H, E)
            q = jax.nn.elu(q * E ** (-0.5)) + EPS_FEAT
            k = jax.nn.elu(k) + EPS_FEAT
            qL = jnp.moveaxis(q, 1, 0)
            kL = jnp.moveaxis(k, 1, 0)
            vL = jnp.moveaxis(v, 1, 0)
            kv0 = jnp.zeros((B, H, E, E), dtype=x.dtype)
            ks0 = jnp.zeros((B, H, E), dtype=x.dtype)

            def step(carry, qkv_t):
                kv_s, k_s = carry
                q_t, k_t, v_t = qkv_t
                kv_s = kv_s + jnp.einsum('bhe,bhf->bhef', k_t, v_t)
                k_s = k_s + k_t
                num = jnp.einsum('bhe,bhef->bhf', q_t, kv_s)
                den = jnp.einsum('bhe,bhe->bh', q_t, k_s)[..., None] + EPS_DEN
                return ((kv_s, k_s), num / den)
            _, out = jax.lax.scan(step, (kv0, ks0), (qL, kL, vL))
            out = jnp.moveaxis(out, 0, 1).reshape(B, L, D)
            return out @ W_out + b_out
        return _linear_attention(x, W_qkv, b_qkv, W_out, b_out)

    def _L1_ffn_ref(hidden_states, router_w, router_bias, gate_w, up_w, down_w, s_gate_w, s_up_w, s_down_w):
        import jax, jax.numpy as jnp
        import numpy as np
        K = 4
        ROUTED_SCALING = 1.0
        NORM_TOPK = True

        def _gate(hidden_states, router_w, router_bias):
            logits = jnp.einsum('bsh,he->bse', hidden_states, router_w).astype(jnp.float32)
            scores = jax.nn.softmax(logits, axis=-1)
            corrected = scores + router_bias
            _, top_k_indices = jax.lax.top_k(corrected, K)
            top_k_weights = jnp.take_along_axis(scores, top_k_indices, axis=-1)
            if NORM_TOPK:
                top_k_weights = top_k_weights / (top_k_weights.sum(-1, keepdims=True) + 1e-20)
            top_k_weights = top_k_weights * ROUTED_SCALING
            return (top_k_weights.astype(hidden_states.dtype), top_k_indices)
        B, S, H = hidden_states.shape
        tk_w, tk_i = _gate(hidden_states, router_w, router_bias)
        hf = hidden_states.reshape(-1, H)
        tk_w = tk_w.reshape(-1, K)
        tk_i = tk_i.reshape(-1, K)
        gate_all = jnp.einsum('nh,ehi->nei', hf, gate_w)
        up_all = jnp.einsum('nh,ehi->nei', hf, up_w)
        act = jax.nn.silu(gate_all) * up_all
        down_all = jnp.einsum('nei,eih->neh', act, down_w)
        sel = jnp.take_along_axis(down_all, tk_i[:, :, None], axis=1)
        routed = (sel * tk_w[:, :, None]).sum(axis=1).reshape(B, S, H)
        g = jnp.einsum('bsh,hm->bsm', hidden_states, s_gate_w)
        u = jnp.einsum('bsh,hm->bsm', hidden_states, s_up_w)
        shared = jnp.einsum('bsm,mh->bsh', jax.nn.silu(g) * u, s_down_w)
        return routed + shared
    x = L0_attn_x
    x = x + _layernorm(_L0_attn_ref(_layernorm(x, axis=-1), L0_attn_w_attn, L0_attn_w_proj), axis=-1)
    x = x + _layernorm(_L0_ffn_ref(_layernorm(x, axis=-1), L0_ffn_router_weight, L0_ffn_expert_bias, L0_ffn_w1, L0_ffn_w2, L0_ffn_sw1, L0_ffn_sw2), axis=-1)
    x = x + _layernorm(_L1_attn_ref(_layernorm(x, axis=-1), L1_attn_W_qkv, L1_attn_b_qkv, L1_attn_W_out, L1_attn_b_out), axis=-1)
    x = x + _layernorm(_L1_ffn_ref(_layernorm(x, axis=-1), L1_ffn_router_w, L1_ffn_router_bias, L1_ffn_gate_w, L1_ffn_up_w, L1_ffn_down_w, L1_ffn_s_gate_w, L1_ffn_s_up_w, L1_ffn_s_down_w), axis=-1)
    return x

_drawn_inputs = setup_inputs


def setup_inputs(seed=0):
    import zlib

    import numpy as np

    out = dict(_drawn_inputs(seed))
    spreads = {'L0_ffn_expert_bias': (0.0, 0.1), 'L1_attn_b_qkv': (0.0, 0.1), 'L1_attn_b_out': (0.0, 0.1)}
    factors = {}
    for name, (base, spread) in spreads.items():
        noise = np.random.default_rng([zlib.crc32(name.encode()), seed]).standard_normal(out[name].shape)
        drawn = base * np.exp(spread * noise) if base else spread * noise
        out[name] = jnp.asarray(drawn.astype(out[name].dtype))
    for name, factor in factors.items():
        out[name] = (out[name] * factor).astype(out[name].dtype)
    return out
```

```python
import concourse.bass as bass
from concourse import mybir
from contextlib import ExitStack

fp32 = mybir.dt.float32
f32r = mybir.dt.float32r
bf16 = mybir.dt.bfloat16
u32 = mybir.dt.uint32
i32 = mybir.dt.int32
ALU = mybir.AluOpType
ACT = mybir.ActivationFunctionType
AX = mybir.AxisListType

B, T, C = 8, 1024, 256
N = B * T
NH, HD = 16, 16
P = 128
KC = C // P
BLK = 512
TPB = BLK // P
NBLK = N // BLK
GH = 4
NG = NH // GH
VW = HD + 1
KB = T // P
E0, K0, F0, SF0 = 64, 6, 128, 512
CAP = 2 * ((512 * K0 + E0 - 1) // E0)
E1, K1, F1, SF1 = 8, 4, 128, 512
XW = C + E0
EPS = 1e-5



def take(eng, *pairs):
    for sem, n in pairs:
        eng.sem_inc(sem, -n)


class Phase:

    def __init__(self, nc, name):
        self.nc, self.name, self.ctx, self.sems = nc, name, ExitStack(), []

    def sb(self, name, shape, dt=fp32):
        return self.ctx.enter_context(self.nc.sbuf_tensor(f"{self.name}_{name}", shape, dt))

    def ps(self, name, shape, dt=fp32):
        return self.ctx.enter_context(self.nc.psum_tensor(f"{self.name}_{name}", shape, dt))

    def sem(self, name):
        self.sems.append(self.nc.alloc_semaphore(f"{self.name}_{name}"))
        return self.sems[-1]

    def __enter__(self):
        return self

    def __exit__(self, *a):
        self.nc.clear_and_free_semaphores(self.sems)
        self.nc.all_engine_barrier()
        return self.ctx.__exit__(*a)


def phase_qkv(nc, x_d, w_d, qh_d, ql_d, kh_d, kl_d, v_d):
    with Phase(nc, "qkv") as ph:
        wf = ph.sb("wf", [P, KC, 3 * C])
        wh = ph.sb("wh", [P, KC, 3 * C], f32r)
        wl = ph.sb("wl", [P, KC, 3 * C], f32r)
        ident = ph.sb("ident", [P, P])
        mhalf = ph.sb("mhalf", [P, TPB])
        x = ph.sb("x", [P, 2, TPB, C])
        st = ph.sb("st", [P, TPB, 6])
        mv = ph.sb("mv", [P, TPB, 2])
        ve = ph.sb("ve", [P, TPB])
        rs = ph.sb("rs", [P, TPB])
        xn = ph.sb("xn", [P, TPB, C])
        xh = ph.sb("xh", [P, KC, BLK], f32r)
        xl = ph.sb("xl", [P, KC, BLK], f32r)
        oh = ph.sb("oh", [P, 2, 4, BLK], f32r)
        ol = ph.sb("ol", [P, 2, 4, BLK], f32r)
        vo = ph.sb("vo", [P, 2, TPB, NH, VW])
        tp = ph.ps("tp", [P, KC, BLK])
        qk = ph.ps("qk", [P, 4, BLK])
        vp = ph.ps("vp", [P, 2, 2, C])

        w_loaded = ph.sem("w_loaded")
        w_chain = ph.sem("w_chain")
        w_split = ph.sem("w_split")
        consts = ph.sem("consts")
        x_loaded = [ph.sem(f"x_loaded{j}") for j in range(2)]
        x_free = ph.sem("x_free")
        dve = ph.sem("dve")
        var_ready = ph.sem("var_ready")
        rstd_ready = ph.sem("rstd_ready")
        xn_ready = ph.sem("xn_ready")
        xt_ready = ph.sem("xt_ready")
        xh_ready = ph.sem("xh_ready")
        xhl_ready = ph.sem("xhl_ready")
        xhl_free = ph.sem("xhl_free")
        qk_ready = ph.sem("qk_ready")
        qkh_ready = ph.sem("qkh_ready")
        qkl_ready = ph.sem("qkl_ready")
        qk_free = ph.sem("qk_free")
        v_ready = ph.sem("v_ready")
        v_out = ph.sem("v_out")
        v_free = ph.sem("v_free")
        stored = [ph.sem(f"stored{j}") for j in range(2)]
        STORES = 16 * (4 + TPB)

        x_v = x_d.rearrange("(b j t p) c -> b j p t c", j=2, t=TPB, p=P)
        v_v = v_d.rearrange("(b g j t p) c -> b j t p g c", b=B, g=NG, j=2, t=TPB, p=P)

        def rows(d):
            return d.rearrange("(b c p) (j t) -> b j p c t", b=B, p=P, j=2)

        with nc.Block() as block:
            @block.sync
            def _(e):
                e.dma_start(wf[:], w_d).then_inc(w_loaded, 16)

                def load(b, j):
                    e.dma_start(x[:, j], x_v[b, j]).then_inc(x_loaded[j], 16)

                def store(b, j):
                    for c in range(4):
                        e.wait_ge(qkl_ready, c + 1)
                        e.sem_inc(qk_free, 1)
                    for d, s, c in ((qh_d, oh, 0), (kh_d, oh, 2), (ql_d, ol, 0), (kl_d, ol, 2)):
                        e.dma_start(rows(d)[b, j], s[:, j, c:c + 2].bitcast(fp32)).then_inc(stored[j], 16)
                    e.wait_ge(v_out, 2)
                    e.sem_inc(v_free, 1)
                    for t in range(TPB):
                        e.dma_start(v_v[b, j, t], vo[:, j, t].rearrange("p (g h) d -> p g (h d)", g=NG)
                                    ).then_inc(stored[j], 16)
                    take(e, (qkl_ready, 4), (v_out, 2))

                for j in range(2):
                    load(0, j)
                with e.Fori(0, B - 1) as b:
                    for j in range(2):
                        e.wait_ge(x_free, 1)
                        load(b + 1, j)
                        take(e, (x_free, 1))
                        store(b, j)
                for j in range(2):
                    store(B - 1, j)

            @block.gpsimd
            def _(e):
                e.memset(mhalf[:], -0.5)
                e.memset(vo[:].rearrange("p j t h d -> p (j t h) d")[:, :, HD:VW], 1.0).then_inc(consts, 1)
                e.memset(ident[:], 0.0).then_inc(consts, 1)
                e.wait_ge(consts, 2)
                e.affine_select(out=ident[:], in_=ident[:], compare_op=ALU.not_equal, fill=1.0, base=0,
                                pattern=[[-1, P]], channel_multiplier=1).then_inc(w_split, 1)
                with e.Fori(0, B):
                    for j in range(2):
                        e.wait_ge(var_ready, 1)
                        e.tensor_tensor(rs[:], ve[:], mhalf[:], ALU.pow).then_inc(rstd_ready, 1)
                        take(e, (var_ready, 1))

            @block.vector
            def _(e):
                e.wait_ge(w_loaded, 16)
                e.tensor_scalar(wf[:, :, 0:C], wf[:, :, 0:C], HD ** -0.5, None, ALU.mult).then_inc(w_chain, 1)
                e.wait_ge(w_chain, 1)
                e.tensor_copy(wh[:], wf[:]).then_inc(w_chain, 1)
                e.wait_ge(w_chain, 2)
                e.tensor_tensor(wl[:], wf[:], wh[:].bitcast(fp32), ALU.subtract).then_inc(w_split, 1)
                with e.Fori(0, B):
                    for j in range(2):
                        e.wait_ge(x_loaded[j], 16)
                        for t in range(TPB):
                            e.bn_stats(st[:, t], x[:, j, t]).then_inc(dve, 1)
                        for t in range(TPB):
                            e.wait_ge(dve, t + 1)
                            e.bn_aggr(mv[:, t], st[:, t]).then_inc(dve, 1)
                        e.wait_ge(dve, 2 * TPB)
                        e.tensor_scalar(ve[:], mv[:, :, 1], EPS, None, ALU.add).then_inc(var_ready, 1)
                        e.wait_ge(rstd_ready, 1)
                        for t in range(TPB):
                            e.tensor_scalar(xn[:, t], x[:, j, t], mv[:, t, 0:1], rs[:, t:t + 1],
                                            ALU.subtract, ALU.mult).then_inc(xn_ready, 1)
                        e.wait_ge(xh_ready, 1)
                        e.sem_inc(x_free, 1)
                        e.tensor_tensor(xl[:], tp[:], xh[:].bitcast(fp32), ALU.subtract).then_inc(xhl_ready, 1)
                        for c in range(4):
                            e.wait_ge(qkh_ready, c + 1)
                            e.tensor_tensor(ol[:, j, c], qk[:, c], oh[:, j, c].bitcast(fp32),
                                            ALU.subtract).then_inc(qkl_ready, 1)
                        take(e, (dve, 2 * TPB), (rstd_ready, 1), (x_loaded[j], 16), (xh_ready, 1), (qkh_ready, 4))

            @block.scalar
            def _(e):
                e.sem_inc(stored[0], STORES)
                e.sem_inc(stored[1], STORES)
                e.sem_inc(xhl_free, 1)
                e.wait_ge(consts, 1)
                with e.Fori(0, B):
                    for j in range(2):
                        e.wait_ge(xt_ready, 1)
                        e.wait_ge(xhl_free, 1)
                        e.activation(xh[:], tp[:], ACT.Copy).then_inc(xh_ready, 1)
                        e.wait_ge(stored[j], STORES)
                        for c in range(4):
                            e.wait_ge(qk_ready, c + 1)
                            e.activation(oh[:, j, c], qk[:, c], ACT.Copy).then_inc(qkh_ready, 1)
                        for m in range(2):
                            e.wait_ge(v_ready, m + 1)
                            e.activation(vo[:, j, 2 * m:2 * m + 2, :, 0:HD],
                                         vp[:, m].rearrange("p t (h d) -> p t h d", d=HD),
                                         ACT.Copy).then_inc(v_out, 1)
                        take(e, (xt_ready, 1), (xhl_free, 1), (stored[j], STORES), (qk_ready, 4), (v_ready, 2))
                for j in range(2):
                    e.wait_ge(stored[j], STORES)

            @block.tensor
            def _(e):
                e.sem_inc(qk_free, 4)
                e.sem_inc(v_free, 1)
                e.wait_ge(w_split, 2)
                with e.Fori(0, 2 * B):
                    for t in range(TPB):
                        e.wait_ge(xn_ready, t + 1)
                        for k in range(KC):
                            i = e.transpose(tp[:, k, t * P:(t + 1) * P], xn[:, t, k * P:(k + 1) * P], ident[:])
                    i.then_inc(xt_ready, 1)
                    e.wait_ge(xhl_ready, 1)
                    for c in range(4):
                        e.wait_ge(qk_free, c + 1)
                        terms = [(wa, xa, k) for k in range(KC) for wa, xa in ((wh, xh), (wh, xl), (wl, xh))]
                        for n, (wa, xa, k) in enumerate(terms):
                            i = e.matmul(qk[:, c], wa[:, k, c * P:(c + 1) * P], xa[:, k],
                                         start=n == 0, stop=n == len(terms) - 1)
                        i.then_inc(qk_ready, 1)
                    e.wait_ge(v_free, 1)
                    for t in range(TPB):
                        terms = [(xa, wa, k) for k in range(KC) for xa, wa in ((xh, wh), (xh, wl), (xl, wh))]
                        for n, (xa, wa, k) in enumerate(terms):
                            i = e.matmul(vp[:, t // 2, t % 2], xa[:, k, t * P:(t + 1) * P], wa[:, k, 2 * C:3 * C],
                                         start=n == 0, stop=n == len(terms) - 1)
                        if t == 1:
                            i.then_inc(v_ready, 1)
                        if t == TPB - 1:
                            i.then_inc(xhl_free, 1)
                            e.drain().then_inc(v_ready, 1)
                    take(e, (xn_ready, TPB), (xhl_ready, 1), (qk_free, 4), (v_free, 1))


def phase_softmax_attention(nc, qh_d, ql_d, kh_d, kl_d, v_d, o_d):
    G = B * NG
    NBUF = 3
    SR = 4 * HD
    with Phase(nc, "att") as ph:
        qs = ph.sb("qs", [P, NBUF, GH, T], f32r)
        ks = ph.sb("ks", [P, NBUF, GH, T], f32r)
        vs = ph.sb("vs", [P, NBUF, KB, GH * VW])
        pr = ph.sb("pr", [P, 2, GH, BLK])
        ot = ph.sb("ot", [P, 2, BLK])
        zero = ph.sb("zero", [32, P])
        identf = ph.sb("identf", [P, P])
        identb = ph.sb("identb", [P, P], bf16)
        causal = ph.sb("causal", [P, P], bf16)
        mx = ph.sb("mx", [P, 2, GH, KB])
        nmt = ph.sb("nmt", [32, P], f32r)
        e_ps = ph.ps("e_ps", [P, 2, 2, BLK])
        m_ps = ph.ps("m_ps", [P, 2, BLK])
        o_ps = ph.ps("o_ps", [P, BLK])
        t_ps = ph.ps("t_ps", [32, P])

        consts = ph.sem("consts")
        consts_pe = ph.sem("consts_pe")
        const_chain = ph.sem("const_chain")
        stack_loaded = [ph.sem(f"stack_loaded{j}") for j in range(NBUF)]
        m_scores = ph.sem("m_scores")
        m_free = ph.sem("m_free")
        pieces_done = ph.sem("pieces_done")
        max_ready = ph.sem("max_ready")
        maxt_ready = ph.sem("maxt_ready")
        nmt_ready = ph.sem("nmt_ready")
        mrow_loaded = ph.sem("mrow_loaded")
        e_scores = ph.sem("e_scores")
        exp_done = ph.sem("exp_done")
        mask_due = ph.sem("mask_due")
        exp_relayed = ph.sem("exp_relayed")
        masked = ph.sem("masked")
        pv_done = ph.sem("pv_done")
        ot_ready = ph.sem("ot_ready")
        o_free = ph.sem("o_free")
        ot_stored = [ph.sem(f"ot_stored{j}") for j in range(2)]
        LOADS = 16 * 10
        LOOPS = G // NBUF

        steps = [(h, k, p) for h in range(2) for k in range(4 * h + 4) for p in range(2)]
        pieces = [(q, h, n) for q in range(KB) for h in range(q // 4 + 1) for n in range(GH)]
        MSTEPS = 20

        def width(h, k):
            return BLK - max(0, k * P - h * BLK)

        def diagonal(s):
            h, k, p = steps[s]
            return k * P >= h * BLK

        def share(s):
            n = len(pieces)
            return range(n * min(s, MSTEPS) // MSTEPS, n * min(s + 1, MSTEPS) // MSTEPS)

        def nth(s):
            return sum(diagonal(r) == diagonal(s) for r in range(s + 1))

        NDIAG = sum(diagonal(s) for s in range(len(steps)))
        NFULL = len(steps) - NDIAG
        UNITS = len(steps) // 2
        src_rows = {n: d.rearrange("(g h d) t -> g d h t", h=GH, d=HD)
                    for n, d in (("qh", qh_d), ("ql", ql_d), ("kh", kh_d), ("kl", kl_d))}
        v_rows = v_d.rearrange("(g k p) c -> g p k c", k=KB, p=P)
        o_rows = o_d.rearrange("(g p) (h t) -> g h p t", p=P, h=2)

        with nc.Block() as block:
            @block.sync
            def _(e):
                def maxima_row(j):
                    return qs[SR:SR + 1, j].bitcast(fp32).rearrange("o h (k p) -> o (h k) p", p=P)

                def load(g, j):
                    for name, dst, parts in (("qh", qs, (0, 1)), ("ql", qs, (2, 3)),
                                             ("kh", ks, (0, 2)), ("kl", ks, (1, 3))):
                        for r in parts:
                            e.dma_start(dst[r * HD:(r + 1) * HD, j].bitcast(fp32), src_rows[name][g]
                                        ).then_inc(stack_loaded[j], 16)
                    e.dma_start(vs[:, j], v_rows[g]).then_inc(stack_loaded[j], 16)
                    e.dma_start(maxima_row(j), zero[:]).then_inc(stack_loaded[j], 16)

                def row(j):
                    e.wait_ge(nmt_ready, 1)
                    e.dma_start(maxima_row(j), nmt[:].bitcast(fp32)).then_inc(mrow_loaded, 16)
                    take(e, (nmt_ready, 1))

                def outputs(g, j, more):
                    for h in range(2):
                        e.wait_ge(ot_ready, h + 1)
                        e.sem_inc(o_free, 1)
                        e.dma_start(o_rows[g, h], ot[:, h]).then_inc(ot_stored[h], 16)
                        if h == 0 and more:
                            row((j + 1) % NBUF)
                    take(e, (ot_ready, 2))

                e.wait_ge(consts, 1)
                for j in range(NBUF):
                    load(j, j)
                row(0)
                with e.Fori(0, LOOPS - 1) as i:
                    for j in range(NBUF):
                        outputs(NBUF * i + j, j, True)
                        load(NBUF * i + j + NBUF, j)
                for g in range(NBUF * (LOOPS - 1), G):
                    outputs(g, g % NBUF, g < G - 1)
                    if g + NBUF < G:
                        load(g + NBUF, g % NBUF)

            @block.gpsimd
            def _(e):
                e.memset(zero[:], 0.0).then_inc(const_chain, 1)
                e.memset(identf[:], 0.0).then_inc(const_chain, 1)
                e.memset(causal[:], 0.0).then_inc(const_chain, 1)
                e.wait_ge(const_chain, 3)
                e.affine_select(out=causal[:], in_=causal[:], compare_op=ALU.is_ge, fill=-1e30, base=0,
                                pattern=[[-1, P]], channel_multiplier=1).then_inc(consts_pe, 1)
                e.affine_select(out=identf[:], in_=identf[:], compare_op=ALU.not_equal, fill=1.0, base=0,
                                pattern=[[-1, P]], channel_multiplier=1).then_inc(const_chain, 1)
                e.wait_ge(const_chain, 4)
                e.tensor_copy(identb[:], identf[:]).then_inc(const_chain, 1)
                e.wait_ge(const_chain, 5)
                e.sem_inc(consts_pe, 1)
                e.memset(qs[SR:P].bitcast(fp32), 0.0).then_inc(consts, 1)
                with e.Fori(0, G):
                    for s, (h, k, p) in enumerate(steps):
                        if diagonal(s):
                            e.wait_ge(mask_due, nth(s))
                            e.sem_inc(exp_relayed, 1)
                            blk = pr[:, k % 2, 2 * p:2 * p + 2, 0:P]
                            e.affine_select(out=blk, in_=blk, compare_op=ALU.is_ge, fill=0.0, base=0,
                                            pattern=[[0, 2], [1, P]], channel_multiplier=-1).then_inc(masked, 1)
                    take(e, (mask_due, NDIAG))

            @block.vector
            def _(e):
                e.memset(o_ps[:], 0.0).then_inc(consts_pe, 1)
                e.memset(ks[SR:P].bitcast(fp32), 0.0).then_inc(pieces_done, 1)
                e.wait_ge(pieces_done, 1)
                take(e, (pieces_done, 1))
                e.memset(ks[SR:SR + 1].bitcast(fp32), 1.0).then_inc(consts_pe, 1)
                with e.Fori(0, G):
                    for n, (q, h, hd) in enumerate(pieces):
                        w = min(BLK, (q + 1) * P - h * BLK)
                        e.wait_ge(m_scores, n + 1)
                        i = e.reduce_max(mx[:, h, hd, q:q + 1], m_ps[:, n % 2, 0:w], AX.X)
                        i.then_inc(m_free, 1)
                    e.drain().then_inc(pieces_done, 1)
                    e.wait_ge(pieces_done, 1)
                    e.tensor_tensor(mx[:, 0, :, 4:8], mx[:, 0, :, 4:8], mx[:, 1, :, 4:8], ALU.max
                                    ).then_inc(max_ready, 1)
                    take(e, (m_scores, len(pieces)), (pieces_done, 1))

            @block.scalar
            def _(e):
                def maxima():
                    e.wait_ge(maxt_ready, 1)
                    e.activation(nmt[:], t_ps[:], ACT.Copy, scale=-1.0).then_inc(nmt_ready, 1)
                    take(e, (maxt_ready, 1))

                def outputs(h):
                    e.wait_ge(pv_done, 4 + 8 * h)
                    e.wait_ge(ot_stored[h], 16)
                    e.activation(ot[:, h], o_ps[:], ACT.Copy).then_inc(ot_ready, 1)
                    take(e, (ot_stored[h], 16))

                def group(more):
                    for s, (h, k, p) in enumerate(steps):
                        w, u = width(h, k), s // 2
                        if p == 0 and u >= 2:
                            e.wait_ge(pv_done, u - 1)
                        e.wait_ge(e_scores, s + 1)
                        i = e.activation(pr[:, k % 2, 2 * p:2 * p + 2, 0:w], e_ps[:, s % 2, :, 0:w], ACT.Exp)
                        i.then_inc(mask_due if diagonal(s) else exp_done, 1)
                        if u == 4 and p == 1:
                            outputs(0)
                        if s == MSTEPS + 2 and more:
                            maxima()
                    outputs(1)
                    take(e, (pv_done, UNITS), (e_scores, len(steps)))

                for h in range(2):
                    e.sem_inc(ot_stored[h], 16)
                maxima()
                with e.Fori(0, G - 1):
                    group(True)
                group(False)
                for h in range(2):
                    e.wait_ge(ot_stored[h], 16)

            @block.tensor
            def _(e):
                def piece(j, n):
                    q, h, hd = pieces[n]
                    w = min(BLK, (q + 1) * P - h * BLK)
                    diag = h == q // 4
                    if n >= 2:
                        e.wait_ge(m_free, n - 1)
                    i = e.matmul(m_ps[:, n % 2, 0:w], qs[:, j, hd, q * P:(q + 1) * P],
                                 ks[:, j, hd, h * BLK:h * BLK + w], start=True, stop=not diag)
                    if diag:
                        i = e.matmul(m_ps[:, n % 2, w - P:w], identb[:], causal[:], start=False, stop=True)
                    i.then_inc(m_scores, 1)

                def maxima():
                    e.wait_ge(max_ready, 1)
                    e.transpose(t_ps[:], mx[:, 0].rearrange("p h k -> p (h k)"), identf[:]).then_inc(maxt_ready, 1)
                    take(e, (max_ready, 1), (m_free, len(pieces)))

                def scores(j, s):
                    h, k, p = steps[s]
                    w = width(h, k)
                    if s >= 2:
                        e.wait_ge(exp_relayed if diagonal(s - 2) else exp_done, nth(s - 2))
                    for n in range(2):
                        hd = 2 * p + n
                        i = e.matmul(e_ps[:, s % 2, n, 0:w], ks[:, j, hd, k * P:(k + 1) * P],
                                     qs[:, j, hd, (h + 1) * BLK - w:(h + 1) * BLK], start=True, stop=True)
                    i.then_inc(e_scores, 1)

                def products(j, u):
                    h, k, _ = steps[2 * u]
                    w = width(h, k)
                    s = 2 * u + 1
                    e.wait_ge(masked if diagonal(s) else exp_done, nth(s))
                    if k == 0:
                        e.wait_ge(o_free, 1)
                        take(e, (o_free, 1))
                    for hd in range(GH):
                        i = e.matmul(o_ps[32 * hd:32 * hd + VW, BLK - w:BLK], vs[:, j, k, hd * VW:(hd + 1) * VW],
                                     pr[:, k % 2, hd, 0:w], start=k == 0, stop=k == 4 * h + 3)
                    i.then_inc(pv_done, 1)

                def group(j, more):
                    e.wait_ge(mrow_loaded, 16)
                    take(e, (mrow_loaded, 16))
                    nxt = (j + 1) % NBUF
                    if more:
                        e.wait_ge(stack_loaded[nxt], LOADS)
                        take(e, (stack_loaded[nxt], LOADS))
                    for s in range(len(steps)):
                        scores(j, s)
                        if more:
                            for n in share(s):
                                piece(nxt, n)
                            if s == MSTEPS + 1:
                                maxima()
                        if s % 2 and s > 1:
                            products(j, s // 2 - 1)
                    products(j, UNITS - 1)
                    take(e, (exp_relayed, NDIAG), (masked, NDIAG), (exp_done, NFULL))

                e.sem_inc(o_free, 1)
                e.wait_ge(consts_pe, 4)
                e.wait_ge(stack_loaded[0], LOADS)
                take(e, (stack_loaded[0], LOADS))
                for n in range(len(pieces)):
                    piece(0, n)
                maxima()
                with e.Fori(0, LOOPS):
                    for j in range(NBUF):
                        group(j, True)
                for g in range(NBUF * LOOPS, G):
                    group(g % NBUF, g < G - 1)


class Chain:

    def __init__(self, eng, sem):
        self.eng, self.sem, self.n = eng, sem, 0

    def __call__(self, ins):
        ins.then_inc(self.sem, 1)
        self.n += 1
        self.eng.wait_ge(self.sem, self.n)

    def settle(self):
        self(self.eng.drain())

    def close(self):
        take(self.eng, (self.sem, self.n))
        self.n = 0


def identity(e, step, ident):
    step(e.memset(ident[:], 0.0))
    step(e.affine_select(out=ident[:], in_=ident[:], compare_op=ALU.not_equal, fill=1.0, base=0,
                         pattern=[[-1, ident.shape[0]]], channel_multiplier=1))


def split_weights(e, step, wf, wh, wl):
    step(e.tensor_copy(wh[:], wf[:]))
    step(e.tensor_tensor(wl[:], wf[:], wh[:].bitcast(fp32), ALU.subtract))


def parts3(ah, al, bh, bl):
    return ((ah, bh), (ah, bl), (al, bh))


def product(e, out, lhs, rhs, n_k, first=True, last=True, **kw):
    terms = [(a(k), b(k)) for k in range(n_k) for a, b in parts3(lhs[0], lhs[1], rhs[0], rhs[1])]
    for n, (a, b) in enumerate(terms):
        i = e.matmul(out, a, b, start=first and n == 0, stop=last and n == len(terms) - 1, **kw)
    return i


def variance(e, step, src, st, mv, ve, var_ready):
    for t in range(TPB):
        e.bn_stats(st[:, t], src[:, t])
    step.settle()
    for t in range(TPB):
        e.bn_aggr(mv[:, t], st[:, t])
    step.settle()
    e.tensor_scalar(ve[:], mv[:, :, 1], EPS, None, ALU.add).then_inc(var_ready, 1)


def scaling(e, mv, rs, nmr, rstd_ready, signal):
    e.wait_ge(rstd_ready, 1)
    e.scalar_tensor_tensor(nmr[:], mv[:, :, 0], -1.0, rs[:], ALU.mult, ALU.mult).then_inc(signal, 1)
    take(e, (rstd_ready, 1))


def pipeline(e, stages):
    last = 2 * B - 1

    def blocks(n):
        return [((n - s) // 2, (n - s) % 2) if 0 <= n - s <= last else None for s in range(4)]

    for n in (0, 1, 2, 3):
        stages(*blocks(n))
    with e.Fori(2, B) as i:
        stages((i, 0), (i - 1, 1), (i - 1, 0), (i - 2, 1))
        stages((i, 1), (i, 0), (i - 1, 1), (i - 1, 0))
    for n in (last + 1, last + 2, last + 3):
        stages(*blocks(n))


def phase_project_route(nc, layer, o_d, x_d, wp_d, rw_d, rb_d, yb_d, xo_d, xh_d, xl_d, xg_d, rt_d):
    E, K, NB = (E0, K0, E0) if layer == 0 else (E1, K1, 1)
    with Phase(nc, f"prj{layer}") as ph:
        wf = ph.sb("wf", [P, KC, C + E])
        wh = ph.sb("wh", [P, KC, C + E], f32r)
        wl = ph.sb("wl", [P, KC, C + E], f32r)
        rbias = ph.sb("rbias", [P, NB])
        ident = ph.sb("ident", [P, P])
        mhalf = ph.sb("mhalf", [P, TPB])
        o = ph.sb("o", [P, 2, NG, BLK])
        x = ph.sb("x", [P, 2, TPB, C])
        den = ph.sb("den", [P, NH])
        rden = ph.sb("rden", [P, TPB, NH])
        att = ph.sb("att", [P, TPB, C])
        ah = ph.sb("ah", [P, KC, BLK], f32r)
        al = ph.sb("al", [P, KC, BLK], f32r)
        st = ph.sb("st", [P, 2, TPB, 6])
        mv = ph.sb("mv", [P, 2, TPB, 2])
        ve = ph.sb("ve", [P, 2, TPB])
        rs = ph.sb("rs", [P, 2, TPB])
        nmr = ph.sb("nmr", [P, 2, TPB])
        yn = ph.sb("yn", [P, TPB, C])
        xo = ph.sb("xo", [P, 2, TPB, C])
        xn = ph.sb("xn", [P, 2, TPB, XW])
        xh = ph.sb("xh", [P, 2, KC, BLK], f32r)
        xl = ph.sb("xl", [P, 2, KC, BLK], f32r)
        sc = ph.sb("sc", [P, TPB, E])
        sb = ph.sb("sb", [P, TPB, E + 8 - K])
        rep = ph.sb("rep", [P, TPB, E + 8 - K])
        top = ph.sb("top", [P, TPB, 8])
        pick = ph.sb("pick", [P, TPB, 8])
        mask = ph.sb("mask", [P, TPB, E])
        ssum = ph.sb("ssum", [P, TPB])
        rt = ph.sb("rt", [E, 2, BLK])
        o_ps = ph.ps("o_ps", [P, 2, NG, P])
        t_ps = ph.ps("t_ps", [P, KC, BLK])
        y_ps = ph.ps("y_ps", [P, TPB, C])
        l_ps = ph.ps("l_ps", [P, TPB, E])
        r_ps = ph.ps("r_ps", [E, BLK])
        if layer == 1:
            ybias = ph.sb("ybias", [P, C])
            y = ph.sb("y", [P, TPB, C])
            ls = ph.sb("ls", [P, TPB, E])
            lmax = ph.sb("lmax", [P, TPB])
            shifted = ph.sem("shifted")
        else:
            y = y_ps

        w_loaded = ph.sem("w_loaded")
        pe_consts = ph.sem("pe_consts")
        pool_chain = ph.sem("pool_chain")
        dve_chain = ph.sem("dve_chain")
        o_loaded = [ph.sem(f"o_loaded{j}") for j in range(2)]
        x_loaded = [ph.sem(f"x_loaded{j}") for j in range(2)]
        o_free = ph.sem("o_free")
        o_turned = ph.sem("o_turned")
        att_ready = ph.sem("att_ready")
        att_turned = ph.sem("att_turned")
        ah_ready = ph.sem("ah_ready")
        al_ready = ph.sem("al_ready")
        y_ready = ph.sem("y_ready")
        y_free = ph.sem("y_free")
        yvar_ready = ph.sem("yvar_ready")
        yrstd_ready = ph.sem("yrstd_ready")
        y_scale = ph.sem("y_scale")
        yn_ready = ph.sem("yn_ready")
        xvar_ready = ph.sem("xvar_ready")
        xrstd_ready = ph.sem("xrstd_ready")
        x_scale = ph.sem("x_scale")
        xn_ready = ph.sem("xn_ready")
        xn_turned = ph.sem("xn_turned")
        xh_ready = ph.sem("xh_ready")
        xl_ready = ph.sem("xl_ready")
        xhl_relayed = ph.sem("xhl_relayed")
        logits = ph.sem("logits")
        scores = ph.sem("scores")
        choice_ready = ph.sem("choice_ready")
        choice_turned = ph.sem("choice_turned")
        rt_ready = ph.sem("rt_ready")
        weights_ready = ph.sem("weights_ready")
        x_stored = [ph.sem(f"x_stored{j}") for j in range(2)]
        r_stored = [ph.sem(f"r_stored{j}") for j in range(2)]
        X_STORES = 16 * 3
        R_STORES = 16 * (2 if layer == 0 else 1)

        def tiles(d):
            return d.rearrange("(b j t p) c -> b j p t c", j=2, t=TPB, p=P)

        def turned(d):
            return d.rearrange("(b c p) (j t) -> b j p c t", b=B, p=P, j=2)

        o_rows = o_d.rearrange("(b g p) (j t) -> b j p g t", b=B, p=P, j=2)
        r_rows = rt_d.rearrange("e (b j t) -> b j e t", b=B, j=2)

        with nc.Block() as block:
            @block.sync
            def _(e):
                def load_o(b, j):
                    e.dma_start(o[:, j], o_rows[b, j]).then_inc(o_loaded[j], 16)

                def load_x(b, j):
                    e.dma_start(x[:, j], tiles(x_d)[b, j]).then_inc(x_loaded[j], 16)

                def stages(a, b, c, d, loads=True):
                    if a is not None:
                        e.wait_ge(o_free, 1)
                        if loads:
                            load_o(a[0] + 1, a[1])
                        take(e, (o_free, 1))
                    if d is not None:
                        if layer == 0:
                            e.wait_ge(weights_ready, 1)
                            e.dma_start(tiles(xg_d[0:N])[d[0], d[1]], xn[:, d[1]]).then_inc(r_stored[d[1]], 16)
                            take(e, (weights_ready, 1))
                        e.wait_ge(rt_ready, 1)
                        e.dma_start(r_rows[d[0], d[1]], rt[:, d[1]]).then_inc(r_stored[d[1]], 16)
                        take(e, (rt_ready, 1))
                    if c is not None:
                        j = c[1]
                        e.wait_ge(xl_ready, 1)
                        e.sem_inc(xhl_relayed, 1)
                        e.dma_start(turned(xh_d)[c[0], j], xh[:, j].bitcast(fp32)).then_inc(x_stored[j], 16)
                        e.dma_start(turned(xl_d)[c[0], j], xl[:, j].bitcast(fp32)).then_inc(x_stored[j], 16)
                        e.dma_start(tiles(xo_d)[c[0], j], xo[:, j]).then_inc(x_stored[j], 16)
                        if a is not None:
                            load_x(a[0], a[1])
                        take(e, (xl_ready, 1))

                e.dma_start(wf[:, :, 0:C], wp_d).then_inc(w_loaded, 16)
                e.dma_start(wf[:, :, C:C + E], rw_d).then_inc(w_loaded, 16)
                e.dma_start(rbias[:], rb_d.rearrange("(o n) -> o n", o=1).broadcast_to((P, NB))).then_inc(w_loaded, 16)
                if layer == 1:
                    e.dma_start(ybias[:], yb_d.rearrange("(o n) -> o n", o=1).broadcast_to((P, C))
                                ).then_inc(w_loaded, 16)
                for j in range(2):
                    load_o(0, j)
                for j in range(2):
                    load_x(0, j)
                stages((0, 0), None, None, None)
                stages((0, 1), (0, 0), None, None)
                stages((1, 0), (0, 1), (0, 0), None)
                stages((1, 1), (1, 0), (0, 1), (0, 0))
                with e.Fori(2, B - 1) as i:
                    stages((i, 0), (i - 1, 1), (i - 1, 0), (i - 2, 1))
                    stages((i, 1), (i, 0), (i - 1, 1), (i - 1, 0))
                stages((B - 1, 0), (B - 2, 1), (B - 2, 0), (B - 3, 1), False)
                stages((B - 1, 1), (B - 1, 0), (B - 2, 1), (B - 2, 0), False)
                stages(None, (B - 1, 1), (B - 1, 0), (B - 2, 1))
                stages(None, None, (B - 1, 1), (B - 1, 0))
                stages(None, None, None, (B - 1, 1))

            @block.gpsimd
            def _(e):
                step = Chain(e, pool_chain)
                identity(e, step, ident)
                step(e.memset(mhalf[:], -0.5))
                e.sem_inc(pe_consts, 1)
                step.close()

                def stages(a, b, c, d):
                    if c is not None:
                        e.wait_ge(xvar_ready, 1)
                        e.tensor_tensor(rs[:, 1], ve[:, 1], mhalf[:], ALU.pow).then_inc(xrstd_ready, 1)
                        take(e, (xvar_ready, 1))
                    if b is not None:
                        e.wait_ge(yvar_ready, 1)
                        e.tensor_tensor(rs[:, 0], ve[:, 0], mhalf[:], ALU.pow).then_inc(yrstd_ready, 1)
                        take(e, (yvar_ready, 1))

                pipeline(e, stages)

            @block.vector
            def _(e):
                step = Chain(e, dve_chain)
                e.wait_ge(w_loaded, 48 if layer == 0 else 64)
                split_weights(e, step, wf, wh, wl)
                step(e.memset(sb[:, :, E:E + 8 - K], 3e38))
                step(e.memset(pick[:, :, K:8], 3e38))
                e.sem_inc(pe_consts, 1)
                step.close()

                def residual(j):
                    e.wait_ge(x_loaded[j], 16)
                    e.wait_ge(yn_ready, 1)
                    e.sem_inc(y_free, 1)
                    step(e.tensor_tensor(xo[:, j], x[:, j], yn[:], ALU.add))
                    variance(e, step, xo[:, j], st[:, 1], mv[:, 1], ve[:, 1], xvar_ready)
                    take(e, (x_loaded[j], 16), (yn_ready, 1))

                def projected():
                    e.wait_ge(y_ready, 1)
                    if layer == 1:
                        step(e.tensor_tensor(y[:], y_ps[:], ybias[:].unsqueeze(1).broadcast_to((P, TPB, C)), ALU.add))
                    variance(e, step, y, st[:, 0], mv[:, 0], ve[:, 0], yvar_ready)
                    take(e, (y_ready, 1))

                def divide():
                    for t in range(TPB):
                        e.wait_ge(o_turned, t + 1)
                        heads = o_ps[:, t % 2].rearrange("p g (h d) -> p (g h) d", d=32)
                        if layer == 0:
                            step(e.reciprocal(rden[:, t], heads[:, :, HD]))
                        else:
                            step(e.tensor_scalar(den[:], heads[:, :, HD], 1e-6, None, ALU.add))
                            step(e.reciprocal(rden[:, t], den[:]))
                        e.tensor_tensor(att[:, t].rearrange("p (h d) -> p h d", d=HD), heads[:, :, 0:HD],
                                        rden[:, t].unsqueeze(2).broadcast_to((P, NH, HD)), ALU.mult
                                        ).then_inc(att_ready, 1)
                    take(e, (o_turned, TPB))

                def softmax_shift():
                    e.wait_ge(logits, 1)
                    step(e.reduce_max(lmax[:], l_ps[:], AX.X))
                    e.tensor_tensor(ls[:], l_ps[:], lmax[:].unsqueeze(2).broadcast_to((P, TPB, E)), ALU.subtract
                                    ).then_inc(shifted, 1)
                    take(e, (logits, 1))

                def choose(j):
                    e.wait_ge(scores, 1)
                    if layer == 1:
                        step(e.reduce_sum(ssum[:], sc[:], AX.X))
                        step(e.reciprocal(ssum[:], ssum[:]))
                        step(e.tensor_tensor(sc[:], sc[:], ssum[:].unsqueeze(2).broadcast_to((P, TPB, E)), ALU.mult))
                    step(e.tensor_tensor(sb[:, :, 0:E], sc[:], rbias[:].unsqueeze(1).broadcast_to((P, TPB, E)),
                                         ALU.add))
                    for t in range(TPB):
                        e.max(top[:, t], sb[:, t, 0:E])
                    step.settle()
                    step(e.tensor_copy(pick[:, :, 0:K], top[:, :, 0:K]))
                    for t in range(TPB):
                        e.match_replace(rep[:, t], pick[:, t], sb[:, t], -3e38)
                    step.settle()
                    choice = e.tensor_scalar(mask[:], rep[:, :, 0:E], -1e38, None, ALU.is_lt)
                    if layer == 0:
                        choice.then_inc(choice_ready, 1)
                        step.settle()
                    else:
                        step(choice)
                    step(e.tensor_tensor(sc[:], sc[:], mask[:], ALU.mult))
                    step(e.reduce_sum(ssum[:], sc[:], AX.X))
                    step(e.tensor_scalar(ssum[:], ssum[:], 1e-20, None, ALU.add))
                    step(e.reciprocal(ssum[:], ssum[:]))
                    weights = xn[:, j, :, C:XW] if layer == 0 else mask[:]
                    e.tensor_tensor(weights, sc[:], ssum[:].unsqueeze(2).broadcast_to((P, TPB, E)), ALU.mult
                                    ).then_inc(weights_ready if layer == 0 else choice_ready, 1)
                    take(e, (scores, 1))

                def stages(a, b, c, d):
                    if c is not None:
                        residual(c[1])
                    if b is not None:
                        projected()
                    if c is not None:
                        scaling(e, mv[:, 1], rs[:, 1], nmr[:, 1], xrstd_ready, x_scale)
                    if a is not None:
                        divide()
                    if b is not None:
                        scaling(e, mv[:, 0], rs[:, 0], nmr[:, 0], yrstd_ready, y_scale)
                    if layer == 1 and d is not None:
                        softmax_shift()
                    if d is not None:
                        choose(d[1])
                    if a is not None:
                        e.wait_ge(ah_ready, 1)
                        e.tensor_tensor(al[:], t_ps[:], ah[:].bitcast(fp32), ALU.subtract).then_inc(al_ready, 1)
                        take(e, (ah_ready, 1))
                    if c is not None:
                        e.wait_ge(xh_ready, 1)
                        e.tensor_tensor(xl[:, c[1]], t_ps[:], xh[:, c[1]].bitcast(fp32), ALU.subtract
                                        ).then_inc(xl_ready, 1)
                        take(e, (xh_ready, 1))
                    step.close()

                pipeline(e, stages)

            @block.scalar
            def _(e):
                for j in range(2):
                    e.sem_inc(x_stored[j], X_STORES)
                    e.sem_inc(r_stored[j], R_STORES)

                def stages(a, b, c, d):
                    if c is not None:
                        j = c[1]
                        e.wait_ge(r_stored[j], R_STORES)
                        e.wait_ge(x_scale, 1)
                        for t in range(TPB):
                            e.activation(xn[:, j, t, 0:C], xo[:, j, t], ACT.Identity, bias=nmr[:, 1, t:t + 1],
                                         scale=rs[:, 1, t:t + 1]).then_inc(xn_ready, 1)
                        take(e, (r_stored[j], R_STORES), (x_scale, 1))
                    if b is not None:
                        j = b[1]
                        e.wait_ge(x_stored[j], X_STORES)
                        e.wait_ge(y_scale, 1)
                        for t in range(TPB):
                            i = e.activation(yn[:, t], y[:, t], ACT.Identity, bias=nmr[:, 0, t:t + 1],
                                             scale=rs[:, 0, t:t + 1])
                        i.then_inc(yn_ready, 1)
                        take(e, (x_stored[j], X_STORES), (y_scale, 1))
                    if d is not None:
                        if layer == 0:
                            e.wait_ge(logits, 1)
                            e.activation(sc[:], l_ps[:], ACT.Sigmoid).then_inc(scores, 1)
                            take(e, (logits, 1))
                        else:
                            e.wait_ge(shifted, 1)
                            e.activation(sc[:], ls[:], ACT.Exp).then_inc(scores, 1)
                            take(e, (shifted, 1))
                    if a is not None:
                        e.wait_ge(att_turned, 1)
                        e.activation(ah[:], t_ps[:], ACT.Copy).then_inc(ah_ready, 1)
                        take(e, (att_turned, 1))
                    if c is not None:
                        e.wait_ge(xn_turned, 1)
                        e.activation(xh[:, c[1]], t_ps[:], ACT.Copy).then_inc(xh_ready, 1)
                        take(e, (xn_turned, 1))
                    if d is not None:
                        e.wait_ge(choice_turned, 1)
                        e.activation(rt[:, d[1]], r_ps[:], ACT.Copy).then_inc(rt_ready, 1)
                        take(e, (choice_turned, 1))

                pipeline(e, stages)
                for j in range(2):
                    e.wait_ge(x_stored[j], X_STORES)
                    e.wait_ge(r_stored[j], R_STORES)

            @block.tensor
            def _(e):
                e.wait_ge(pe_consts, 2)
                e.sem_inc(y_free, 1)

                def turn(src, ready):
                    for t in range(TPB):
                        e.wait_ge(ready, t + 1)
                        for k in range(KC):
                            i = e.transpose(t_ps[:, k, t * P:(t + 1) * P], src[:, t, k * P:(k + 1) * P], ident[:])
                    return i

                def stages(a, b, c, d):
                    if b is not None:
                        e.wait_ge(al_ready, 1)
                        e.wait_ge(y_free, 1)
                        for t in range(TPB):
                            cols = slice(t * P, (t + 1) * P)
                            i = product(e, y_ps[:, t], (lambda k: ah[:, k, cols], lambda k: al[:, k, cols]),
                                        (lambda k: wh[:, k, 0:C], lambda k: wl[:, k, 0:C]), KC)
                        i.then_inc(y_ready, 1)
                        take(e, (al_ready, 1), (y_free, 1))
                    if a is not None:
                        e.wait_ge(o_loaded[a[1]], 16)
                        for t in range(TPB):
                            if t >= 2:
                                e.wait_ge(att_ready, t - 1)
                            for g in range(NG):
                                i = e.transpose(o_ps[:, t % 2, g], o[:, a[1], g, t * P:(t + 1) * P], ident[:])
                            i.then_inc(o_turned, 1)
                        take(e, (o_loaded[a[1]], 16))
                    if d is not None:
                        e.wait_ge(xhl_relayed, 1)
                        for t in range(TPB):
                            cols = slice(t * P, (t + 1) * P)
                            i = product(e, l_ps[:, t], (lambda k: xh[:, d[1], k, cols], lambda k: xl[:, d[1], k, cols]),
                                        (lambda k: wh[:, k, C:C + E], lambda k: wl[:, k, C:C + E]), KC)
                        i.then_inc(logits, 1)
                        take(e, (xhl_relayed, 1))
                    if a is not None:
                        turn(att, att_ready).then_inc(att_turned, 1)
                        e.sem_inc(o_free, 1)
                        take(e, (att_ready, TPB))
                    if c is not None:
                        if a is not None:
                            e.wait_ge(al_ready, 1)
                        turn(xn[:, c[1]], xn_ready).then_inc(xn_turned, 1)
                        take(e, (xn_ready, TPB))
                    if d is not None:
                        e.wait_ge(choice_ready, 1)
                        for t in range(TPB):
                            i = e.transpose(r_ps[:, t * P:(t + 1) * P], mask[:, t], ident[:])
                        i.then_inc(choice_turned, 1)
                        take(e, (choice_ready, 1))

                pipeline(e, stages)


DUMMY = CAP


def phase_shared_and_slots(nc, xh_d, xl_d, s1_d, s2_d, mt_d, acc0_d, acc1_d, xg_d, slots):
    HALF = N // 2
    ROUNDS = CAP // 8
    with Phase(nc, "shf") as ph:
        w1f = ph.sb("w1f", [P, KC, SF0])
        w1h = ph.sb("w1h", [P, KC, SF0], f32r)
        w1l = ph.sb("w1l", [P, KC, SF0], f32r)
        NF = SF0 // P
        w2f = ph.sb("w2f", [P, NF, C])
        w2h = ph.sb("w2h", [P, NF, C], f32r)
        w2l = ph.sb("w2l", [P, NF, C], f32r)
        xh = ph.sb("xh", [P, 2, KC, BLK], f32r)
        xl = ph.sb("xl", [P, 2, KC, BLK], f32r)
        hg = ph.sb("hg", [P, 2, NF, BLK])
        hh = ph.sb("hh", [P, NF, BLK], f32r)
        hl = ph.sb("hl", [P, NF, BLK], f32r)
        out = ph.sb("out", [P, 2, TPB, C])
        zero = ph.sb("zero", [P, 2048])
        key = ph.sb("key", [P, HALF])
        early = ph.sb("early", [P, HALF])
        val = ph.sb("val", [P, CAP])
        both = ph.sb("both", [E0, 2, CAP])
        first = ph.sb("first", [E0, CAP])
        slot_no = ph.sb("slot_no", [E0, CAP])
        ident = ph.sb("ident", [P, P])
        h_ps = ph.ps("h_ps", [P, NF, BLK])
        y_ps = ph.ps("y_ps", [P, TPB, C])
        i_ps = ph.ps("i_ps", [CAP, E0])

        w_loaded = ph.sem("w_loaded")
        w_split = ph.sem("w_split")
        pool_chain = ph.sem("pool_chain")
        dve_chain = ph.sem("dve_chain")
        loaded = [ph.sem(f"loaded{j}") for j in range(2)]
        zeros_ready = ph.sem("zeros_ready")
        zeros_stored = ph.sem("zeros_stored")
        iotas_ready = ph.sem("iotas_ready")
        choice_loaded = ph.sem("choice_loaded")
        moved = ph.sem("moved")
        local_ready = ph.sem("local_ready")
        list_ready = ph.sem("list_ready")
        list_turned = ph.sem("list_turned")
        h_ready = ph.sem("h_ready")
        h_free = ph.sem("h_free")
        hg_ready = ph.sem("hg_ready")
        gelu_done = ph.sem("gelu_done")
        hl_ready = ph.sem("hl_ready")
        y_ready = ph.sem("y_ready")
        out_ready = ph.sem("out_ready")
        y_free = ph.sem("y_free")
        stored = [ph.sem(f"stored{j}") for j in range(2)]

        def turned(d):
            return d.rearrange("(b c p) (j t) -> b j p c t", b=B, p=P, j=2)

        acc0_v = acc0_d[0:N].rearrange("(b j t p) c -> b j p t c", j=2, t=TPB, p=P)
        ZR = 2048 // C
        acc1_v = acc1_d[0:N].rearrange("(n p r) c -> n p (r c)", p=P, r=ZR)

        with nc.Block() as block:
            @block.sync
            def _(e):
                def load(b, j):
                    e.dma_start(xh[:, j].bitcast(fp32), turned(xh_d)[b, j]).then_inc(loaded[j], 16)
                    e.dma_start(xl[:, j].bitcast(fp32), turned(xl_d)[b, j]).then_inc(loaded[j], 16)

                def store(b, j):
                    e.wait_ge(out_ready, 1)
                    e.sem_inc(y_free, 1)
                    e.dma_start(acc0_v[b, j], out[:, j]).then_inc(stored[j], 16)
                    take(e, (out_ready, 1))

                e.dma_start(w1f[:], s1_d).then_inc(w_loaded, 16)
                e.dma_start(w2f[:], s2_d).then_inc(w_loaded, 16)
                for j in range(2):
                    load(0, j)
                with e.Fori(0, B - 1) as b:
                    for j in range(2):
                        store(b, j)
                        load(b + 1, j)
                for j in range(2):
                    store(B - 1, j)

            @block.gpsimd
            def _(e):
                step = Chain(e, pool_chain)
                identity(e, step, ident)
                step(e.memset(zero[:], 0.0))
                e.sem_inc(zeros_ready, 1)
                step(e.iota(early[:], [[-1, HALF]], base=HALF, channel_multiplier=0,
                            allow_small_or_imprecise_dtypes=True))
                e.sem_inc(iotas_ready, 1)
                step(e.iota(slot_no[:], [[1, CAP]], base=0, channel_multiplier=0,
                            allow_small_or_imprecise_dtypes=True))
                e.sem_inc(iotas_ready, 1)
                step.close()
                with e.Fori(0, B):
                    for j in range(2):
                        e.wait_ge(hg_ready, 1)
                        e.tensor_tensor(hl[:], hg[:, j], hh[:].bitcast(fp32), ALU.subtract).then_inc(hl_ready, 1)
                        take(e, (hg_ready, 1))

            @block.vector
            def _(e):
                step = Chain(e, dve_chain)
                e.wait_ge(w_loaded, 32)
                split_weights(e, step, w1f, w1h, w1l)
                split_weights(e, step, w2f, w2h, w2l)
                e.sem_inc(w_split, 1)
                e.wait_ge(choice_loaded, 32)
                e.wait_ge(iotas_ready, 2)
                step(e.tensor_tensor(key[:], key[:], early[:], ALU.mult))

                def largest(dst, src):
                    for r in range(ROUNDS):
                        step(e.max(dst[:, 8 * r:8 * r + 8], src))
                        step(e.match_replace(src, dst[:, 8 * r:8 * r + 8], src, -1.0))

                largest(val[:], key[:])
                step(e.tensor_scalar(first[:], val[0:E0], 0.0, float(HALF), ALU.is_gt, ALU.mult))
                step(e.tensor_scalar(val[:], val[:], 0.0, None, ALU.max))
                step(e.tensor_tensor(both[:, 0], val[0:E0], first[:], ALU.add))
                e.sem_inc(local_ready, 1)
                e.wait_ge(moved, 16)
                largest(first[:], both[:].rearrange("e h c -> e (h c)"))
                step(e.tensor_scalar(first[:], first[:], 0.0, None, ALU.max))
                step(e.tensor_scalar(both[:, 0], first[:], 0.0, None, ALU.is_equal))
                step(e.tensor_tensor(both[:, 0], both[:, 0], slot_no[:], ALU.mult))
                step(e.tensor_scalar(first[:], first[:], -1.0, float(N), ALU.mult, ALU.add))
                e.tensor_tensor(first[:], first[:], both[:, 0], ALU.add).then_inc(list_ready, 1)
                e.wait_ge(list_turned, 1)
                step(e.tensor_copy(slots[:], i_ps[:]))

            @block.scalar
            def _(e):
                for h in range(2):
                    e.dma_start(key[h * E0:(h + 1) * E0], mt_d[:, h * HALF:(h + 1) * HALF]).then_inc(choice_loaded, 16)
                e.wait_ge(zeros_ready, 1)
                for n in range(N // (P * ZR)):
                    e.dma_start(acc1_v[n], zero[:]).then_inc(zeros_stored, 16)
                for d in (acc0_d, acc1_d):
                    e.dma_start(d[N:N + DUMMY], zero[0:DUMMY, 0:C]).then_inc(zeros_stored, 16)
                e.dma_start(xg_d[N:N + DUMMY], zero[0:DUMMY, 0:XW]).then_inc(zeros_stored, 16)
                for j in range(2):
                    e.sem_inc(stored[j], 16)
                with e.Fori(0, B):
                    for j in range(2):
                        for f in range(NF):
                            e.wait_ge(h_ready, f + 1)
                            i = e.activation(hg[:, j, f], h_ps[:, f], ACT.Gelu_apprx_tanh)
                            i.then_inc(h_free, 1)
                        e.drain().then_inc(gelu_done, 1)
                        e.wait_ge(gelu_done, 1)
                        e.activation(hh[:], hg[:, j], ACT.Copy).then_inc(hg_ready, 1)
                        e.wait_ge(stored[j], 16)
                        e.wait_ge(y_ready, 1)
                        e.activation(out[:, j], y_ps[:], ACT.Copy).then_inc(out_ready, 1)
                        take(e, (h_ready, NF), (gelu_done, 1), (stored[j], 16), (y_ready, 1))
                for j in range(2):
                    e.wait_ge(stored[j], 16)
                e.wait_ge(zeros_stored, 16 * (N // (P * ZR) + 3))
                e.wait_ge(local_ready, 1)
                e.dma_start(both[:, 1], val[E0:P]).then_inc(moved, 16)

            @block.tensor
            def _(e):
                e.sem_inc(h_free, NF)
                e.sem_inc(y_free, 1)
                e.wait_ge(w_split, 1)
                with e.Fori(0, B):
                    for j in range(2):
                        e.wait_ge(loaded[j], 32)
                        for f in range(NF):
                            e.wait_ge(h_free, f + 1)
                            cols = slice(f * P, (f + 1) * P)
                            product(e, h_ps[:, f], (lambda k: w1h[:, k, cols], lambda k: w1l[:, k, cols]),
                                    (lambda k: xh[:, j, k], lambda k: xl[:, j, k]), KC).then_inc(h_ready, 1)
                        e.wait_ge(hl_ready, 1)
                        e.wait_ge(y_free, 1)
                        for t in range(TPB):
                            cols = slice(t * P, (t + 1) * P)
                            i = product(e, y_ps[:, t], (lambda k: hh[:, k, cols], lambda k: hl[:, k, cols]),
                                        (lambda k: w2h[:, k], lambda k: w2l[:, k]), NF)
                            if t == TPB - 1:
                                i.then_inc(y_ready, 1)
                        take(e, (loaded[j], 32), (h_free, NF), (hl_ready, 1), (y_free, 1))
                e.wait_ge(list_ready, 1)
                e.transpose(i_ps[:], first[:], ident[0:E0, 0:E0]).then_inc(list_turned, 1)


def phase_experts(nc, slots, xg_d, w1_d, w2_d, acc0_d, acc1_d):
    with Phase(nc, "exp") as ph:
        NBUF = 2
        cur = [ph.sb(f"cur{j}", [CAP, 1], i32) for j in range(NBUF)]
        xs = ph.sb("xs", [CAP, NBUF, XW])
        xt = ph.sb("xt", [P, NBUF, KC, CAP])
        w1 = ph.sb("w1", [P, NBUF, KC, F0])
        w2 = ph.sb("w2", [P, NBUF, C])
        h = ph.sb("h", [P, NBUF, CAP])
        y = ph.sb("y", [CAP, NBUF, C])
        ident = ph.sb("ident", [P, P])
        t_ps = ph.ps("t_ps", [P, NBUF, BLK])
        h_ps = ph.ps("h_ps", [P, NBUF, BLK])
        y_ps = ph.ps("y_ps", [CAP, NBUF, BLK])

        pool_chain = ph.sem("pool_chain")
        ident_ready = ph.sem("ident_ready")
        w_loaded = [ph.sem(f"w_loaded{j}") for j in range(NBUF)]
        w_free = ph.sem("w_free")
        gathered = [ph.sem(f"gathered{j}") for j in range(NBUF)]
        x_turned = ph.sem("x_turned")
        xt_ready = ph.sem("xt_ready")
        h_ready = ph.sem("h_ready")
        gelu_ready = ph.sem("gelu_ready")
        y_ready = ph.sem("y_ready")
        out_ready = ph.sem("out_ready")
        added = [ph.sem(f"added{j}") for j in range(NBUF)]
        xs_free = ph.sem("xs_free")
        accs = (acc0_d, acc1_d)

        with nc.Block() as block:
            @block.sync
            def _(e):
                e.sem_inc(w_free, NBUF)
                with e.Fori(0, E0 // NBUF) as i:
                    for j in range(NBUF):
                        e.wait_ge(w_free, 1)
                        e.dma_start(w1[:, j], w1_d.rearrange("(i j) (k p) f -> i j p k f", j=NBUF, p=P)[i, j]
                                    ).then_inc(w_loaded[j], 16)
                        e.dma_start(w2[:, j], w2_d.rearrange("(i j) p c -> i j p c", j=NBUF)[i, j]
                                    ).then_inc(w_loaded[j], 16)
                        take(e, (w_free, 1))

            @block.gpsimd
            def _(e):
                step = Chain(e, pool_chain)
                identity(e, step, ident)
                e.sem_inc(ident_ready, 1)
                step.close()
                e.sem_inc(xs_free, NBUF)
                with e.Fori(0, E0 // NBUF) as i:
                    for j in range(NBUF):
                        e.wait_ge(xs_free, j + 1)
                        e.wait_ge(added[j], i * 16)
                        step(e.tensor_copy(cur[j][:], slots[:, bass.ds(i * NBUF + j, 1)]))
                        e.indirect_dma_start(xs[:, j], None, xg_d, bass.IndirectOffsetOnAxis(ap=cur[j][:], axis=0)
                                             ).then_inc(gathered[j], 16)
                    step.close()
                    take(e, (xs_free, NBUF))
                    for j in range(NBUF):
                        e.wait_ge(out_ready, j + 1)
                        e.indirect_dma_start(accs[j], bass.IndirectOffsetOnAxis(ap=cur[j][:], axis=0), y[:, j], None,
                                             compute_op=ALU.add).then_inc(added[j], 16)
                    take(e, (out_ready, NBUF))
                for j in range(NBUF):
                    e.wait_ge(added[j], 16 * (E0 // NBUF))

            @block.vector
            def _(e):
                with e.Fori(0, E0 // NBUF) as i:
                    for j in range(NBUF):
                        e.wait_ge(x_turned, j + 1)
                        e.tensor_copy(xt[:, j], t_ps[:, j, 0:KC * CAP].rearrange("p (k c) -> p k c", k=KC)
                                      ).then_inc(xt_ready, 1)
                    for j in range(NBUF):
                        e.wait_ge(y_ready, j + 1)
                        e.tensor_scalar(y[:, j], y_ps[:, j, 0:C], xs[:, j, bass.ds(i * NBUF + j + C, 1)], None,
                                        ALU.mult).then_inc(out_ready, 1)
                    take(e, (x_turned, NBUF), (y_ready, NBUF))
                    e.drain()
                    e.sem_inc(xs_free, NBUF)

            @block.scalar
            def _(e):
                with e.Fori(0, E0 // NBUF):
                    for j in range(NBUF):
                        e.wait_ge(h_ready, j + 1)
                        e.activation(h[:, j], h_ps[:, j, 0:CAP], ACT.Gelu_apprx_tanh).then_inc(gelu_ready, 1)
                    take(e, (h_ready, NBUF))

            @block.tensor
            def _(e):
                e.wait_ge(ident_ready, 1)
                with e.Fori(0, E0 // NBUF) as i:
                    for j in range(NBUF):
                        e.wait_ge(gathered[j], i * 16 + 16)
                        for k in range(KC):
                            n = e.transpose(t_ps[:, j, k * CAP:(k + 1) * CAP], xs[:, j, k * P:(k + 1) * P],
                                            ident[0:CAP, 0:CAP])
                        n.then_inc(x_turned, 1)
                    for j in range(NBUF):
                        e.wait_ge(xt_ready, j + 1)
                        e.wait_ge(w_loaded[j], 32)
                        for k in range(KC):
                            n = e.matmul(h_ps[:, j, 0:CAP], w1[:, j, k], xt[:, j, k], start=k == 0, stop=k == KC - 1)
                        n.then_inc(h_ready, 1)
                    for j in range(NBUF):
                        e.wait_ge(gelu_ready, j + 1)
                        e.matmul(y_ps[:, j, 0:C], h[:, j], w2[:, j], start=True, stop=True).then_inc(y_ready, 1)
                    take(e, (xt_ready, NBUF), (gelu_ready, NBUF), (w_loaded[0], 32), (w_loaded[1], 32))
                    e.drain().then_inc(w_free, NBUF)


def normaliser(e, step, src, st, mv, ve, rs, nmr, var_ready, rstd_ready, signal):
    for t in range(TPB):
        e.bn_stats(st[:, t], src[:, t])
    step.settle()
    for t in range(TPB):
        e.bn_aggr(mv[:, t], st[:, t])
    step.settle()
    e.tensor_scalar(ve[:], mv[:, :, 1], EPS, None, ALU.add).then_inc(var_ready, 1)
    e.wait_ge(rstd_ready, 1)
    e.scalar_tensor_tensor(nmr[:], mv[:, :, 0], -1.0, rs[:], ALU.mult, ALU.mult).then_inc(signal, 1)
    take(e, (rstd_ready, 1))


def phase_linear_qkv(nc, x1_d, acc0_d, acc1_d, w_d, bqk_d, bv_d, x2_d, fq_d, fqh_d, fql_d, fkh_d, fkl_d, fkt_d, v_d):
    FE = 1e-4
    with Phase(nc, "lqk") as ph:
        wf = ph.sb("wf", [P, KC, 3 * C])
        wh = ph.sb("wh", [P, KC, 3 * C], f32r)
        wl = ph.sb("wl", [P, KC, 3 * C], f32r)
        bqk = ph.sb("bqk", [P, 4])
        bqke = ph.sb("bqke", [P, 4])
        bv = ph.sb("bv", [P, C])
        ident = ph.sb("ident", [P, P])
        mhalf = ph.sb("mhalf", [P, TPB])
        x1 = ph.sb("x1", [P, 2, TPB, C])
        a0 = ph.sb("a0", [P, 2, TPB, C])
        a1 = ph.sb("a1", [P, 2, TPB, C])
        st = ph.sb("st", [P, TPB, 6])
        mv = ph.sb("mv", [P, TPB, 2])
        ve = ph.sb("ve", [P, TPB])
        rs = ph.sb("rs", [P, TPB])
        nmr = ph.sb("nmr", [P, TPB])
        xn = ph.sb("xn", [P, TPB, C])
        xh = ph.sb("xh", [P, KC, BLK], f32r)
        xl = ph.sb("xl", [P, KC, BLK], f32r)
        ex = ph.sb("ex", [P, 2, BLK])
        re = ph.sb("re", [P, 2, BLK])
        phi = ph.sb("phi", [P, 4, BLK])
        oh = ph.sb("oh", [P, 4, BLK], f32r)
        ol = ph.sb("ol", [P, 4, BLK], f32r)
        kt = ph.sb("kt", [P, 2, TPB, P])
        vo = ph.sb("vo", [P, TPB, NH, VW])
        t_ps = ph.ps("t_ps", [P, 2, BLK])
        qk = ph.ps("qk", [P, 4, BLK])
        vp = ph.ps("vp", [P, TPB, C])

        w_loaded = ph.sem("w_loaded")
        pe_consts = ph.sem("pe_consts")
        ones_ready = ph.sem("ones_ready")
        bias_ready = ph.sem("bias_ready")
        pool_chain = ph.sem("pool_chain")
        dve_chain = ph.sem("dve_chain")
        loaded = [ph.sem(f"loaded{j}") for j in range(2)]
        sum_ready = ph.sem("sum_ready")
        var_ready = ph.sem("var_ready")
        rstd_ready = ph.sem("rstd_ready")
        y_scale = ph.sem("y_scale")
        yn_ready = ph.sem("yn_ready")
        x_scale = ph.sem("x_scale")
        xn_ready = ph.sem("xn_ready")
        xn_turned = ph.sem("xn_turned")
        xh_ready = ph.sem("xh_ready")
        xl_ready = ph.sem("xl_ready")
        qk_ready = ph.sem("qk_ready")
        exp_ready = ph.sem("exp_ready")
        phi_ready = ph.sem("phi_ready")
        oh_ready = ph.sem("oh_ready")
        ol_ready = ph.sem("ol_ready")
        phi_relayed = ph.sem("phi_relayed")
        k_turned = ph.sem("k_turned")
        kt_ready = ph.sem("kt_ready")
        v_ready = ph.sem("v_ready")
        vo_ready = ph.sem("vo_ready")
        loads_due = ph.sem("loads_due")
        drained = ph.sem("drained")
        stored = ph.sem("stored")
        STORES = 16 * (1 + 5 + 2 + 8)

        def tiles(d):
            return d.rearrange("(b j t p) c -> b j p t c", j=2, t=TPB, p=P)

        def turned(d):
            return d.rearrange("(b c p) (j t) -> b j p c t", b=B, p=P, j=2)

        kt_v = fkt_d.rearrange("(b f j t p) c -> b j f p t c", b=B, f=2, j=2, t=TPB)
        v_v = v_d.rearrange("(b f j t p) c -> b j f t p c", b=B, f=2, j=2, t=TPB)

        with nc.Block() as block:
            @block.sync
            def _(e):
                def load(b, j):
                    e.dma_start(a0[:, j], tiles(acc0_d[0:N])[b, j]).then_inc(loaded[j], 16)
                    e.dma_start(a1[:, j], tiles(acc1_d[0:N])[b, j]).then_inc(loaded[j], 16)
                    e.dma_start(x1[:, j], tiles(x1_d)[b, j]).then_inc(loaded[j], 16)

                def store(b, j):
                    e.wait_ge(phi_ready, 4)
                    e.sem_inc(phi_relayed, 1)
                    e.dma_start(tiles(x2_d)[b, j], x1[:, j]).then_inc(stored, 16)
                    e.dma_start(turned(fq_d)[b, j], phi[:, 0:2]).then_inc(stored, 16)
                    e.wait_ge(vo_ready, 1)
                    for f in range(2):
                        for t in range(TPB):
                            e.dma_start(v_v[b, j, f, t], vo[:, t, 8 * f:8 * f + 8].rearrange("p h d -> p (h d)")
                                        ).then_inc(stored, 16)
                    e.wait_ge(ol_ready, 4)
                    for d, s, c in ((fqh_d, oh, 0), (fkh_d, oh, 2), (fql_d, ol, 0), (fkl_d, ol, 2)):
                        e.dma_start(turned(d)[b, j], s[:, c:c + 2].bitcast(fp32)).then_inc(stored, 16)
                    e.wait_ge(kt_ready, 1)
                    for f in range(2):
                        e.dma_start(kt_v[b, j, f], kt[:, f]).then_inc(stored, 16)
                    take(e, (phi_ready, 4), (vo_ready, 1), (ol_ready, 4), (kt_ready, 1))

                e.dma_start(wf[:], w_d).then_inc(w_loaded, 16)
                e.dma_start(bqk[:], bqk_d).then_inc(w_loaded, 16)
                e.dma_start(bv[:], bv_d.rearrange("(o n) -> o n", o=1).broadcast_to((P, C))).then_inc(w_loaded, 16)
                for j in range(2):
                    load(0, j)
                with e.Fori(0, B - 1) as b:
                    for j in range(2):
                        store(b, j)
                        e.wait_ge(loads_due, 1)
                        load(b + 1, j)
                        take(e, (loads_due, 1))
                for j in range(2):
                    store(B - 1, j)

            @block.gpsimd
            def _(e):
                step = Chain(e, pool_chain)
                identity(e, step, ident)
                step(e.memset(mhalf[:], -0.5))
                e.sem_inc(pe_consts, 1)
                step(e.memset(vo[:].rearrange("p t h d -> p (t h) d")[:, :, HD:VW], 1.0))
                e.sem_inc(ones_ready, 1)
                step.close()
                with e.Fori(0, B):
                    for j in range(2):
                        e.wait_ge(loaded[j], 48)
                        e.tensor_tensor(a0[:, j], a0[:, j], a1[:, j], ALU.add).then_inc(sum_ready, 1)
                        for _ in range(2):
                            e.wait_ge(var_ready, 1)
                            e.tensor_tensor(rs[:], ve[:], mhalf[:], ALU.pow).then_inc(rstd_ready, 1)
                            take(e, (var_ready, 1))
                        for c in range(4):
                            e.wait_ge(oh_ready, c + 1)
                            e.tensor_tensor(ol[:, c], phi[:, c], oh[:, c].bitcast(fp32), ALU.subtract
                                            ).then_inc(ol_ready, 1)
                        take(e, (loaded[j], 48), (oh_ready, 4))

            @block.vector
            def _(e):
                step = Chain(e, dve_chain)
                e.wait_ge(w_loaded, 48)
                step(e.tensor_scalar(wf[:, :, 0:C], wf[:, :, 0:C], HD ** -0.5, None, ALU.mult))
                step(e.tensor_scalar(bqk[:, 0:2], bqk[:, 0:2], HD ** -0.5, None, ALU.mult))
                step(e.tensor_scalar(bqke[:], bqk[:], FE, None, ALU.add))
                e.sem_inc(bias_ready, 1)
                split_weights(e, step, wf, wh, wl)
                e.sem_inc(pe_consts, 1)
                e.wait_ge(ones_ready, 1)
                step.close()
                with e.Fori(0, B):
                    for j in range(2):
                        e.wait_ge(sum_ready, 1)
                        normaliser(e, step, a0[:, j], st, mv, ve, rs, nmr, var_ready, rstd_ready, y_scale)
                        e.wait_ge(yn_ready, 1)
                        step(e.tensor_tensor(x1[:, j], x1[:, j], a1[:, j], ALU.add))
                        normaliser(e, step, x1[:, j], st, mv, ve, rs, nmr, var_ready, rstd_ready, x_scale)
                        e.wait_ge(xh_ready, 1)
                        e.tensor_tensor(xl[:], t_ps[:], xh[:].bitcast(fp32), ALU.subtract).then_inc(xl_ready, 1)
                        for c in range(4):
                            e.wait_ge(exp_ready, c + 1)
                            step(e.tensor_scalar(re[:, c % 2], qk[:, c], bqke[:, c:c + 1], FE, ALU.add, ALU.max))
                            e.scalar_tensor_tensor(phi[:, c], ex[:, c % 2], 1.0, re[:, c % 2], ALU.min, ALU.add
                                                   ).then_inc(phi_ready, 1)
                            e.drain().then_inc(drained, 1)
                        e.wait_ge(v_ready, 1)
                        e.tensor_tensor(vo[:, :, :, 0:HD].rearrange("p t h d -> p t h d"),
                                        vp[:].rearrange("p t (h d) -> p t h d", d=HD),
                                        bv[:].rearrange("p (h d) -> p h d", d=HD).unsqueeze(1)
                                        .broadcast_to((P, TPB, NH, HD)), ALU.add).then_inc(vo_ready, 1)
                        take(e, (sum_ready, 1), (yn_ready, 1), (xh_ready, 1), (exp_ready, 4), (v_ready, 1))
                        step.close()

            @block.scalar
            def _(e):
                e.wait_ge(bias_ready, 1)
                e.sem_inc(stored, STORES)
                with e.Fori(0, B):
                    for j in range(2):
                        e.wait_ge(y_scale, 1)
                        for t in range(TPB):
                            i = e.activation(a1[:, j, t], a0[:, j, t], ACT.Identity, bias=nmr[:, t:t + 1],
                                             scale=rs[:, t:t + 1])
                        i.then_inc(yn_ready, 1)
                        e.wait_ge(x_scale, 1)
                        for t in range(TPB):
                            e.activation(xn[:, t], x1[:, j, t], ACT.Identity, bias=nmr[:, t:t + 1],
                                         scale=rs[:, t:t + 1]).then_inc(xn_ready, 1)
                        e.wait_ge(xn_turned, 1)
                        e.activation(xh[:], t_ps[:], ACT.Copy).then_inc(xh_ready, 1)
                        e.wait_ge(stored, STORES)
                        e.sem_inc(loads_due, 1)
                        for c in range(4):
                            e.wait_ge(qk_ready, c + 1)
                            if c >= 2:
                                e.wait_ge(drained, c - 1)
                            e.activation(ex[:, c % 2], qk[:, c], ACT.Exp, bias=bqk[:, c:c + 1]).then_inc(exp_ready, 1)
                            if c:
                                e.wait_ge(drained, c)
                                e.activation(oh[:, c - 1], phi[:, c - 1], ACT.Copy).then_inc(oh_ready, 1)
                        e.wait_ge(drained, 4)
                        e.activation(oh[:, 3], phi[:, 3], ACT.Copy).then_inc(oh_ready, 1)
                        e.wait_ge(k_turned, 1)
                        e.activation(kt[:], t_ps[:].rearrange("p f (t c) -> p f t c", t=TPB), ACT.Copy
                                     ).then_inc(kt_ready, 1)
                        take(e, (y_scale, 1), (x_scale, 1), (xn_turned, 1), (stored, STORES), (qk_ready, 4),
                             (drained, 4), (k_turned, 1))
                e.wait_ge(stored, STORES)

            @block.tensor
            def _(e):
                e.wait_ge(pe_consts, 2)
                with e.Fori(0, 2 * B):
                    for t in range(TPB):
                        e.wait_ge(xn_ready, t + 1)
                        for k in range(KC):
                            i = e.transpose(t_ps[:, k, t * P:(t + 1) * P], xn[:, t, k * P:(k + 1) * P], ident[:])
                    i.then_inc(xn_turned, 1)
                    e.wait_ge(xl_ready, 1)
                    for c in range(4):
                        cols = slice(c * P, (c + 1) * P)
                        product(e, qk[:, c], (lambda k: wh[:, k, cols], lambda k: wl[:, k, cols]),
                                (lambda k: xh[:, k], lambda k: xl[:, k]), KC).then_inc(qk_ready, 1)
                    for t in range(TPB):
                        cols = slice(t * P, (t + 1) * P)
                        i = product(e, vp[:, t], (lambda k: xh[:, k, cols], lambda k: xl[:, k, cols]),
                                    (lambda k: wh[:, k, 2 * C:3 * C], lambda k: wl[:, k, 2 * C:3 * C]), KC)
                    i.then_inc(v_ready, 1)
                    e.wait_ge(phi_relayed, 1)
                    for f in range(2):
                        for t in range(TPB):
                            i = e.transpose(t_ps[:, f, t * P:(t + 1) * P], phi[:, 2 + f, t * P:(t + 1) * P], ident[:])
                    i.then_inc(k_turned, 1)
                    take(e, (xn_ready, TPB), (xl_ready, 1), (phi_relayed, 1))


def phase_linear_attention(nc, fq_d, fqh_d, fql_d, fkh_d, fkl_d, fkt_d, v_d, o_d):
    G, F = 2 * B, 8
    NBUF = 2
    with Phase(nc, "lin") as ph:
        qx = [ph.sb(f"qx{n}", [P, NBUF, F, T], f32r) for n in ("h", "l")]
        kk = [ph.sb(f"kk{n}", [P, NBUF, T], f32r) for n in ("h", "l")]
        fq = ph.sb("fq", [P, NBUF, T])
        kt = ph.sb("kt", [P, NBUF, KB, P])
        vs = ph.sb("vs", [P, NBUF, KB, F * VW])
        am = ph.sb("am", [P, 2, F, P])
        tri = ph.sb("tri", [P, P])
        own = ph.sb("own", [P, F])
        state = ph.sb("state", [P, F, 32])
        ot = ph.sb("ot", [P, 2, BLK])
        a_ps = ph.ps("a_ps", [P, 2, F // 2, P])
        b_ps = ph.ps("b_ps", [P, 2, F // 2, P])
        o_ps = ph.ps("o_ps", [P, 2, BLK])
        s_ps = ph.ps("s_ps", [P, F, VW])

        zeroed = ph.sem("zeroed")
        pool_chain = ph.sem("pool_chain")
        dve_chain = ph.sem("dve_chain")
        masks_ready = ph.sem("masks_ready")
        loaded = [ph.sem(f"loaded{j}") for j in range(NBUF)]
        a_ready = ph.sem("a_ready")
        am_ready = ph.sem("am_ready")
        s_ready = ph.sem("s_ready")
        state_ready = ph.sem("state_ready")
        o_ready = ph.sem("o_ready")
        ot_ready = ph.sem("ot_ready")
        o_free = ph.sem("o_free")
        ot_stored = ph.sem("ot_stored")
        LOADS = 16 * (2 * F + 5)
        scores = (a_ps, b_ps)

        rows = {n: d.rearrange("(g p) t -> g p t", p=P) for n, d in
                (("fq", fq_d), ("fqh", fqh_d), ("fql", fql_d), ("fkh", fkh_d), ("fkl", fkl_d))}
        kt_rows = fkt_d.rearrange("(g k p) c -> g p k c", k=KB, p=P)
        v_rows = v_d.rearrange("(g k p) c -> g p k c", k=KB, p=P)
        o_rows = o_d.rearrange("(g s p) (h t) -> g h p s t", s=2, p=P, h=2)

        with nc.Block() as block:
            @block.sync
            def _(e):
                def load(g, j):
                    for dst, name in ((qx[0], "fqh"), (qx[1], "fql")):
                        for h in range(F):
                            e.dma_start(dst[h * HD:(h + 1) * HD, j, h].bitcast(fp32),
                                        rows[name][g, h * HD:(h + 1) * HD]).then_inc(loaded[j], 16)
                    e.dma_start(kk[0][:, j].bitcast(fp32), rows["fkh"][g]).then_inc(loaded[j], 16)
                    e.dma_start(kk[1][:, j].bitcast(fp32), rows["fkl"][g]).then_inc(loaded[j], 16)
                    e.dma_start(fq[:, j], rows["fq"][g]).then_inc(loaded[j], 16)
                    e.dma_start(kt[:, j], kt_rows[g]).then_inc(loaded[j], 16)
                    e.dma_start(vs[:, j], v_rows[g]).then_inc(loaded[j], 16)

                def outputs(g):
                    for h in range(2):
                        e.wait_ge(ot_ready, h + 1)
                        e.sem_inc(o_free, 1)
                        e.dma_start(o_rows[g, h], ot[:]).then_inc(ot_stored, 16)
                    take(e, (ot_ready, 2))

                e.wait_ge(zeroed, 4)
                for j in range(NBUF):
                    load(j, j)
                with e.Fori(0, G // NBUF - 1) as i:
                    for j in range(NBUF):
                        outputs(NBUF * i + j)
                        load(NBUF * i + j + NBUF, j)
                outputs(G - 2)
                outputs(G - 1)

            @block.gpsimd
            def _(e):
                step = Chain(e, pool_chain)
                step(e.memset(tri[:], 1.0))
                step(e.affine_select(out=tri[:], in_=tri[:], compare_op=ALU.is_ge, fill=0.0, base=0,
                                     pattern=[[1, P]], channel_multiplier=-1))
                step(e.memset(own[:], 1.0))
                step(e.affine_select(out=own[:], in_=own[:], compare_op=ALU.is_ge, fill=0.0, base=0,
                                     pattern=[[-HD, F]], channel_multiplier=1))
                step(e.affine_select(out=own[:], in_=own[:], compare_op=ALU.is_ge, fill=0.0, base=HD - 1,
                                     pattern=[[HD, F]], channel_multiplier=-1))
                e.sem_inc(masks_ready, 1)
                for j in range(NBUF):
                    step(e.memset(qx[1][:, j].bitcast(fp32), 0.0))
                    e.sem_inc(zeroed, 1)

            @block.vector
            def _(e):
                step = Chain(e, dve_chain)
                for j in range(NBUF):
                    step(e.memset(qx[0][:, j].bitcast(fp32), 0.0))
                    e.sem_inc(zeroed, 1)
                e.wait_ge(masks_ready, 1)
                step.close()
                with e.Fori(0, G):
                    step(e.memset(state[:], 0.0))
                    e.sem_inc(state_ready, 1)
                    for c in range(KB):
                        e.wait_ge(a_ready, c + 1)
                        src = scores[c % 2][:].rearrange("p a h q -> p (a h) q")
                        e.tensor_tensor(am[:, c % 2], src, tri[:].unsqueeze(1).broadcast_to((P, F, P)), ALU.mult
                                        ).then_inc(am_ready, 1)
                        if c < KB - 1:
                            e.wait_ge(s_ready, c + 1)
                            e.tensor_tensor(state[:, :, 0:VW], s_ps[:], own[:].unsqueeze(2)
                                            .broadcast_to((P, F, VW)), ALU.mult).then_inc(state_ready, 1)
                    e.wait_ge(s_ready, KB)
                    take(e, (a_ready, KB), (s_ready, KB))
                    step.close()

            @block.scalar
            def _(e):
                e.sem_inc(ot_stored, 16)
                with e.Fori(0, 2 * G):
                    e.wait_ge(o_ready, 1)
                    e.wait_ge(ot_stored, 16)
                    e.activation(ot[:], o_ps[:], ACT.Copy).then_inc(ot_ready, 1)
                    take(e, (o_ready, 1), (ot_stored, 16))
                e.wait_ge(ot_stored, 16)

            @block.tensor
            def _(e):
                def chunk_scores(j, c):
                    cols = slice(c * P, (c + 1) * P)
                    for s in range(2):
                        heads = slice(4 * s, 4 * s + 4)
                        i = product(e, scores[c % 2][:, s],
                                    (lambda _: kk[0][:, j, cols], lambda _: kk[1][:, j, cols]),
                                    (lambda _: qx[0][:, j, heads, cols], lambda _: qx[1][:, j, heads, cols]), 1)
                    i.then_inc(a_ready, 1)

                def chunk_outputs(j, c):
                    cols = slice(c * P, (c + 1) * P)
                    oc = slice((c % TPB) * P, (c % TPB + 1) * P)
                    if c % TPB == 0:
                        e.wait_ge(o_free, 1)
                        take(e, (o_free, 1))
                    e.wait_ge(state_ready, c + 1)
                    for s in range(2):
                        e.matmul(o_ps[:, s, oc], state[:, 4 * s:4 * s + 4].rearrange("p h d -> p (h d)"),
                                 fq[:, j, cols], start=True, stop=False, skip_group_check=True)
                    e.matmul(s_ps[:].rearrange("p h d -> p (h d)"), kt[:, j, c], vs[:, j, c], start=c == 0,
                             stop=True, skip_group_check=True).then_inc(s_ready, 1)
                    e.wait_ge(am_ready, c + 1)
                    for s in range(2):
                        for h in range(4):
                            i = e.matmul(o_ps[32 * h:32 * h + VW, s, oc],
                                         vs[:, j, c, (4 * s + h) * VW:(4 * s + h + 1) * VW],
                                         am[:, c % 2, 4 * s + h], start=False, stop=True, skip_group_check=True)
                    if c % TPB == TPB - 1:
                        i.then_inc(o_ready, 1)

                e.sem_inc(o_free, 1)
                with e.Fori(0, G // NBUF):
                    for j in range(NBUF):
                        e.wait_ge(loaded[j], LOADS)
                        chunk_scores(j, 0)
                        for c in range(KB):
                            if c < KB - 1:
                                chunk_scores(j, c + 1)
                            chunk_outputs(j, c)
                        take(e, (loaded[j], LOADS), (am_ready, KB), (state_ready, KB))


def phase_gated_ffn(nc, xh_d, xl_d, x3_d, wt_d, weights, out_d):
    NCH = E1 + SF1 // P
    gw_d, sgw_d, uw_d, suw_d, dw_d, sdw_d = weights
    with Phase(nc, "ffn") as ph:
        raw = [ph.sb(f"raw{n}", [P, KC, NCH * P]) for n in ("g", "u", "d")]
        wh = [ph.sb(f"wh{n}", [P, KC, NCH * P], f32r) for n in ("g", "u", "d")]
        wl = [ph.sb(f"wl{n}", [P, KC, NCH * P], f32r) for n in ("g", "u", "d")]
        mhalf = ph.sb("mhalf", [P, TPB])
        xh = ph.sb("xh", [P, 2, KC, BLK], f32r)
        xl = ph.sb("xl", [P, 2, KC, BLK], f32r)
        wt = ph.sb("wt", [P, 2, E1, BLK])
        x3 = ph.sb("x3", [P, 2, TPB, C])
        gate = ph.sb("gate", [P, 2, BLK])
        hid = ph.sb("hid", [P, 2, BLK])
        hh = ph.sb("hh", [P, 3, BLK], f32r)
        hl = ph.sb("hl", [P, 3, BLK], f32r)
        st = ph.sb("st", [P, TPB, 6])
        mv = ph.sb("mv", [P, TPB, 2])
        ve = ph.sb("ve", [P, TPB])
        rs = ph.sb("rs", [P, TPB])
        nmr = ph.sb("nmr", [P, TPB])
        yn = ph.sb("yn", [P, 2, TPB, C])
        g_ps = ph.ps("g_ps", [P, 2, BLK])
        u_ps = ph.ps("u_ps", [P, 2, BLK])
        y_ps = ph.ps("y_ps", [P, 2, TPB, C])

        raw_loaded = [ph.sem(f"raw_loaded{n}") for n in range(3)]
        high_ready = ph.sem("high_ready")
        low_ready = ph.sem("low_ready")
        dve_chain = ph.sem("dve_chain")
        pow_ready = ph.sem("pow_ready")
        x_loaded = [ph.sem(f"x_loaded{j}") for j in range(2)]
        w_loaded = [ph.sem(f"w_loaded{j}") for j in range(2)]
        g_ready = ph.sem("g_ready")
        u_ready = ph.sem("u_ready")
        gate_ready = ph.sem("gate_ready")
        hid_ready = ph.sem("hid_ready")
        hh_ready = ph.sem("hh_ready")
        hl_ready = ph.sem("hl_ready")
        gu_free = ph.sem("gu_free")
        y_ready = ph.sem("y_ready")
        var_ready = ph.sem("var_ready")
        rstd_ready = ph.sem("rstd_ready")
        scale_ready = ph.sem("scale_ready")
        yn_ready = ph.sem("yn_ready")
        out_ready = ph.sem("out_ready")
        stored = [ph.sem(f"stored{j}") for j in range(2)]

        def tiles(d):
            return d.rearrange("(b j t p) c -> b j p t c", j=2, t=TPB, p=P)

        def turned(d):
            return d.rearrange("(b c p) (j t) -> b j p c t", b=B, p=P, j=2)

        wt_rows = wt_d.rearrange("e (b j t) -> b j e t", b=B, j=2)

        def down(a):
            return a[:].rearrange("p k (c f) -> p (k c f)", f=P).rearrange("p (c h) -> p c h", h=C)

        with nc.Block() as block:
            @block.sync
            def _(e):
                def load(b, j):
                    e.dma_start(xh[:, j].bitcast(fp32), turned(xh_d)[b, j]).then_inc(x_loaded[j], 16)
                    e.dma_start(xl[:, j].bitcast(fp32), turned(xl_d)[b, j]).then_inc(x_loaded[j], 16)
                    e.dma_start(wt[:, j], wt_rows[b, j].unsqueeze(0).broadcast_to((P, E1, BLK))
                                ).then_inc(w_loaded[j], 16)
                    e.dma_start(x3[:, j], tiles(x3_d)[b, j]).then_inc(w_loaded[j], 16)

                def store(b, j):
                    e.wait_ge(out_ready, 1)
                    e.dma_start(tiles(out_d)[b, j], yn[:, j]).then_inc(stored[j], 16)
                    take(e, (out_ready, 1))

                for n, (routed, shared) in enumerate(((gw_d, sgw_d), (uw_d, suw_d))):
                    e.dma_start(raw[n][:, :, 0:E1 * P], routed).then_inc(raw_loaded[n], 16)
                    e.dma_start(raw[n][:, :, E1 * P:], shared).then_inc(raw_loaded[n], 16)
                e.dma_start(down(raw[2])[:, 0:E1], dw_d).then_inc(raw_loaded[2], 16)
                e.dma_start(down(raw[2])[:, E1:], sdw_d).then_inc(raw_loaded[2], 16)
                for j in range(2):
                    load(0, j)
                with e.Fori(0, B - 1) as b:
                    for j in range(2):
                        store(b, j)
                        load(b + 1, j)
                for j in range(2):
                    store(B - 1, j)

            @block.gpsimd
            def _(e):
                e.memset(mhalf[:], -0.5).then_inc(pow_ready, 1)
                e.wait_ge(pow_ready, 1)
                with e.Fori(0, 2 * B):
                    e.wait_ge(var_ready, 1)
                    e.tensor_tensor(rs[:], ve[:], mhalf[:], ALU.pow).then_inc(rstd_ready, 1)
                    take(e, (var_ready, 1))

            @block.vector
            def _(e):
                step = Chain(e, dve_chain)
                for n in range(3):
                    e.wait_ge(high_ready, n + 1)
                    step(e.tensor_tensor(wl[n][:], raw[n][:], wh[n][:].bitcast(fp32), ALU.subtract))
                    e.sem_inc(low_ready, 1)
                step.close()

                def result(j, part):
                    if part == 0:
                        e.wait_ge(y_ready, 1)
                        variance(e, step, y_ps[:, j], st, mv, ve, var_ready)
                        take(e, (y_ready, 1))
                    elif part == 1:
                        scaling(e, mv, rs, nmr, rstd_ready, scale_ready)
                    else:
                        e.wait_ge(yn_ready, 1)
                        e.tensor_tensor(yn[:, j], yn[:, j], x3[:, j], ALU.add).then_inc(out_ready, 1)
                        take(e, (yn_ready, 1))

                def hidden(j, prev):
                    e.wait_ge(w_loaded[j], 32)
                    for c in range(NCH):
                        e.wait_ge(gate_ready, c + 1)
                        e.wait_ge(u_ready, c + 1)
                        product_ = e.tensor_tensor(hid[:, c % 2], gate[:, c % 2], u_ps[:, c % 2], ALU.mult)
                        if c < E1:
                            step(product_)
                            e.sem_inc(gu_free, 1)
                            e.tensor_tensor(hid[:, c % 2], hid[:, c % 2], wt[:, j, c], ALU.mult).then_inc(hid_ready, 1)
                        else:
                            product_.then_inc(hid_ready, 1)
                        e.wait_ge(hh_ready, c + 1)
                        if c >= E1:
                            e.sem_inc(gu_free, 1)
                        e.tensor_tensor(hl[:, c % 3], hid[:, c % 2], hh[:, c % 3].bitcast(fp32), ALU.subtract
                                        ).then_inc(hl_ready, 1)
                        if prev and c in (2, 3, 6):
                            result(1 - j, (2, 3, 6).index(c))
                    take(e, (w_loaded[j], 32), (gate_ready, NCH), (u_ready, NCH), (hh_ready, NCH))
                    step.close()

                hidden(0, False)
                hidden(1, True)
                with e.Fori(1, B):
                    for j in range(2):
                        hidden(j, True)
                for part in range(3):
                    result(1, part)
                step.close()

            @block.scalar
            def _(e):
                for n in range(3):
                    e.wait_ge(raw_loaded[n], 32)
                    e.activation(wh[n][:], raw[n][:], ACT.Copy).then_inc(high_ready, 1)
                for j in range(2):
                    e.sem_inc(stored[j], 16)

                def normalise(j):
                    e.wait_ge(stored[j], 16)
                    e.wait_ge(scale_ready, 1)
                    for t in range(TPB):
                        i = e.activation(yn[:, j, t], y_ps[:, j, t], ACT.Identity, bias=nmr[:, t:t + 1],
                                         scale=rs[:, t:t + 1])
                    i.then_inc(yn_ready, 1)
                    take(e, (stored[j], 16), (scale_ready, 1))

                def hidden(j, prev):
                    for c in range(NCH):
                        e.wait_ge(g_ready, c + 1)
                        e.activation(gate[:, c % 2], g_ps[:, c % 2], ACT.Silu).then_inc(gate_ready, 1)
                        e.wait_ge(hid_ready, c + 1)
                        e.activation(hh[:, c % 3], hid[:, c % 2], ACT.Copy).then_inc(hh_ready, 1)
                        if prev and c == 4:
                            normalise(1 - j)
                    take(e, (g_ready, NCH), (hid_ready, NCH))

                hidden(0, False)
                hidden(1, True)
                with e.Fori(1, B):
                    for j in range(2):
                        hidden(j, True)
                normalise(1)
                for j in range(2):
                    e.wait_ge(stored[j], 16)

            @block.tensor
            def _(e):
                def gate_up(j, c):
                    e.wait_ge(gu_free, c + 1)
                    cols = slice(c * P, (c + 1) * P)
                    for ps, n, ready in ((g_ps, 0, g_ready), (u_ps, 1, u_ready)):
                        product(e, ps[:, c % 2], (lambda k: wh[n][:, k, cols], lambda k: wl[n][:, k, cols]),
                                (lambda k: xh[:, j, k], lambda k: xl[:, j, k]), KC).then_inc(ready, 1)

                def down_product(j, c, wait):
                    e.wait_ge(hl_ready, wait)
                    for t in range(TPB):
                        cols = slice(t * P, (t + 1) * P)
                        i = product(e, y_ps[:, j, t], (lambda _: hh[:, c % 3, cols], lambda _: hl[:, c % 3, cols]),
                                    (lambda _: down(wh[2])[:, c], lambda _: down(wl[2])[:, c]), 1,
                                    first=c == 0 and t % 2 == 0, last=c == NCH - 1, skip_group_check=True)
                    return i

                def chunks(j, prev):
                    e.wait_ge(x_loaded[j], 32)
                    for c in range(NCH):
                        gate_up(j, c)
                        if c >= 2:
                            down_product(j, c - 2, c + 1)
                        elif prev:
                            i = down_product(1 - j, NCH - 2 + c, c + 1)
                            if c == 1:
                                i.then_inc(y_ready, 1)
                    take(e, (x_loaded[j], 32), (gu_free, NCH), (hl_ready, NCH))

                e.wait_ge(low_ready, 3)
                e.sem_inc(gu_free, 2)
                e.sem_inc(hl_ready, 2)
                chunks(0, False)
                chunks(1, True)
                with e.Fori(1, B):
                    for j in range(2):
                        chunks(j, True)
                down_product(1, NCH - 2, 1)
                down_product(1, NCH - 1, 2).then_inc(y_ready, 1)


def build(nc, x, w_attn, w_proj, router0, bias0, w1, w2, sw1, sw2, w_qkv, bqk, bv, w_out, b_out, router1, bias1,
          gate, up, down, s_gate, s_up, s_down, out):
    def dram(name, *shape):
        return nc.dram_tensor(name, shape, fp32, kind="Internal").ap()

    features = (B * C, T)
    heads = (B * NG * P, T)
    qh, ql, kh, kl = (dram(n, *features) for n in ("q_high", "q_low", "k_high", "k_low"))
    v = dram("values", B * NG * T, GH * VW)
    o = dram("attended", *heads)
    x1 = dram("x1", N, C)
    x1h, x1l = dram("x1_high", *features), dram("x1_low", *features)
    rows = dram("expert_rows", N + DUMMY, XW)
    chosen = dram("chosen", E0, N)
    acc0, acc1 = dram("acc0", N + DUMMY, C), dram("acc1", N + DUMMY, C)
    x2 = dram("x2", N, C)
    fq = dram("phi_q", *features)
    fqh, fql, fkh, fkl = (dram(n, *features) for n in ("phi_q_high", "phi_q_low", "phi_k_high", "phi_k_low"))
    fkt = dram("phi_k_rows", 2 * N, P)
    v1 = dram("values1", 2 * N, P + 8)
    o1 = dram("attended1", *heads)
    x3 = dram("x3", N, C)
    x3h, x3l = dram("x3_high", *features), dram("x3_low", *features)
    weights = dram("weights", E1, N)

    phase_qkv(nc, x, w_attn, qh, ql, kh, kl, v)
    phase_softmax_attention(nc, qh, ql, kh, kl, v, o)
    phase_project_route(nc, 0, o, x, w_proj, router0, bias0, None, x1, x1h, x1l, rows, chosen)
    with nc.sbuf_tensor("slots", [CAP, E0], i32) as slots:
        phase_shared_and_slots(nc, x1h, x1l, sw1, sw2, chosen, acc0, acc1, rows, slots)
        phase_experts(nc, slots, rows, w1, w2, acc0, acc1)
    phase_linear_qkv(nc, x1, acc0, acc1, w_qkv, bqk, bv, x2, fq, fqh, fql, fkh, fkl, fkt, v1)
    phase_linear_attention(nc, fq, fqh, fql, fkh, fkl, fkt, v1, o1)
    phase_project_route(nc, 1, o1, x2, w_out, router1, bias1, b_out, x3, x3h, x3l, None, weights)
    phase_gated_ffn(nc, x3h, x3l, x3, weights, (gate, s_gate, up, s_up, down, s_down), out)


def kernel(**inputs):
    import numpy as np
    import concourse.bacc as bacc
    from concourse.bass_utils import run_bass_kernel_spmd

    def chunked(w):
        return w.reshape(-1, P, w.shape[-1]).transpose(1, 0, 2)

    def gated(w):
        return w.reshape(E1, KC, P, F1).transpose(2, 1, 0, 3).reshape(P, KC, E1 * F1)

    get = {n: np.asarray(a) for n, a in inputs.items()}
    laid = {
        "x": get["L0_attn_x"].reshape(N, C),
        "w_attn": chunked(get["L0_attn_w_attn"]),
        "w_proj": chunked(get["L0_attn_w_proj"]),
        "router0": chunked(get["L0_ffn_router_weight"].T),
        "bias0": get["L0_ffn_expert_bias"],
        "w1": get["L0_ffn_w1"],
        "w2": get["L0_ffn_w2"],
        "sw1": chunked(get["L0_ffn_sw1"].T),
        "sw2": chunked(get["L0_ffn_sw2"].T),
        "w_qkv": chunked(get["L1_attn_W_qkv"]),
        "bqk": get["L1_attn_b_qkv"][:2 * C].reshape(4, P).T,
        "bv": get["L1_attn_b_qkv"][2 * C:],
        "w_out": chunked(get["L1_attn_W_out"]),
        "b_out": get["L1_attn_b_out"],
        "router1": chunked(get["L1_ffn_router_w"]),
        "bias1": get["L1_ffn_router_bias"].reshape(1),
        "gate": gated(get["L1_ffn_gate_w"]),
        "up": gated(get["L1_ffn_up_w"]),
        "down": get["L1_ffn_down_w"].transpose(1, 0, 2),
        "s_gate": chunked(get["L1_ffn_s_gate_w"]),
        "s_up": chunked(get["L1_ffn_s_up_w"]),
        "s_down": chunked(get["L1_ffn_s_down_w"]),
    }
    laid = {n: np.ascontiguousarray(a) for n, a in laid.items()}
    nc = bacc.Bacc("TRN2", target_bir_lowering=False, num_devices=1)
    args = {n: nc.dram_tensor(n, a.shape, mybir.dt.from_np(a.dtype), kind="ExternalInput").ap()
            for n, a in laid.items()}
    out = nc.dram_tensor("out", (N, C), fp32, kind="ExternalOutput").ap()
    build(nc, *args.values(), out)
    r = run_bass_kernel_spmd(nc, [laid], core_ids=[0])
    return r.results[0]["out"].reshape(B, T, C)
```

```python
import concourse.bass as bass
from concourse import mybir
from contextlib import ExitStack

fp32 = mybir.dt.float32
f32r = mybir.dt.float32r
bf16 = mybir.dt.bfloat16
u32 = mybir.dt.uint32
i32 = mybir.dt.int32
ALU = mybir.AluOpType
ACT = mybir.ActivationFunctionType
AX = mybir.AxisListType

B, T, C = 8, 1024, 256
N = B * T
NH, HD = 16, 16
P = 128
KC = C // P
BLK = 512
TPB = BLK // P
NBLK = N // BLK
GH = 4
NG = NH // GH
VW = HD + 1
KB = T // P
E0, K0, F0, SF0 = 64, 6, 128, 512
CAP = 2 * ((512 * K0 + E0 - 1) // E0)
E1, K1, F1, SF1 = 8, 4, 128, 512
XW = C + E0
EPS = 1e-5



def take(eng, *pairs):
    for sem, n in pairs:
        eng.sem_inc(sem, -n)


class Phase:

    def __init__(self, nc, name):
        self.nc, self.name, self.ctx, self.sems = nc, name, ExitStack(), []

    def sb(self, name, shape, dt=fp32):
        return self.ctx.enter_context(self.nc.sbuf_tensor(f"{self.name}_{name}", shape, dt))

    def ps(self, name, shape, dt=fp32):
        return self.ctx.enter_context(self.nc.psum_tensor(f"{self.name}_{name}", shape, dt))

    def sem(self, name):
        self.sems.append(self.nc.alloc_semaphore(f"{self.name}_{name}"))
        return self.sems[-1]

    def __enter__(self):
        return self

    def __exit__(self, *a):
        self.nc.clear_and_free_semaphores(self.sems)
        self.nc.all_engine_barrier()
        return self.ctx.__exit__(*a)


def phase_qkv(nc, x_d, w_d, qh_d, ql_d, kh_d, kl_d, v_d):
    with Phase(nc, "qkv") as ph:
        wf = ph.sb("wf", [P, KC, 3 * C])
        wh = ph.sb("wh", [P, KC, 3 * C], f32r)
        wl = ph.sb("wl", [P, KC, 3 * C], f32r)
        ident = ph.sb("ident", [P, P])
        mhalf = ph.sb("mhalf", [P, TPB])
        x = ph.sb("x", [P, 2, TPB, C])
        st = ph.sb("st", [P, TPB, 6])
        mv = ph.sb("mv", [P, TPB, 2])
        ve = ph.sb("ve", [P, TPB])
        rs = ph.sb("rs", [P, TPB])
        xn = ph.sb("xn", [P, TPB, C])
        xh = ph.sb("xh", [P, KC, BLK], f32r)
        xl = ph.sb("xl", [P, KC, BLK], f32r)
        oh = ph.sb("oh", [P, 2, 4, BLK], f32r)
        ol = ph.sb("ol", [P, 2, 4, BLK], f32r)
        vo = ph.sb("vo", [P, 2, TPB, NH, VW])
        tp = ph.ps("tp", [P, KC, BLK])
        qk = ph.ps("qk", [P, 4, BLK])
        vp = ph.ps("vp", [P, 2, 2, C])

        w_loaded = ph.sem("w_loaded")
        w_chain = ph.sem("w_chain")
        w_split = ph.sem("w_split")
        consts = ph.sem("consts")
        x_loaded = [ph.sem(f"x_loaded{j}") for j in range(2)]
        x_free = ph.sem("x_free")
        dve = ph.sem("dve")
        var_ready = ph.sem("var_ready")
        rstd_ready = ph.sem("rstd_ready")
        xn_ready = ph.sem("xn_ready")
        xt_ready = ph.sem("xt_ready")
        xh_ready = ph.sem("xh_ready")
        xhl_ready = ph.sem("xhl_ready")
        xhl_free = ph.sem("xhl_free")
        qk_ready = ph.sem("qk_ready")
        qkh_ready = ph.sem("qkh_ready")
        qkl_ready = ph.sem("qkl_ready")
        qk_free = ph.sem("qk_free")
        v_ready = ph.sem("v_ready")
        v_out = ph.sem("v_out")
        v_free = ph.sem("v_free")
        stored = [ph.sem(f"stored{j}") for j in range(2)]
        STORES = 16 * (4 + TPB)

        x_v = x_d.rearrange("(b j t p) c -> b j p t c", j=2, t=TPB, p=P)
        v_v = v_d.rearrange("(b g j t p) c -> b j t p g c", b=B, g=NG, j=2, t=TPB, p=P)

        def rows(d):
            return d.rearrange("(b c p) (j t) -> b j p c t", b=B, p=P, j=2)

        with nc.Block() as block:
            @block.sync
            def _(e):
                e.dma_start(wf[:], w_d).then_inc(w_loaded, 16)

                def load(b, j):
                    e.dma_start(x[:, j], x_v[b, j]).then_inc(x_loaded[j], 16)

                def store(b, j):
                    for c in range(4):
                        e.wait_ge(qkl_ready, c + 1)
                        e.sem_inc(qk_free, 1)
                    for d, s, c in ((qh_d, oh, 0), (kh_d, oh, 2), (ql_d, ol, 0), (kl_d, ol, 2)):
                        e.dma_start(rows(d)[b, j], s[:, j, c:c + 2].bitcast(fp32)).then_inc(stored[j], 16)
                    e.wait_ge(v_out, 2)
                    e.sem_inc(v_free, 1)
                    for t in range(TPB):
                        e.dma_start(v_v[b, j, t], vo[:, j, t].rearrange("p (g h) d -> p g (h d)", g=NG)
                                    ).then_inc(stored[j], 16)
                    take(e, (qkl_ready, 4), (v_out, 2))

                for j in range(2):
                    load(0, j)
                with e.Fori(0, B - 1) as b:
                    for j in range(2):
                        e.wait_ge(x_free, 1)
                        load(b + 1, j)
                        take(e, (x_free, 1))
                        store(b, j)
                for j in range(2):
                    store(B - 1, j)

            @block.gpsimd
            def _(e):
                e.memset(mhalf[:], -0.5)
                e.memset(vo[:].rearrange("p j t h d -> p (j t h) d")[:, :, HD:VW], 1.0).then_inc(consts, 1)
                e.memset(ident[:], 0.0).then_inc(consts, 1)
                e.wait_ge(consts, 2)
                e.affine_select(out=ident[:], in_=ident[:], compare_op=ALU.not_equal, fill=1.0, base=0,
                                pattern=[[-1, P]], channel_multiplier=1).then_inc(w_split, 1)
                with e.Fori(0, B):
                    for j in range(2):
                        e.wait_ge(var_ready, 1)
                        e.tensor_tensor(rs[:], ve[:], mhalf[:], ALU.pow).then_inc(rstd_ready, 1)
                        take(e, (var_ready, 1))

            @block.vector
            def _(e):
                e.wait_ge(w_loaded, 16)
                e.tensor_scalar(wf[:, :, 0:C], wf[:, :, 0:C], HD ** -0.5, None, ALU.mult).then_inc(w_chain, 1)
                e.wait_ge(w_chain, 1)
                e.tensor_copy(wh[:], wf[:]).then_inc(w_chain, 1)
                e.wait_ge(w_chain, 2)
                e.tensor_tensor(wl[:], wf[:], wh[:].bitcast(fp32), ALU.subtract).then_inc(w_split, 1)
                with e.Fori(0, B):
                    for j in range(2):
                        e.wait_ge(x_loaded[j], 16)
                        for t in range(TPB):
                            e.bn_stats(st[:, t], x[:, j, t]).then_inc(dve, 1)
                        for t in range(TPB):
                            e.wait_ge(dve, t + 1)
                            e.bn_aggr(mv[:, t], st[:, t]).then_inc(dve, 1)
                        e.wait_ge(dve, 2 * TPB)
                        e.tensor_scalar(ve[:], mv[:, :, 1], EPS, None, ALU.add).then_inc(var_ready, 1)
                        e.wait_ge(rstd_ready, 1)
                        for t in range(TPB):
                            e.tensor_scalar(xn[:, t], x[:, j, t], mv[:, t, 0:1], rs[:, t:t + 1],
                                            ALU.subtract, ALU.mult).then_inc(xn_ready, 1)
                        e.wait_ge(xh_ready, 1)
                        e.sem_inc(x_free, 1)
                        e.tensor_tensor(xl[:], tp[:], xh[:].bitcast(fp32), ALU.subtract).then_inc(xhl_ready, 1)
                        for c in range(4):
                            e.wait_ge(qkh_ready, c + 1)
                            e.tensor_tensor(ol[:, j, c], qk[:, c], oh[:, j, c].bitcast(fp32),
                                            ALU.subtract).then_inc(qkl_ready, 1)
                        take(e, (dve, 2 * TPB), (rstd_ready, 1), (x_loaded[j], 16), (xh_ready, 1), (qkh_ready, 4))

            @block.scalar
            def _(e):
                e.sem_inc(stored[0], STORES)
                e.sem_inc(stored[1], STORES)
                e.sem_inc(xhl_free, 1)
                e.wait_ge(consts, 1)
                with e.Fori(0, B):
                    for j in range(2):
                        e.wait_ge(xt_ready, 1)
                        e.wait_ge(xhl_free, 1)
                        e.activation(xh[:], tp[:], ACT.Copy).then_inc(xh_ready, 1)
                        e.wait_ge(stored[j], STORES)
                        for c in range(4):
                            e.wait_ge(qk_ready, c + 1)
                            e.activation(oh[:, j, c], qk[:, c], ACT.Copy).then_inc(qkh_ready, 1)
                        for m in range(2):
                            e.wait_ge(v_ready, m + 1)
                            e.activation(vo[:, j, 2 * m:2 * m + 2, :, 0:HD],
                                         vp[:, m].rearrange("p t (h d) -> p t h d", d=HD),
                                         ACT.Copy).then_inc(v_out, 1)
                        take(e, (xt_ready, 1), (xhl_free, 1), (stored[j], STORES), (qk_ready, 4), (v_ready, 2))
                for j in range(2):
                    e.wait_ge(stored[j], STORES)

            @block.tensor
            def _(e):
                e.sem_inc(qk_free, 4)
                e.sem_inc(v_free, 1)
                e.wait_ge(w_split, 2)
                with e.Fori(0, 2 * B):
                    for t in range(TPB):
                        e.wait_ge(xn_ready, t + 1)
                        for k in range(KC):
                            i = e.transpose(tp[:, k, t * P:(t + 1) * P], xn[:, t, k * P:(k + 1) * P], ident[:])
                    i.then_inc(xt_ready, 1)
                    e.wait_ge(xhl_ready, 1)
                    for c in range(4):
                        e.wait_ge(qk_free, c + 1)
                        terms = [(wa, xa, k) for k in range(KC) for wa, xa in ((wh, xh), (wh, xl), (wl, xh))]
                        for n, (wa, xa, k) in enumerate(terms):
                            i = e.matmul(qk[:, c], wa[:, k, c * P:(c + 1) * P], xa[:, k],
                                         start=n == 0, stop=n == len(terms) - 1)
                        i.then_inc(qk_ready, 1)
                    e.wait_ge(v_free, 1)
                    for t in range(TPB):
                        terms = [(xa, wa, k) for k in range(KC) for xa, wa in ((xh, wh), (xh, wl), (xl, wh))]
                        for n, (xa, wa, k) in enumerate(terms):
                            i = e.matmul(vp[:, t // 2, t % 2], xa[:, k, t * P:(t + 1) * P], wa[:, k, 2 * C:3 * C],
                                         start=n == 0, stop=n == len(terms) - 1)
                        if t == 1:
                            i.then_inc(v_ready, 1)
                        if t == TPB - 1:
                            i.then_inc(xhl_free, 1)
                            e.drain().then_inc(v_ready, 1)
                    take(e, (xn_ready, TPB), (xhl_ready, 1), (qk_free, 4), (v_free, 1))


def phase_softmax_attention(nc, qh_d, ql_d, kh_d, kl_d, v_d, o_d):
    G = B * NG
    NBUF = 3
    NPR = 4
    MBUF = 3
    SR = 4 * HD
    with Phase(nc, "att") as ph:
        qs = ph.sb("qs", [P, NBUF, GH, T], f32r)
        ks = ph.sb("ks", [P, NBUF, GH, T], f32r)
        vs = ph.sb("vs", [P, NBUF, KB, GH * VW])
        pr = ph.sb("pr", [P, NPR, GH, BLK])
        ot = ph.sb("ot", [P, 2, BLK])
        zero = ph.sb("zero", [32, P])
        identf = ph.sb("identf", [P, P])
        identb = ph.sb("identb", [P, P], bf16)
        causal = ph.sb("causal", [P, P], bf16)
        mx = ph.sb("mx", [P, 2, GH, KB])
        mxs = ph.sb("mxs", [P, GH, KB])
        nmt = ph.sb("nmt", [32, P], f32r)
        e_ps = ph.ps("e_ps", [P, 2, 2, BLK])
        m_ps = ph.ps("m_ps", [P, MBUF, BLK])
        o_ps = ph.ps("o_ps", [P, BLK])

        consts = ph.sem("consts")
        consts_pe = ph.sem("consts_pe")
        later_stacks = ph.sem("later_stacks")
        const_chain = ph.sem("const_chain")
        stack_loaded = [ph.sem(f"stack_loaded{j}") for j in range(NBUF)]
        m_scores = ph.sem("m_scores")
        m_free = ph.sem("m_free")
        pieces_done = ph.sem("pieces_done")
        max_ready = ph.sem("max_ready")
        maxt_ready = ph.sem("maxt_ready")
        nmt_ready = ph.sem("nmt_ready")
        mrow_loaded = ph.sem("mrow_loaded")
        e_scores = ph.sem("e_scores")
        exp_done = ph.sem("exp_done")
        mask_due = ph.sem("mask_due")
        masked = ph.sem("masked")
        pv_done = ph.sem("pv_done")
        ot_ready = ph.sem("ot_ready")
        o_free = ph.sem("o_free")
        ot_stored = [ph.sem(f"ot_stored{j}") for j in range(2)]
        LOADS = 16 * 10
        LOOPS = (G - 4) // NBUF

        steps = [(h, k, p) for h in range(2) for k in range(4 * h + 4) for p in range(2)]
        pieces = []
        for q in range(KB):
            for h in range(q // 4 + 1):
                per = max(1, min(GH, BLK // (min(BLK, (q + 1) * P - h * BLK))))
                if (q, h) == (1, 0):
                    pieces += [(q, h, (0, 1)), (q, h, (2,)), (q, h, (3,))]
                else:
                    pieces += [(q, h, tuple(range(n, n + per))) for n in range(0, GH, per)]
        NPC, MEND, MAXIMA = len(pieces), 19, 20
        assert NPC % MBUF == 0

        def width(h, k):
            return BLK - max(0, k * P - h * BLK)

        def keys(q, h):
            return min(BLK, (q + 1) * P - h * BLK)

        def diagonal(s):
            h, k, p = steps[s]
            return k * P >= h * BLK

        def shares():
            order = list(range(MEND, len(steps))) + list(range(MEND))
            load = [keys(q, h) * len(heads) + 96 for q, h, heads in pieces]
            work = [width(*steps[s][:2]) + 160 for s in order]
            out, n, done, due = {}, 0, 0.0, 0.0
            for s, w in zip(order, work):
                due += w * sum(load) / sum(work)
                out[s] = []
                while n < NPC and done + load[n] / 2 <= due:
                    done += load[n]
                    out[s].append(n)
                    n += 1
            return out

        share = shares()
        NDIAG = sum(diagonal(s) for s in range(len(steps)))
        UNITS = len(steps) // 2
        LAG = 2

        def masks_before(u):
            return sum(diagonal(2 * (v % UNITS)) for v in range(-LAG, u + 1)) * 2

        src_rows = {n: d.rearrange("(g h d) t -> g d h t", h=GH, d=HD)
                    for n, d in (("qh", qh_d), ("ql", ql_d), ("kh", kh_d), ("kl", kl_d))}
        v_rows = v_d.rearrange("(g k p) c -> g p k c", k=KB, p=P)
        o_rows = o_d.rearrange("(g p) (h t) -> g h p t", p=P, h=2)

        with nc.Block() as block:
            @block.sync
            def _(e):
                def maxima_row(j):
                    return qs[SR:SR + 1, j].bitcast(fp32).rearrange("o h (k p) -> o (h k) p", p=P)

                def load(g, j):
                    for name, dst, parts in (("qh", qs, (0, 1)), ("ql", qs, (2, 3)),
                                             ("kh", ks, (0, 2)), ("kl", ks, (1, 3))):
                        for r in parts:
                            e.dma_start(dst[r * HD:(r + 1) * HD, j].bitcast(fp32), src_rows[name][g]
                                        ).then_inc(stack_loaded[j], 16)
                    e.dma_start(vs[:, j], v_rows[g]).then_inc(stack_loaded[j], 16)
                    e.dma_start(maxima_row(j), zero[:]).then_inc(stack_loaded[j], 16)

                def row(j):
                    e.wait_ge(nmt_ready, 1)
                    e.dma_start(maxima_row(j), nmt[:].bitcast(fp32)).then_inc(mrow_loaded, 16)
                    take(e, (nmt_ready, 1))

                def outputs(g, h):
                    e.wait_ge(ot_ready, 1)
                    e.sem_inc(o_free, 1)
                    e.dma_start(o_rows[g, h], ot[:, h]).then_inc(ot_stored[h], 16)
                    take(e, (ot_ready, 1))

                def group(g, nxt, loads, more):
                    outputs(g - 1, 1)
                    if loads:
                        load(g + 2, (nxt + 1) % NBUF)
                    outputs(g, 0)
                    if more:
                        row(nxt)

                for j in range(NBUF):
                    e.wait_ge(consts, j + 1)
                    load(j, j)
                row(0)
                outputs(0, 0)
                row(1)
                with e.Fori(0, LOOPS) as i:
                    for j in range(NBUF):
                        group(NBUF * i + j + 1, (j + 2) % NBUF, True, True)
                for g in range(NBUF * LOOPS + 1, G):
                    group(g, (g + 1) % NBUF, g + 2 < G, g + 1 < G)
                outputs(G - 1, 1)

            @block.gpsimd
            def _(e):
                step = Chain(e, const_chain)
                step(e.memset(zero[:], 0.0))
                step(e.memset(qs[SR:P, 0].bitcast(fp32), 0.0))
                e.sem_inc(consts, 1)
                step(e.memset(causal[:], 0.0))
                step(e.affine_select(out=causal[:], in_=causal[:], compare_op=ALU.is_ge, fill=-1e30, base=0,
                                     pattern=[[-1, P]], channel_multiplier=1))
                identity(e, step, identf)
                step(e.tensor_copy(identb[:], identf[:]))
                e.sem_inc(consts_pe, 1)
                for j in range(1, NBUF):
                    step(e.memset(qs[SR:P, j].bitcast(fp32), 0.0))
                    e.sem_inc(consts, 1)
                step.close()
                with e.Fori(0, G):
                    for s, (h, k, p) in enumerate(steps):
                        if diagonal(s):
                            e.wait_ge(mask_due, sum(diagonal(r) for r in range(s + 1)))
                            blk = pr[:, (s // 2) % NPR, 2 * p:2 * p + 2, 0:P]
                            e.affine_select(out=blk, in_=blk, compare_op=ALU.is_ge, fill=0.0, base=0,
                                            pattern=[[0, 2], [1, P]], channel_multiplier=-1).then_inc(masked, 1)
                    take(e, (mask_due, NDIAG))

            @block.vector
            def _(e):
                for j in range(NBUF):
                    e.memset(ks[SR:P, j].bitcast(fp32), 0.0).then_inc(pieces_done, 1)
                    e.wait_ge(pieces_done, 1)
                    take(e, (pieces_done, 1))
                    e.memset(ks[SR:SR + 1, j].bitcast(fp32), 1.0).then_inc(consts_pe if j == 0 else later_stacks, 1)
                    if j == 0:
                        e.memset(o_ps[:], 0.0).then_inc(consts_pe, 1)
                        e.memset(mx[:], -3e38).then_inc(pieces_done, 1)
                        e.wait_ge(pieces_done, 1)
                        take(e, (pieces_done, 1))
                with e.Fori(0, G):
                    for n, (q, h, heads) in enumerate(pieces):
                        w = keys(q, h)
                        e.wait_ge(m_scores, n + 1)
                        src = m_ps[:, n % MBUF, 0:len(heads) * w].rearrange("p (n w) -> p n w", w=w)
                        e.reduce_max(mx[:, h, heads[0]:heads[-1] + 1, q], src, AX.X).then_inc(m_free, 1)
                    e.drain().then_inc(pieces_done, 1)
                    e.wait_ge(pieces_done, 1)
                    e.tensor_tensor(mxs[:], mx[:, 0], mx[:, 1], ALU.max).then_inc(pieces_done, 1)
                    e.wait_ge(pieces_done, 2)
                    e.sem_inc(max_ready, 1)
                    take(e, (m_scores, NPC), (pieces_done, 2))

            @block.scalar
            def _(e):
                def maxima():
                    e.wait_ge(maxt_ready, 1)
                    e.activation(nmt[:], e_ps[0:32, 0, 1, BLK - P:BLK], ACT.Copy, scale=-1.0).then_inc(nmt_ready, 1)
                    take(e, (maxt_ready, 1))

                def outputs(h, products_done):
                    e.wait_ge(pv_done, products_done)
                    e.wait_ge(ot_stored[h], 16)
                    e.activation(ot[:, h], o_ps[:], ACT.Copy).then_inc(ot_ready, 1)
                    take(e, (ot_stored[h], 16))

                def group(first, more):
                    for s, (h, k, p) in enumerate(steps):
                        w, u = width(h, k), s // 2
                        if s == MAXIMA and more:
                            e.wait_ge(e_scores, s + 1)
                            maxima()
                        if p == 0:
                            e.wait_ge(pv_done, u + 1)
                        e.wait_ge(e_scores, s + 1)
                        e.activation(pr[:, u % NPR, 2 * p:2 * p + 2, 0:w], e_ps[:, s % 2, :, 0:w], ACT.Exp
                                     ).then_inc(exp_done, 1)
                        if s == 2 * LAG - 1 and not first:
                            outputs(1, NPR)
                        if s == 2 * (LAG + 3) + 1:
                            outputs(0, NPR + 4)
                    take(e, (pv_done, UNITS), (e_scores, len(steps)))

                for h in range(2):
                    e.sem_inc(ot_stored[h], 16)
                e.sem_inc(pv_done, NPR)
                maxima()
                group(True, True)
                with e.Fori(0, G - 2):
                    group(False, True)
                group(False, False)
                outputs(1, NPR)
                for h in range(2):
                    e.wait_ge(ot_stored[h], 16)

            @block.tensor
            def _(e):
                def piece(j, n):
                    q, h, heads = pieces[n]
                    w = keys(q, h)
                    e.wait_ge(m_free, n + 1)
                    for i, hd in enumerate(heads):
                        out = m_ps[:, n % MBUF, i * w:(i + 1) * w]
                        ins = e.matmul(out, qs[:, j, hd, q * P:(q + 1) * P], ks[:, j, hd, h * BLK:h * BLK + w],
                                       start=True, stop=h != q // 4)
                        if h == q // 4:
                            ins = e.matmul(out[:, w - P:w], identb[:], causal[:], start=False, stop=True)
                    ins.then_inc(m_scores, 1)
                    if n == NPC - 1:
                        take(e, (m_free, NPC))

                def maxima():
                    e.wait_ge(max_ready, 1)
                    e.transpose(e_ps[0:32, 0, 1, BLK - P:BLK], mxs[:].rearrange("p h k -> p (h k)"), identf[:]
                                ).then_inc(maxt_ready, 1)
                    take(e, (max_ready, 1))

                def exponentials(s, first):
                    e.wait_ge(exp_done, s + 1)
                    if diagonal(s - 2) and not (first and s < 2):
                        e.sem_inc(mask_due, 1)

                def scores(j, s):
                    h, k, p = steps[s]
                    w = width(h, k)
                    for n in range(2):
                        hd = 2 * p + n
                        i = e.matmul(e_ps[:, s % 2, n, 0:w], ks[:, j, hd, k * P:(k + 1) * P],
                                     qs[:, j, hd, (h + 1) * BLK - w:(h + 1) * BLK], start=True, stop=True)
                    i.then_inc(e_scores, 1)

                def products(j, u):
                    if u < 0:
                        j = (j - 1) % NBUF
                    h, k, _ = steps[2 * (u % UNITS)]
                    w = width(h, k)
                    if diagonal(2 * (u % UNITS)):
                        e.wait_ge(masked, masks_before(u))
                    if k == 0:
                        e.wait_ge(o_free, 1)
                        take(e, (o_free, 1))
                    for hd in range(GH):
                        i = e.matmul(o_ps[32 * hd:32 * hd + VW, BLK - w:BLK], vs[:, j, k, hd * VW:(hd + 1) * VW],
                                     pr[:, u % NPR, hd, 0:w], start=k == 0, stop=k == 4 * h + 3)
                    i.then_inc(pv_done, 1)

                def group(j, first, more, more2):
                    e.wait_ge(mrow_loaded, 16)
                    take(e, (mrow_loaded, 16))
                    nxt, nxt2 = (j + 1) % NBUF, (j + 2) % NBUF
                    for s in range(len(steps)):
                        exponentials(s, first)
                        if s == MAXIMA and more:
                            maxima()
                        scores(j, s)
                        if s == MEND and more2:
                            e.wait_ge(stack_loaded[nxt2], LOADS)
                            take(e, (stack_loaded[nxt2], LOADS))
                        if more2 if s >= MEND else more:
                            for n in share[s]:
                                piece(nxt2 if s >= MEND else nxt, n)
                        if s % 2 and not (first and s < 2 * LAG):
                            products(j, s // 2 - LAG)
                    take(e, (exp_done, len(steps)), (masked, NDIAG))

                e.sem_inc(o_free, 1)
                e.sem_inc(m_free, MBUF)
                e.sem_inc(exp_done, 2)
                e.sem_inc(masked, masks_before(-1))
                e.wait_ge(consts_pe, 3)
                e.wait_ge(stack_loaded[0], LOADS)
                take(e, (stack_loaded[0], LOADS))
                for n in range(NPC):
                    piece(0, n)
                maxima()
                e.wait_ge(later_stacks, NBUF - 1)
                e.wait_ge(stack_loaded[1], LOADS)
                take(e, (stack_loaded[1], LOADS))
                for s in range(MEND, len(steps)):
                    for n in share[s]:
                        piece(1, n)
                group(0, True, True, True)
                with e.Fori(0, LOOPS):
                    for j in range(NBUF):
                        group((j + 1) % NBUF, False, True, True)
                for g in range(NBUF * LOOPS + 1, G):
                    group(g % NBUF, False, g + 1 < G, g + 2 < G)
                for s in range(2):
                    exponentials(s, False)
                for u in range(-LAG, 0):
                    products(G % NBUF, u)


class Chain:

    def __init__(self, eng, sem):
        self.eng, self.sem, self.n = eng, sem, 0

    def __call__(self, ins):
        ins.then_inc(self.sem, 1)
        self.n += 1
        self.eng.wait_ge(self.sem, self.n)

    def settle(self):
        self(self.eng.drain())

    def close(self):
        if self.n:
            take(self.eng, (self.sem, self.n))
        self.n = 0


def identity(e, step, ident):
    step(e.memset(ident[:], 0.0))
    step(e.affine_select(out=ident[:], in_=ident[:], compare_op=ALU.not_equal, fill=1.0, base=0,
                         pattern=[[-1, ident.shape[0]]], channel_multiplier=1))


def split_weights(e, step, wf, wh, wl):
    step(e.tensor_copy(wh[:], wf[:]))
    step(e.tensor_tensor(wl[:], wf[:], wh[:].bitcast(fp32), ALU.subtract))


def parts3(ah, al, bh, bl):
    return ((ah, bh), (ah, bl), (al, bh))


def product(e, out, lhs, rhs, n_k, first=True, last=True, **kw):
    terms = [(a(k), b(k)) for k in range(n_k) for a, b in parts3(lhs[0], lhs[1], rhs[0], rhs[1])]
    for n, (a, b) in enumerate(terms):
        i = e.matmul(out, a, b, start=first and n == 0, stop=last and n == len(terms) - 1, **kw)
    return i


def variance(e, step, src, st, mv, ve, var_ready):
    for t in range(TPB):
        e.bn_stats(st[:, t], src[:, t])
    step.settle()
    for t in range(TPB):
        e.bn_aggr(mv[:, t], st[:, t])
    step.settle()
    e.tensor_scalar(ve[:], mv[:, :, 1], EPS, None, ALU.add).then_inc(var_ready, 1)


def scaling(e, mv, rs, nmr, rstd_ready, signal):
    e.wait_ge(rstd_ready, 1)
    e.scalar_tensor_tensor(nmr[:], mv[:, :, 0], -1.0, rs[:], ALU.mult, ALU.mult).then_inc(signal, 1)
    take(e, (rstd_ready, 1))


def pipeline(e, stages):
    last = 2 * B - 1

    def blocks(n):
        return [((n - s) // 2, (n - s) % 2) if 0 <= n - s <= last else None for s in range(4)]

    for n in (0, 1, 2, 3):
        stages(*blocks(n))
    with e.Fori(2, B) as i:
        stages((i, 0), (i - 1, 1), (i - 1, 0), (i - 2, 1))
        stages((i, 1), (i, 0), (i - 1, 1), (i - 1, 0))
    for n in (last + 1, last + 2, last + 3):
        stages(*blocks(n))


def phase_project_route(nc, layer, o_d, x_d, wp_d, rw_d, rb_d, yb_d, xo_d, xh_d, xl_d, xg_d, rt_d):
    E, K, NB = (E0, K0, E0) if layer == 0 else (E1, K1, 1)
    with Phase(nc, f"prj{layer}") as ph:
        wf = ph.sb("wf", [P, KC, C + E])
        wh = ph.sb("wh", [P, KC, C + E], f32r)
        wl = ph.sb("wl", [P, KC, C + E], f32r)
        rbias = ph.sb("rbias", [P, NB])
        ident = ph.sb("ident", [P, P])
        mhalf = ph.sb("mhalf", [P, TPB])
        o = ph.sb("o", [P, 2, NG, BLK])
        x = ph.sb("x", [P, 2, TPB, C])
        den = ph.sb("den", [P, NH])
        rden = ph.sb("rden", [P, TPB, NH])
        att = ph.sb("att", [P, TPB, C])
        ah = ph.sb("ah", [P, KC, BLK], f32r)
        al = ph.sb("al", [P, KC, BLK], f32r)
        st = ph.sb("st", [P, 2, TPB, 6])
        mv = ph.sb("mv", [P, 2, TPB, 2])
        ve = ph.sb("ve", [P, 2, TPB])
        rs = ph.sb("rs", [P, 2, TPB])
        nmr = ph.sb("nmr", [P, 2, TPB])
        yn = ph.sb("yn", [P, TPB, C])
        xo = ph.sb("xo", [P, 2, TPB, C])
        xn = ph.sb("xn", [P, 2, TPB, XW])
        xh = ph.sb("xh", [P, 2, KC, BLK], f32r)
        xl = ph.sb("xl", [P, 2, KC, BLK], f32r)
        sc = ph.sb("sc", [P, TPB, E])
        sb = ph.sb("sb", [P, TPB, E + 8 - K])
        rep = ph.sb("rep", [P, TPB, E + 8 - K])
        top = ph.sb("top", [P, TPB, 8])
        pick = ph.sb("pick", [P, TPB, 8])
        mask = ph.sb("mask", [P, TPB, E])
        ssum = ph.sb("ssum", [P, TPB])
        rt = ph.sb("rt", [E, 2, BLK])
        o_ps = ph.ps("o_ps", [P, 2, NG, P])
        t_ps = ph.ps("t_ps", [P, KC, BLK])
        y_ps = ph.ps("y_ps", [P, TPB, C])
        l_ps = ph.ps("l_ps", [P, TPB, E])
        r_ps = ph.ps("r_ps", [E, BLK])
        if layer == 1:
            ybias = ph.sb("ybias", [P, C])
            y = ph.sb("y", [P, TPB, C])
            ls = ph.sb("ls", [P, TPB, E])
            lmax = ph.sb("lmax", [P, TPB])
            shifted = ph.sem("shifted")
        else:
            y = y_ps

        w_loaded = ph.sem("w_loaded")
        pe_consts = ph.sem("pe_consts")
        pool_chain = ph.sem("pool_chain")
        dve_chain = ph.sem("dve_chain")
        o_loaded = [ph.sem(f"o_loaded{j}") for j in range(2)]
        x_loaded = [ph.sem(f"x_loaded{j}") for j in range(2)]
        o_free = ph.sem("o_free")
        o_turned = ph.sem("o_turned")
        att_ready = ph.sem("att_ready")
        att_turned = ph.sem("att_turned")
        ah_ready = ph.sem("ah_ready")
        al_ready = ph.sem("al_ready")
        y_ready = ph.sem("y_ready")
        y_free = ph.sem("y_free")
        yvar_ready = ph.sem("yvar_ready")
        yrstd_ready = ph.sem("yrstd_ready")
        y_scale = ph.sem("y_scale")
        yn_ready = ph.sem("yn_ready")
        xvar_ready = ph.sem("xvar_ready")
        xrstd_ready = ph.sem("xrstd_ready")
        x_scale = ph.sem("x_scale")
        xn_ready = ph.sem("xn_ready")
        xn_turned = ph.sem("xn_turned")
        xh_ready = ph.sem("xh_ready")
        xl_ready = ph.sem("xl_ready")
        xhl_relayed = ph.sem("xhl_relayed")
        logits = ph.sem("logits")
        scores = ph.sem("scores")
        choice_ready = ph.sem("choice_ready")
        choice_turned = ph.sem("choice_turned")
        rt_ready = ph.sem("rt_ready")
        weights_ready = ph.sem("weights_ready")
        x_stored = [ph.sem(f"x_stored{j}") for j in range(2)]
        r_stored = [ph.sem(f"r_stored{j}") for j in range(2)]
        X_STORES = 16 * 3
        R_STORES = 16 * (2 if layer == 0 else 1)

        def tiles(d):
            return d.rearrange("(b j t p) c -> b j p t c", j=2, t=TPB, p=P)

        def turned(d):
            return d.rearrange("(b c p) (j t) -> b j p c t", b=B, p=P, j=2)

        o_rows = o_d.rearrange("(b g p) (j t) -> b j p g t", b=B, p=P, j=2)
        r_rows = rt_d.rearrange("e (b j t) -> b j e t", b=B, j=2)

        with nc.Block() as block:
            @block.sync
            def _(e):
                def load_o(b, j):
                    e.dma_start(o[:, j], o_rows[b, j]).then_inc(o_loaded[j], 16)

                def load_x(b, j):
                    e.dma_start(x[:, j], tiles(x_d)[b, j]).then_inc(x_loaded[j], 16)

                def stages(a, b, c, d, loads=True):
                    if a is not None:
                        e.wait_ge(o_free, 1)
                        if loads:
                            load_o(a[0] + 1, a[1])
                        take(e, (o_free, 1))
                    if d is not None:
                        if layer == 0:
                            e.wait_ge(weights_ready, 1)
                            e.dma_start(tiles(xg_d[0:N])[d[0], d[1]], xn[:, d[1]]).then_inc(r_stored[d[1]], 16)
                            take(e, (weights_ready, 1))
                        e.wait_ge(rt_ready, 1)
                        e.dma_start(r_rows[d[0], d[1]], rt[:, d[1]]).then_inc(r_stored[d[1]], 16)
                        take(e, (rt_ready, 1))
                    if c is not None:
                        j = c[1]
                        e.wait_ge(xl_ready, 1)
                        e.sem_inc(xhl_relayed, 1)
                        e.dma_start(turned(xh_d)[c[0], j], xh[:, j].bitcast(fp32)).then_inc(x_stored[j], 16)
                        e.dma_start(turned(xl_d)[c[0], j], xl[:, j].bitcast(fp32)).then_inc(x_stored[j], 16)
                        e.dma_start(tiles(xo_d)[c[0], j], xo[:, j]).then_inc(x_stored[j], 16)
                        if a is not None:
                            load_x(a[0], a[1])
                        take(e, (xl_ready, 1))

                e.dma_start(wf[:, :, 0:C], wp_d).then_inc(w_loaded, 16)
                e.dma_start(wf[:, :, C:C + E], rw_d).then_inc(w_loaded, 16)
                e.dma_start(rbias[:], rb_d.rearrange("(o n) -> o n", o=1).broadcast_to((P, NB))).then_inc(w_loaded, 16)
                if layer == 1:
                    e.dma_start(ybias[:], yb_d.rearrange("(o n) -> o n", o=1).broadcast_to((P, C))
                                ).then_inc(w_loaded, 16)
                for j in range(2):
                    load_o(0, j)
                for j in range(2):
                    load_x(0, j)
                stages((0, 0), None, None, None)
                stages((0, 1), (0, 0), None, None)
                stages((1, 0), (0, 1), (0, 0), None)
                stages((1, 1), (1, 0), (0, 1), (0, 0))
                with e.Fori(2, B - 1) as i:
                    stages((i, 0), (i - 1, 1), (i - 1, 0), (i - 2, 1))
                    stages((i, 1), (i, 0), (i - 1, 1), (i - 1, 0))
                stages((B - 1, 0), (B - 2, 1), (B - 2, 0), (B - 3, 1), False)
                stages((B - 1, 1), (B - 1, 0), (B - 2, 1), (B - 2, 0), False)
                stages(None, (B - 1, 1), (B - 1, 0), (B - 2, 1))
                stages(None, None, (B - 1, 1), (B - 1, 0))
                stages(None, None, None, (B - 1, 1))

            @block.gpsimd
            def _(e):
                step = Chain(e, pool_chain)
                identity(e, step, ident)
                step(e.memset(mhalf[:], -0.5))
                e.sem_inc(pe_consts, 1)
                step.close()

                def stages(a, b, c, d):
                    if c is not None:
                        e.wait_ge(xvar_ready, 1)
                        e.tensor_tensor(rs[:, 1], ve[:, 1], mhalf[:], ALU.pow).then_inc(xrstd_ready, 1)
                        take(e, (xvar_ready, 1))
                    if b is not None:
                        e.wait_ge(yvar_ready, 1)
                        e.tensor_tensor(rs[:, 0], ve[:, 0], mhalf[:], ALU.pow).then_inc(yrstd_ready, 1)
                        take(e, (yvar_ready, 1))

                pipeline(e, stages)

            @block.vector
            def _(e):
                step = Chain(e, dve_chain)
                e.wait_ge(w_loaded, 48 if layer == 0 else 64)
                split_weights(e, step, wf, wh, wl)
                step(e.memset(sb[:, :, E:E + 8 - K], 3e38))
                step(e.memset(pick[:, :, K:8], 3e38))
                e.sem_inc(pe_consts, 1)
                step.close()

                def residual(j):
                    e.wait_ge(x_loaded[j], 16)
                    e.wait_ge(yn_ready, 1)
                    e.sem_inc(y_free, 1)
                    step(e.tensor_tensor(xo[:, j], x[:, j], yn[:], ALU.add))
                    variance(e, step, xo[:, j], st[:, 1], mv[:, 1], ve[:, 1], xvar_ready)
                    take(e, (x_loaded[j], 16), (yn_ready, 1))

                def projected():
                    e.wait_ge(y_ready, 1)
                    if layer == 1:
                        step(e.tensor_tensor(y[:], y_ps[:], ybias[:].unsqueeze(1).broadcast_to((P, TPB, C)), ALU.add))
                    variance(e, step, y, st[:, 0], mv[:, 0], ve[:, 0], yvar_ready)
                    take(e, (y_ready, 1))

                def divide():
                    for t in range(TPB):
                        e.wait_ge(o_turned, t + 1)
                        heads = o_ps[:, t % 2].rearrange("p g (h d) -> p (g h) d", d=32)
                        if layer == 0:
                            step(e.reciprocal(rden[:, t], heads[:, :, HD]))
                        else:
                            step(e.tensor_scalar(den[:], heads[:, :, HD], 1e-6, None, ALU.add))
                            step(e.reciprocal(rden[:, t], den[:]))
                        e.tensor_tensor(att[:, t].rearrange("p (h d) -> p h d", d=HD), heads[:, :, 0:HD],
                                        rden[:, t].unsqueeze(2).broadcast_to((P, NH, HD)), ALU.mult
                                        ).then_inc(att_ready, 1)
                    take(e, (o_turned, TPB))

                def softmax_shift():
                    e.wait_ge(logits, 1)
                    step(e.reduce_max(lmax[:], l_ps[:], AX.X))
                    e.tensor_tensor(ls[:], l_ps[:], lmax[:].unsqueeze(2).broadcast_to((P, TPB, E)), ALU.subtract
                                    ).then_inc(shifted, 1)
                    take(e, (logits, 1))

                def choose(j):
                    e.wait_ge(scores, 1)
                    if layer == 1:
                        step(e.reduce_sum(ssum[:], sc[:], AX.X))
                        step(e.reciprocal(ssum[:], ssum[:]))
                        step(e.tensor_tensor(sc[:], sc[:], ssum[:].unsqueeze(2).broadcast_to((P, TPB, E)), ALU.mult))
                    step(e.tensor_tensor(sb[:, :, 0:E], sc[:], rbias[:].unsqueeze(1).broadcast_to((P, TPB, E)),
                                         ALU.add))
                    for t in range(TPB):
                        e.max(top[:, t], sb[:, t, 0:E])
                    step.settle()
                    step(e.tensor_copy(pick[:, :, 0:K], top[:, :, 0:K]))
                    for t in range(TPB):
                        e.match_replace(rep[:, t], pick[:, t], sb[:, t], -3e38)
                    step.settle()
                    choice = e.tensor_scalar(mask[:], rep[:, :, 0:E], -1e38, None, ALU.is_lt)
                    if layer == 0:
                        choice.then_inc(choice_ready, 1)
                        step.settle()
                    else:
                        step(choice)
                    step(e.tensor_tensor(sc[:], sc[:], mask[:], ALU.mult))
                    step(e.reduce_sum(ssum[:], sc[:], AX.X))
                    step(e.tensor_scalar(ssum[:], ssum[:], 1e-20, None, ALU.add))
                    step(e.reciprocal(ssum[:], ssum[:]))
                    weights = xn[:, j, :, C:XW] if layer == 0 else mask[:]
                    e.tensor_tensor(weights, sc[:], ssum[:].unsqueeze(2).broadcast_to((P, TPB, E)), ALU.mult
                                    ).then_inc(weights_ready if layer == 0 else choice_ready, 1)
                    take(e, (scores, 1))

                def stages(a, b, c, d):
                    if c is not None:
                        residual(c[1])
                    if b is not None:
                        projected()
                    if c is not None:
                        scaling(e, mv[:, 1], rs[:, 1], nmr[:, 1], xrstd_ready, x_scale)
                    if a is not None:
                        divide()
                    if b is not None:
                        scaling(e, mv[:, 0], rs[:, 0], nmr[:, 0], yrstd_ready, y_scale)
                    if layer == 1 and d is not None:
                        softmax_shift()
                    if d is not None:
                        choose(d[1])
                    if a is not None:
                        e.wait_ge(ah_ready, 1)
                        e.tensor_tensor(al[:], t_ps[:], ah[:].bitcast(fp32), ALU.subtract).then_inc(al_ready, 1)
                        take(e, (ah_ready, 1))
                    if c is not None:
                        e.wait_ge(xh_ready, 1)
                        e.tensor_tensor(xl[:, c[1]], t_ps[:], xh[:, c[1]].bitcast(fp32), ALU.subtract
                                        ).then_inc(xl_ready, 1)
                        take(e, (xh_ready, 1))
                    step.close()

                pipeline(e, stages)

            @block.scalar
            def _(e):
                for j in range(2):
                    e.sem_inc(x_stored[j], X_STORES)
                    e.sem_inc(r_stored[j], R_STORES)

                def stages(a, b, c, d):
                    if c is not None:
                        j = c[1]
                        e.wait_ge(r_stored[j], R_STORES)
                        e.wait_ge(x_scale, 1)
                        for t in range(TPB):
                            e.activation(xn[:, j, t, 0:C], xo[:, j, t], ACT.Identity, bias=nmr[:, 1, t:t + 1],
                                         scale=rs[:, 1, t:t + 1]).then_inc(xn_ready, 1)
                        take(e, (r_stored[j], R_STORES), (x_scale, 1))
                    if b is not None:
                        j = b[1]
                        e.wait_ge(x_stored[j], X_STORES)
                        e.wait_ge(y_scale, 1)
                        for t in range(TPB):
                            i = e.activation(yn[:, t], y[:, t], ACT.Identity, bias=nmr[:, 0, t:t + 1],
                                             scale=rs[:, 0, t:t + 1])
                        i.then_inc(yn_ready, 1)
                        take(e, (x_stored[j], X_STORES), (y_scale, 1))
                    if d is not None:
                        if layer == 0:
                            e.wait_ge(logits, 1)
                            e.activation(sc[:], l_ps[:], ACT.Sigmoid).then_inc(scores, 1)
                            take(e, (logits, 1))
                        else:
                            e.wait_ge(shifted, 1)
                            e.activation(sc[:], ls[:], ACT.Exp).then_inc(scores, 1)
                            take(e, (shifted, 1))
                    if a is not None:
                        e.wait_ge(att_turned, 1)
                        e.activation(ah[:], t_ps[:], ACT.Copy).then_inc(ah_ready, 1)
                        take(e, (att_turned, 1))
                    if c is not None:
                        e.wait_ge(xn_turned, 1)
                        e.activation(xh[:, c[1]], t_ps[:], ACT.Copy).then_inc(xh_ready, 1)
                        take(e, (xn_turned, 1))
                    if d is not None:
                        e.wait_ge(choice_turned, 1)
                        e.activation(rt[:, d[1]], r_ps[:], ACT.Copy).then_inc(rt_ready, 1)
                        take(e, (choice_turned, 1))

                pipeline(e, stages)
                for j in range(2):
                    e.wait_ge(x_stored[j], X_STORES)
                    e.wait_ge(r_stored[j], R_STORES)

            @block.tensor
            def _(e):
                e.wait_ge(pe_consts, 2)
                e.sem_inc(y_free, 1)

                def turn(src, ready):
                    for t in range(TPB):
                        e.wait_ge(ready, t + 1)
                        for k in range(KC):
                            i = e.transpose(t_ps[:, k, t * P:(t + 1) * P], src[:, t, k * P:(k + 1) * P], ident[:])
                    return i

                def stages(a, b, c, d):
                    if b is not None:
                        e.wait_ge(al_ready, 1)
                        e.wait_ge(y_free, 1)
                        for t in range(TPB):
                            cols = slice(t * P, (t + 1) * P)
                            i = product(e, y_ps[:, t], (lambda k: ah[:, k, cols], lambda k: al[:, k, cols]),
                                        (lambda k: wh[:, k, 0:C], lambda k: wl[:, k, 0:C]), KC)
                        i.then_inc(y_ready, 1)
                        take(e, (al_ready, 1), (y_free, 1))
                    if a is not None:
                        e.wait_ge(o_loaded[a[1]], 16)
                        for t in range(TPB):
                            if t >= 2:
                                e.wait_ge(att_ready, t - 1)
                            for g in range(NG):
                                i = e.transpose(o_ps[:, t % 2, g], o[:, a[1], g, t * P:(t + 1) * P], ident[:])
                            i.then_inc(o_turned, 1)
                        take(e, (o_loaded[a[1]], 16))
                    if d is not None:
                        e.wait_ge(xhl_relayed, 1)
                        for t in range(TPB):
                            cols = slice(t * P, (t + 1) * P)
                            i = product(e, l_ps[:, t], (lambda k: xh[:, d[1], k, cols], lambda k: xl[:, d[1], k, cols]),
                                        (lambda k: wh[:, k, C:C + E], lambda k: wl[:, k, C:C + E]), KC)
                        i.then_inc(logits, 1)
                        take(e, (xhl_relayed, 1))
                    if a is not None:
                        turn(att, att_ready).then_inc(att_turned, 1)
                        e.sem_inc(o_free, 1)
                        take(e, (att_ready, TPB))
                    if c is not None:
                        if a is not None:
                            e.wait_ge(al_ready, 1)
                        turn(xn[:, c[1]], xn_ready).then_inc(xn_turned, 1)
                        take(e, (xn_ready, TPB))
                    if d is not None:
                        e.wait_ge(choice_ready, 1)
                        for t in range(TPB):
                            i = e.transpose(r_ps[:, t * P:(t + 1) * P], mask[:, t], ident[:])
                        i.then_inc(choice_turned, 1)
                        take(e, (choice_ready, 1))

                pipeline(e, stages)


DUMMY = CAP


def phase_shared_and_slots(nc, xh_d, xl_d, s1_d, s2_d, mt_d, acc0_d, acc1_d, xg_d, slots):
    HALF = N // 2
    ROUNDS = CAP // 8
    with Phase(nc, "shf") as ph:
        w1f = ph.sb("w1f", [P, KC, SF0])
        w1h = ph.sb("w1h", [P, KC, SF0], f32r)
        w1l = ph.sb("w1l", [P, KC, SF0], f32r)
        NF = SF0 // P
        w2f = ph.sb("w2f", [P, NF, C])
        w2h = ph.sb("w2h", [P, NF, C], f32r)
        w2l = ph.sb("w2l", [P, NF, C], f32r)
        xh = ph.sb("xh", [P, 2, KC, BLK], f32r)
        xl = ph.sb("xl", [P, 2, KC, BLK], f32r)
        hg = ph.sb("hg", [P, 2, NF, BLK])
        hh = ph.sb("hh", [P, 2, NF, BLK], f32r)
        hl = ph.sb("hl", [P, 2, NF, BLK], f32r)
        out = ph.sb("out", [P, 2, TPB, C])
        zero = ph.sb("zero", [P, 2048])
        key = ph.sb("key", [P, HALF])
        early = ph.sb("early", [P, HALF])
        val = ph.sb("val", [P, CAP])
        both = ph.sb("both", [E0, 2, CAP])
        first = ph.sb("first", [E0, CAP])
        slot_no = ph.sb("slot_no", [E0, CAP])
        ident = ph.sb("ident", [P, P])
        h_ps = ph.ps("h_ps", [P, NF, BLK])
        y_ps = ph.ps("y_ps", [P, TPB, C])
        i_ps = ph.ps("i_ps", [CAP, E0])

        w_loaded = ph.sem("w_loaded")
        w_split = ph.sem("w_split")
        pool_chain = ph.sem("pool_chain")
        dve_chain = ph.sem("dve_chain")
        loaded = [ph.sem(f"loaded{j}") for j in range(2)]
        zeros_ready = ph.sem("zeros_ready")
        zeros_stored = ph.sem("zeros_stored")
        iotas_ready = ph.sem("iotas_ready")
        choice_loaded = ph.sem("choice_loaded")
        moved = ph.sem("moved")
        local_ready = ph.sem("local_ready")
        list_ready = ph.sem("list_ready")
        list_turned = ph.sem("list_turned")
        h_ready = ph.sem("h_ready")
        h_free = ph.sem("h_free")
        x_free = ph.sem("x_free")
        hg_ready = ph.sem("hg_ready")
        gelu_done = ph.sem("gelu_done")
        hl_ready = ph.sem("hl_ready")
        y_ready = ph.sem("y_ready")
        out_ready = ph.sem("out_ready")
        y_free = ph.sem("y_free")
        stored = [ph.sem(f"stored{j}") for j in range(2)]

        def turned(d):
            return d.rearrange("(b c p) (j t) -> b j p c t", b=B, p=P, j=2)

        acc0_v = acc0_d[0:N].rearrange("(b j t p) c -> b j p t c", j=2, t=TPB, p=P)
        ZR = 2048 // C
        acc1_v = acc1_d[0:N].rearrange("(n p r) c -> n p (r c)", p=P, r=ZR)

        with nc.Block() as block:
            @block.sync
            def _(e):
                def load(b, j):
                    e.dma_start(xh[:, j].bitcast(fp32), turned(xh_d)[b, j]).then_inc(loaded[j], 16)
                    e.dma_start(xl[:, j].bitcast(fp32), turned(xl_d)[b, j]).then_inc(loaded[j], 16)

                def store(b, j):
                    e.wait_ge(out_ready, 1)
                    e.sem_inc(y_free, 1)
                    e.dma_start(acc0_v[b, j], out[:, j]).then_inc(stored[j], 16)
                    take(e, (out_ready, 1))

                e.dma_start(w1f[:], s1_d).then_inc(w_loaded, 16)
                e.dma_start(w2f[:], s2_d).then_inc(w_loaded, 16)
                for j in range(2):
                    load(0, j)

                def reload(b, j):
                    e.wait_ge(x_free, 1)
                    load(b + 1, j)
                    take(e, (x_free, 1))

                def blocks(first, last):
                    with e.Fori(first, last) as b:
                        reload(b, 0)
                        store(b - 1, 1)
                        reload(b, 1)
                        store(b, 0)

                MOVE = B - 2
                reload(0, 0)
                reload(0, 1)
                store(0, 0)
                blocks(1, MOVE)
                e.wait_ge(local_ready, 1)
                e.dma_start(both[:, 1], val[E0:P]).then_inc(moved, 16)
                blocks(MOVE, B - 1)
                store(B - 2, 1)
                for j in range(2):
                    store(B - 1, j)

            @block.gpsimd
            def _(e):
                step = Chain(e, pool_chain)
                identity(e, step, ident)
                step(e.memset(zero[:], 0.0))
                e.sem_inc(zeros_ready, 1)
                step(e.iota(early[:], [[-1, HALF]], base=HALF, channel_multiplier=0,
                            allow_small_or_imprecise_dtypes=True))
                e.sem_inc(iotas_ready, 1)
                step(e.iota(slot_no[:], [[1, CAP]], base=0, channel_multiplier=0,
                            allow_small_or_imprecise_dtypes=True))
                e.sem_inc(iotas_ready, 1)
                step.close()
                with e.Fori(0, B):
                    for j in range(2):
                        e.wait_ge(hg_ready, 1)
                        e.sem_inc(x_free, 1)
                        e.tensor_tensor(hl[:, j], hg[:, j], hh[:, j].bitcast(fp32), ALU.subtract
                                        ).then_inc(hl_ready, 1)
                        take(e, (hg_ready, 1))

            @block.vector
            def _(e):
                step = Chain(e, dve_chain)
                e.wait_ge(w_loaded, 32)
                split_weights(e, step, w1f, w1h, w1l)
                split_weights(e, step, w2f, w2h, w2l)
                e.sem_inc(w_split, 1)
                e.wait_ge(choice_loaded, 32)
                e.wait_ge(iotas_ready, 2)
                step(e.tensor_tensor(key[:], key[:], early[:], ALU.mult))

                def largest(dst, src):
                    for r in range(ROUNDS):
                        step(e.max(dst[:, 8 * r:8 * r + 8], src))
                        step(e.match_replace(src, dst[:, 8 * r:8 * r + 8], src, -1.0))

                largest(val[:], key[:])
                step(e.tensor_scalar(first[:], val[0:E0], 0.0, float(HALF), ALU.is_gt, ALU.mult))
                step(e.tensor_scalar(val[:], val[:], 0.0, None, ALU.max))
                step(e.tensor_tensor(both[:, 0], val[0:E0], first[:], ALU.add))
                e.sem_inc(local_ready, 1)
                e.wait_ge(moved, 16)
                largest(first[:], both[:].rearrange("e h c -> e (h c)"))
                step(e.tensor_scalar(first[:], first[:], 0.0, None, ALU.max))
                step(e.tensor_scalar(both[:, 0], first[:], 0.0, None, ALU.is_equal))
                step(e.tensor_tensor(both[:, 0], both[:, 0], slot_no[:], ALU.mult))
                step(e.tensor_scalar(first[:], first[:], -1.0, float(N), ALU.mult, ALU.add))
                e.tensor_tensor(first[:], first[:], both[:, 0], ALU.add).then_inc(list_ready, 1)
                e.wait_ge(list_turned, 1)
                step(e.tensor_copy(slots[:], i_ps[:]))

            @block.scalar
            def _(e):
                for h in range(2):
                    e.dma_start(key[h * E0:(h + 1) * E0], mt_d[:, h * HALF:(h + 1) * HALF]).then_inc(choice_loaded, 16)
                e.wait_ge(zeros_ready, 1)
                for n in range(N // (P * ZR)):
                    e.dma_start(acc1_v[n], zero[:]).then_inc(zeros_stored, 16)
                for d in (acc0_d, acc1_d):
                    e.dma_start(d[N:N + DUMMY], zero[0:DUMMY, 0:C]).then_inc(zeros_stored, 16)
                e.dma_start(xg_d[N:N + DUMMY], zero[0:DUMMY, 0:XW]).then_inc(zeros_stored, 16)
                for j in range(2):
                    e.sem_inc(stored[j], 16)

                def hidden(j):
                    for f in range(NF):
                        e.wait_ge(h_ready, f + 1)
                        e.activation(hg[:, j, f], h_ps[:, f], ACT.Gelu_apprx_tanh).then_inc(h_free, 1)
                    e.drain().then_inc(gelu_done, 1)
                    e.wait_ge(gelu_done, 1)
                    e.activation(hh[:, j], hg[:, j], ACT.Copy).then_inc(hg_ready, 1)
                    take(e, (h_ready, NF), (gelu_done, 1))

                def output(j):
                    e.wait_ge(stored[j], 16)
                    e.wait_ge(y_ready, 1)
                    e.activation(out[:, j], y_ps[:], ACT.Copy).then_inc(out_ready, 1)
                    take(e, (stored[j], 16), (y_ready, 1))

                hidden(0)
                hidden(1)
                output(0)
                with e.Fori(1, B):
                    for j in range(2):
                        hidden(j)
                        output(1 - j)
                output(1)
                for j in range(2):
                    e.wait_ge(stored[j], 16)
                e.wait_ge(zeros_stored, 16 * (N // (P * ZR) + 3))

            @block.tensor
            def _(e):
                def hidden(j):
                    e.wait_ge(loaded[j], 32)
                    for f in range(NF):
                        e.wait_ge(h_free, f + 1)
                        cols = slice(f * P, (f + 1) * P)
                        product(e, h_ps[:, f], (lambda k: w1h[:, k, cols], lambda k: w1l[:, k, cols]),
                                (lambda k: xh[:, j, k], lambda k: xl[:, j, k]), KC).then_inc(h_ready, 1)
                    take(e, (loaded[j], 32), (h_free, NF))

                def output(j):
                    e.wait_ge(hl_ready, 1)
                    e.wait_ge(y_free, 1)
                    for t in range(TPB):
                        cols = slice(t * P, (t + 1) * P)
                        i = product(e, y_ps[:, t], (lambda k: hh[:, j, k, cols], lambda k: hl[:, j, k, cols]),
                                    (lambda k: w2h[:, k], lambda k: w2l[:, k]), NF)
                    i.then_inc(y_ready, 1)
                    take(e, (hl_ready, 1), (y_free, 1))

                e.sem_inc(h_free, NF)
                e.sem_inc(y_free, 1)
                e.wait_ge(w_split, 1)
                hidden(0)
                hidden(1)
                output(0)
                with e.Fori(1, B):
                    for j in range(2):
                        hidden(j)
                        output(1 - j)
                output(1)
                e.wait_ge(list_ready, 1)
                e.transpose(i_ps[:], first[:], ident[0:E0, 0:E0]).then_inc(list_turned, 1)


def phase_experts(nc, slots, xg_d, w1_d, w2_d, acc0_d, acc1_d):
    PAIRS = E0 // 2
    SETS = 3
    NW = 2 * SETS
    LOOPS = (PAIRS - 2) // SETS
    assert 1 + LOOPS * SETS + 1 == PAIRS
    with Phase(nc, "exp") as ph:
        cur = [ph.sb(f"cur{j}", [CAP, 1], i32) for j in range(NW)]
        xs = ph.sb("xs", [CAP, NW, XW])
        xt = ph.sb("xt", [P, 2, KC, CAP])
        w1 = ph.sb("w1", [P, NW, KC, F0])
        w2 = ph.sb("w2", [P, NW, C])
        h = ph.sb("h", [P, 2, CAP])
        y = ph.sb("y", [CAP, NW, C])
        ident = ph.sb("ident", [P, P])
        t_ps = ph.ps("t_ps", [P, 2, BLK])
        h_ps = ph.ps("h_ps", [P, 2, BLK])
        y_ps = ph.ps("y_ps", [CAP, 2, BLK])

        pool_chain = ph.sem("pool_chain")
        ident_ready = ph.sem("ident_ready")
        w_loaded = [ph.sem(f"w_loaded{j}") for j in range(NW)]
        w_free = ph.sem("w_free")
        gathered = [ph.sem(f"gathered{j}") for j in range(NW)]
        x_turned = ph.sem("x_turned")
        xt_ready = ph.sem("xt_ready")
        h_ready = ph.sem("h_ready")
        gelu_ready = ph.sem("gelu_ready")
        y_ready = ph.sem("y_ready")
        out_ready = ph.sem("out_ready")
        added = [ph.sem(f"added{j}") for j in range(2)]
        accs = (acc0_d, acc1_d)

        def pairs(e, pair):
            pair(0, 0, 0)
            with e.Fori(0, LOOPS) as i:
                for n in range(1, SETS + 1):
                    pair(i * SETS + n, n % SETS, i + n // SETS)
            pair(PAIRS - 1, (PAIRS - 1) % SETS, (PAIRS - 1) // SETS)

        with nc.Block() as block:
            @block.sync
            def _(e):
                def load(expert, buf):
                    e.wait_ge(w_free, 1)
                    e.dma_start(w1[:, buf], w1_d.rearrange("e (k p) f -> e p k f", p=P)[expert]
                                ).then_inc(w_loaded[buf], 16)
                    e.dma_start(w2[:, buf], w2_d[expert]).then_inc(w_loaded[buf], 16)
                    take(e, (w_free, 1))

                e.sem_inc(w_free, NW)
                with e.Fori(0, E0 // NW) as i:
                    for j in range(NW):
                        load(i * NW + j, j)
                for j in range(E0 % NW):
                    load(E0 // NW * NW + j, j)

            @block.gpsimd
            def _(e):
                step = Chain(e, pool_chain)
                identity(e, step, ident)
                e.sem_inc(ident_ready, 1)

                def gather(n, s):
                    for j in range(2):
                        step(e.tensor_copy(cur[2 * s + j][:], slots[:, bass.ds(n * 2 + j, 1)]))
                    for j in range(2):
                        b = 2 * s + j
                        e.indirect_dma_start(xs[:, b], None, xg_d, bass.IndirectOffsetOnAxis(ap=cur[b][:], axis=0)
                                             ).then_inc(gathered[b], 16)

                def pair(n, s, turn):
                    if not (isinstance(n, int) and n == PAIRS - 1):
                        gather(n + 1, (s + 1) % SETS)
                    for j in range(2):
                        b = 2 * s + j
                        e.wait_ge(out_ready, 1)
                        if not (isinstance(n, int) and n == 0):
                            e.wait_ge(added[j], n * 16)
                        take(e, (out_ready, 1))
                        e.indirect_dma_start(accs[j], bass.IndirectOffsetOnAxis(ap=cur[b][:], axis=0), y[:, b], None,
                                             compute_op=ALU.add).then_inc(added[j], 16)
                    step.close()

                gather(0, 0)
                pairs(e, pair)
                for j in range(2):
                    e.wait_ge(added[j], 16 * PAIRS)

            @block.vector
            def _(e):
                def pair(n, s, turn):
                    for j in range(2):
                        e.wait_ge(x_turned, j + 1)
                        e.tensor_copy(xt[:, j], t_ps[:, j, 0:KC * CAP].rearrange("p (k c) -> p k c", k=KC)
                                      ).then_inc(xt_ready, 1)
                    for j in range(2):
                        e.wait_ge(y_ready, j + 1)
                        e.tensor_scalar(y[:, 2 * s + j], y_ps[:, j, 0:C], xs[:, 2 * s + j, bass.ds(n * 2 + j + C, 1)],
                                        None, ALU.mult).then_inc(out_ready, 1)
                    take(e, (x_turned, 2), (y_ready, 2))

                pairs(e, pair)

            @block.scalar
            def _(e):
                def pair(n, s, turn):
                    for j in range(2):
                        e.wait_ge(h_ready, j + 1)
                        e.activation(h[:, j], h_ps[:, j, 0:CAP], ACT.Gelu_apprx_tanh).then_inc(gelu_ready, 1)
                    take(e, (h_ready, 2))

                pairs(e, pair)

            @block.tensor
            def _(e):
                def pair(n, s, turn):
                    for j in range(2):
                        e.wait_ge(gathered[2 * s + j], turn * 16 + 16)
                        for k in range(KC):
                            i = e.transpose(t_ps[:, j, k * CAP:(k + 1) * CAP], xs[:, 2 * s + j, k * P:(k + 1) * P],
                                            ident[0:CAP, 0:CAP])
                        i.then_inc(x_turned, 1)
                    for j in range(2):
                        b = 2 * s + j
                        e.wait_ge(xt_ready, j + 1)
                        e.wait_ge(w_loaded[b], 32)
                        for k in range(KC):
                            i = e.matmul(h_ps[:, j, 0:CAP], w1[:, b, k], xt[:, j, k], start=k == 0, stop=k == KC - 1)
                        i.then_inc(h_ready, 1)
                    for j in range(2):
                        b = 2 * s + j
                        e.wait_ge(gelu_ready, j + 1)
                        e.matmul(y_ps[:, j, 0:C], h[:, j], w2[:, b], start=True, stop=True).then_inc(y_ready, 1)
                        take(e, (w_loaded[b], 32))
                    take(e, (xt_ready, 2), (gelu_ready, 2))
                    e.drain().then_inc(w_free, 2)

                e.wait_ge(ident_ready, 1)
                pairs(e, pair)


def normaliser(e, step, src, st, mv, ve, rs, nmr, var_ready, rstd_ready, signal):
    for t in range(TPB):
        e.bn_stats(st[:, t], src[:, t])
    step.settle()
    for t in range(TPB):
        e.bn_aggr(mv[:, t], st[:, t])
    step.settle()
    e.tensor_scalar(ve[:], mv[:, :, 1], EPS, None, ALU.add).then_inc(var_ready, 1)
    e.wait_ge(rstd_ready, 1)
    e.scalar_tensor_tensor(nmr[:], mv[:, :, 0], -1.0, rs[:], ALU.mult, ALU.mult).then_inc(signal, 1)
    take(e, (rstd_ready, 1))


def phase_linear_qkv(nc, x1_d, acc0_d, acc1_d, w_d, bqk_d, bv_d, x2_d, fq_d, fqh_d, fql_d, fkh_d, fkl_d, fkt_d, v_d):
    FE = 1e-4
    with Phase(nc, "lqk") as ph:
        wf = ph.sb("wf", [P, KC, 3 * C])
        wh = ph.sb("wh", [P, KC, 3 * C], f32r)
        wl = ph.sb("wl", [P, KC, 3 * C], f32r)
        bqk = ph.sb("bqk", [P, 4])
        bqke = ph.sb("bqke", [P, 4])
        bv = ph.sb("bv", [P, C])
        ident = ph.sb("ident", [P, P])
        mhalf = ph.sb("mhalf", [P, TPB])
        x1 = ph.sb("x1", [P, 2, TPB, C])
        a0 = ph.sb("a0", [P, 2, TPB, C])
        a1 = ph.sb("a1", [P, 2, TPB, C])
        st = ph.sb("st", [P, TPB, 6])
        mv = ph.sb("mv", [P, TPB, 2])
        ve = ph.sb("ve", [P, TPB])
        rs = ph.sb("rs", [P, TPB])
        nmr = ph.sb("nmr", [P, TPB])
        xn = ph.sb("xn", [P, TPB, C])
        xh = ph.sb("xh", [P, KC, BLK], f32r)
        xl = ph.sb("xl", [P, KC, BLK], f32r)
        ex = ph.sb("ex", [P, 2, BLK])
        re = ph.sb("re", [P, 2, BLK])
        phi = ph.sb("phi", [P, 4, BLK])
        oh = ph.sb("oh", [P, 4, BLK], f32r)
        ol = ph.sb("ol", [P, 4, BLK], f32r)
        kt = ph.sb("kt", [P, 2, TPB, P])
        vo = ph.sb("vo", [P, TPB, NH, VW])
        t_ps = ph.ps("t_ps", [P, 2, BLK])
        qk = ph.ps("qk", [P, 4, BLK])
        vp = ph.ps("vp", [P, TPB, C])

        w_loaded = ph.sem("w_loaded")
        pe_consts = ph.sem("pe_consts")
        ones_ready = ph.sem("ones_ready")
        bias_ready = ph.sem("bias_ready")
        pool_chain = ph.sem("pool_chain")
        dve_chain = ph.sem("dve_chain")
        loaded = [ph.sem(f"loaded{j}") for j in range(2)]
        sum_ready = ph.sem("sum_ready")
        var_ready = ph.sem("var_ready")
        rstd_ready = ph.sem("rstd_ready")
        y_scale = ph.sem("y_scale")
        yn_ready = ph.sem("yn_ready")
        x_scale = ph.sem("x_scale")
        xn_ready = ph.sem("xn_ready")
        xn_turned = ph.sem("xn_turned")
        xh_ready = ph.sem("xh_ready")
        xl_ready = ph.sem("xl_ready")
        qk_ready = ph.sem("qk_ready")
        exp_ready = ph.sem("exp_ready")
        phi_ready = ph.sem("phi_ready")
        oh_ready = ph.sem("oh_ready")
        ol_ready = ph.sem("ol_ready")
        phi_relayed = ph.sem("phi_relayed")
        k_turned = ph.sem("k_turned")
        kt_ready = ph.sem("kt_ready")
        v_ready = ph.sem("v_ready")
        vo_ready = ph.sem("vo_ready")
        loads_due = ph.sem("loads_due")
        drained = ph.sem("drained")
        stored = ph.sem("stored")
        STORES = 16 * (1 + 5 + 2 + 8)

        def tiles(d):
            return d.rearrange("(b j t p) c -> b j p t c", j=2, t=TPB, p=P)

        def turned(d):
            return d.rearrange("(b c p) (j t) -> b j p c t", b=B, p=P, j=2)

        kt_v = fkt_d.rearrange("(b f j t p) c -> b j f p t c", b=B, f=2, j=2, t=TPB)
        v_v = v_d.rearrange("(b f j t p) c -> b j f t p c", b=B, f=2, j=2, t=TPB)

        with nc.Block() as block:
            @block.sync
            def _(e):
                def load(b, j):
                    e.dma_start(a0[:, j], tiles(acc0_d[0:N])[b, j]).then_inc(loaded[j], 16)
                    e.dma_start(a1[:, j], tiles(acc1_d[0:N])[b, j]).then_inc(loaded[j], 16)
                    e.dma_start(x1[:, j], tiles(x1_d)[b, j]).then_inc(loaded[j], 16)

                def store(b, j):
                    e.wait_ge(phi_ready, 4)
                    e.sem_inc(phi_relayed, 1)
                    e.dma_start(tiles(x2_d)[b, j], x1[:, j]).then_inc(stored, 16)
                    e.dma_start(turned(fq_d)[b, j], phi[:, 0:2]).then_inc(stored, 16)
                    e.wait_ge(vo_ready, 1)
                    for f in range(2):
                        for t in range(TPB):
                            e.dma_start(v_v[b, j, f, t], vo[:, t, 8 * f:8 * f + 8].rearrange("p h d -> p (h d)")
                                        ).then_inc(stored, 16)
                    e.wait_ge(ol_ready, 4)
                    for d, s, c in ((fqh_d, oh, 0), (fkh_d, oh, 2), (fql_d, ol, 0), (fkl_d, ol, 2)):
                        e.dma_start(turned(d)[b, j], s[:, c:c + 2].bitcast(fp32)).then_inc(stored, 16)
                    e.wait_ge(kt_ready, 1)
                    for f in range(2):
                        e.dma_start(kt_v[b, j, f], kt[:, f]).then_inc(stored, 16)
                    take(e, (phi_ready, 4), (vo_ready, 1), (ol_ready, 4), (kt_ready, 1))

                e.dma_start(wf[:], w_d).then_inc(w_loaded, 16)
                e.dma_start(bqk[:], bqk_d).then_inc(w_loaded, 16)
                e.dma_start(bv[:], bv_d.rearrange("(o n) -> o n", o=1).broadcast_to((P, C))).then_inc(w_loaded, 16)
                for j in range(2):
                    load(0, j)
                with e.Fori(0, B - 1) as b:
                    for j in range(2):
                        store(b, j)
                        e.wait_ge(loads_due, 1)
                        load(b + 1, j)
                        take(e, (loads_due, 1))
                for j in range(2):
                    store(B - 1, j)

            @block.gpsimd
            def _(e):
                step = Chain(e, pool_chain)
                identity(e, step, ident)
                step(e.memset(mhalf[:], -0.5))
                e.sem_inc(pe_consts, 1)
                step(e.memset(vo[:].rearrange("p t h d -> p (t h) d")[:, :, HD:VW], 1.0))
                e.sem_inc(ones_ready, 1)
                step.close()
                with e.Fori(0, B):
                    for j in range(2):
                        e.wait_ge(loaded[j], 48)
                        e.tensor_tensor(a0[:, j], a0[:, j], a1[:, j], ALU.add).then_inc(sum_ready, 1)
                        for _ in range(2):
                            e.wait_ge(var_ready, 1)
                            e.tensor_tensor(rs[:], ve[:], mhalf[:], ALU.pow).then_inc(rstd_ready, 1)
                            take(e, (var_ready, 1))
                        for c in range(4):
                            e.wait_ge(oh_ready, c + 1)
                            e.tensor_tensor(ol[:, c], phi[:, c], oh[:, c].bitcast(fp32), ALU.subtract
                                            ).then_inc(ol_ready, 1)
                        take(e, (loaded[j], 48), (oh_ready, 4))

            @block.vector
            def _(e):
                step = Chain(e, dve_chain)
                e.wait_ge(w_loaded, 48)
                step(e.tensor_scalar(wf[:, :, 0:C], wf[:, :, 0:C], HD ** -0.5, None, ALU.mult))
                step(e.tensor_scalar(bqk[:, 0:2], bqk[:, 0:2], HD ** -0.5, None, ALU.mult))
                step(e.tensor_scalar(bqke[:], bqk[:], FE, None, ALU.add))
                e.sem_inc(bias_ready, 1)
                split_weights(e, step, wf, wh, wl)
                e.sem_inc(pe_consts, 1)
                e.wait_ge(ones_ready, 1)
                step.close()
                with e.Fori(0, B):
                    for j in range(2):
                        e.wait_ge(sum_ready, 1)
                        normaliser(e, step, a0[:, j], st, mv, ve, rs, nmr, var_ready, rstd_ready, y_scale)
                        e.wait_ge(yn_ready, 1)
                        step(e.tensor_tensor(x1[:, j], x1[:, j], a1[:, j], ALU.add))
                        normaliser(e, step, x1[:, j], st, mv, ve, rs, nmr, var_ready, rstd_ready, x_scale)
                        e.wait_ge(xh_ready, 1)
                        e.tensor_tensor(xl[:], t_ps[:], xh[:].bitcast(fp32), ALU.subtract).then_inc(xl_ready, 1)
                        for c in range(4):
                            e.wait_ge(exp_ready, c + 1)
                            step(e.tensor_scalar(re[:, c % 2], qk[:, c], bqke[:, c:c + 1], FE, ALU.add, ALU.max))
                            e.scalar_tensor_tensor(phi[:, c], ex[:, c % 2], 1.0, re[:, c % 2], ALU.min, ALU.add
                                                   ).then_inc(phi_ready, 1)
                            e.drain().then_inc(drained, 1)
                        e.wait_ge(v_ready, 1)
                        e.tensor_tensor(vo[:, :, :, 0:HD].rearrange("p t h d -> p t h d"),
                                        vp[:].rearrange("p t (h d) -> p t h d", d=HD),
                                        bv[:].rearrange("p (h d) -> p h d", d=HD).unsqueeze(1)
                                        .broadcast_to((P, TPB, NH, HD)), ALU.add).then_inc(vo_ready, 1)
                        take(e, (sum_ready, 1), (yn_ready, 1), (xh_ready, 1), (exp_ready, 4), (v_ready, 1))
                        step.close()

            @block.scalar
            def _(e):
                e.wait_ge(bias_ready, 1)
                e.sem_inc(stored, STORES)
                with e.Fori(0, B):
                    for j in range(2):
                        e.wait_ge(y_scale, 1)
                        for t in range(TPB):
                            i = e.activation(a1[:, j, t], a0[:, j, t], ACT.Identity, bias=nmr[:, t:t + 1],
                                             scale=rs[:, t:t + 1])
                        i.then_inc(yn_ready, 1)
                        e.wait_ge(x_scale, 1)
                        for t in range(TPB):
                            e.activation(xn[:, t], x1[:, j, t], ACT.Identity, bias=nmr[:, t:t + 1],
                                         scale=rs[:, t:t + 1]).then_inc(xn_ready, 1)
                        e.wait_ge(xn_turned, 1)
                        e.activation(xh[:], t_ps[:], ACT.Copy).then_inc(xh_ready, 1)
                        e.wait_ge(stored, STORES)
                        e.sem_inc(loads_due, 1)
                        for c in range(4):
                            e.wait_ge(qk_ready, c + 1)
                            if c >= 2:
                                e.wait_ge(drained, c - 1)
                            e.activation(ex[:, c % 2], qk[:, c], ACT.Exp, bias=bqk[:, c:c + 1]).then_inc(exp_ready, 1)
                            if c:
                                e.wait_ge(drained, c)
                                e.activation(oh[:, c - 1], phi[:, c - 1], ACT.Copy).then_inc(oh_ready, 1)
                        e.wait_ge(drained, 4)
                        e.activation(oh[:, 3], phi[:, 3], ACT.Copy).then_inc(oh_ready, 1)
                        e.wait_ge(k_turned, 1)
                        e.activation(kt[:], t_ps[:].rearrange("p f (t c) -> p f t c", t=TPB), ACT.Copy
                                     ).then_inc(kt_ready, 1)
                        take(e, (y_scale, 1), (x_scale, 1), (xn_turned, 1), (stored, STORES), (qk_ready, 4),
                             (drained, 4), (k_turned, 1))
                e.wait_ge(stored, STORES)

            @block.tensor
            def _(e):
                e.wait_ge(pe_consts, 2)
                with e.Fori(0, 2 * B):
                    for t in range(TPB):
                        e.wait_ge(xn_ready, t + 1)
                        for k in range(KC):
                            i = e.transpose(t_ps[:, k, t * P:(t + 1) * P], xn[:, t, k * P:(k + 1) * P], ident[:])
                    i.then_inc(xn_turned, 1)
                    e.wait_ge(xl_ready, 1)
                    for c in range(4):
                        cols = slice(c * P, (c + 1) * P)
                        product(e, qk[:, c], (lambda k: wh[:, k, cols], lambda k: wl[:, k, cols]),
                                (lambda k: xh[:, k], lambda k: xl[:, k]), KC).then_inc(qk_ready, 1)
                    for t in range(TPB):
                        cols = slice(t * P, (t + 1) * P)
                        i = product(e, vp[:, t], (lambda k: xh[:, k, cols], lambda k: xl[:, k, cols]),
                                    (lambda k: wh[:, k, 2 * C:3 * C], lambda k: wl[:, k, 2 * C:3 * C]), KC)
                    i.then_inc(v_ready, 1)
                    e.wait_ge(phi_relayed, 1)
                    for f in range(2):
                        for t in range(TPB):
                            i = e.transpose(t_ps[:, f, t * P:(t + 1) * P], phi[:, 2 + f, t * P:(t + 1) * P], ident[:])
                    i.then_inc(k_turned, 1)
                    take(e, (xn_ready, TPB), (xl_ready, 1), (phi_relayed, 1))


def phase_linear_attention(nc, fq_d, fqh_d, fql_d, fkh_d, fkl_d, fkt_d, v_d, o_d):
    G, F = 2 * B, 8
    NBUF = 2
    with Phase(nc, "lin") as ph:
        qx = [ph.sb(f"qx{n}", [P, NBUF, F, T], f32r) for n in ("h", "l")]
        kk = [ph.sb(f"kk{n}", [P, NBUF, T], f32r) for n in ("h", "l")]
        fq = ph.sb("fq", [P, NBUF, T])
        kt = ph.sb("kt", [P, NBUF, KB, P])
        vs = ph.sb("vs", [P, NBUF, KB, F * VW])
        am = ph.sb("am", [P, 2, F, P])
        tri = ph.sb("tri", [P, P])
        own = ph.sb("own", [P, F])
        state = ph.sb("state", [P, F, 32])
        ot = ph.sb("ot", [P, 2, BLK])
        a_ps = ph.ps("a_ps", [P, 2, F // 2, P])
        b_ps = ph.ps("b_ps", [P, 2, F // 2, P])
        o_ps = ph.ps("o_ps", [P, 2, BLK])
        s_ps = ph.ps("s_ps", [P, F, VW])

        zeroed = ph.sem("zeroed")
        pool_chain = ph.sem("pool_chain")
        dve_chain = ph.sem("dve_chain")
        masks_ready = ph.sem("masks_ready")
        loaded = [ph.sem(f"loaded{j}") for j in range(NBUF)]
        a_ready = ph.sem("a_ready")
        am_ready = ph.sem("am_ready")
        s_ready = ph.sem("s_ready")
        state_ready = ph.sem("state_ready")
        o_ready = ph.sem("o_ready")
        ot_ready = ph.sem("ot_ready")
        o_free = ph.sem("o_free")
        ot_stored = ph.sem("ot_stored")
        LOADS = 16 * (2 * F + 5)
        scores = (a_ps, b_ps)

        rows = {n: d.rearrange("(g p) t -> g p t", p=P) for n, d in
                (("fq", fq_d), ("fqh", fqh_d), ("fql", fql_d), ("fkh", fkh_d), ("fkl", fkl_d))}
        kt_rows = fkt_d.rearrange("(g k p) c -> g p k c", k=KB, p=P)
        v_rows = v_d.rearrange("(g k p) c -> g p k c", k=KB, p=P)
        o_rows = o_d.rearrange("(g s p) (h t) -> g h p s t", s=2, p=P, h=2)

        with nc.Block() as block:
            @block.sync
            def _(e):
                def load(g, j):
                    for dst, name in ((qx[0], "fqh"), (qx[1], "fql")):
                        for h in range(F):
                            e.dma_start(dst[h * HD:(h + 1) * HD, j, h].bitcast(fp32),
                                        rows[name][g, h * HD:(h + 1) * HD]).then_inc(loaded[j], 16)
                    e.dma_start(kk[0][:, j].bitcast(fp32), rows["fkh"][g]).then_inc(loaded[j], 16)
                    e.dma_start(kk[1][:, j].bitcast(fp32), rows["fkl"][g]).then_inc(loaded[j], 16)
                    e.dma_start(fq[:, j], rows["fq"][g]).then_inc(loaded[j], 16)
                    e.dma_start(kt[:, j], kt_rows[g]).then_inc(loaded[j], 16)
                    e.dma_start(vs[:, j], v_rows[g]).then_inc(loaded[j], 16)

                def outputs(g):
                    for h in range(2):
                        e.wait_ge(ot_ready, h + 1)
                        e.sem_inc(o_free, 1)
                        e.dma_start(o_rows[g, h], ot[:]).then_inc(ot_stored, 16)
                    take(e, (ot_ready, 2))

                e.wait_ge(zeroed, 4)
                for j in range(NBUF):
                    load(j, j)
                with e.Fori(0, G // NBUF - 1) as i:
                    for j in range(NBUF):
                        outputs(NBUF * i + j)
                        load(NBUF * i + j + NBUF, j)
                outputs(G - 2)
                outputs(G - 1)

            @block.gpsimd
            def _(e):
                step = Chain(e, pool_chain)
                step(e.memset(tri[:], 1.0))
                step(e.affine_select(out=tri[:], in_=tri[:], compare_op=ALU.is_ge, fill=0.0, base=0,
                                     pattern=[[1, P]], channel_multiplier=-1))
                step(e.memset(own[:], 1.0))
                step(e.affine_select(out=own[:], in_=own[:], compare_op=ALU.is_ge, fill=0.0, base=0,
                                     pattern=[[-HD, F]], channel_multiplier=1))
                step(e.affine_select(out=own[:], in_=own[:], compare_op=ALU.is_ge, fill=0.0, base=HD - 1,
                                     pattern=[[HD, F]], channel_multiplier=-1))
                e.sem_inc(masks_ready, 1)
                for j in range(NBUF):
                    step(e.memset(qx[1][:, j].bitcast(fp32), 0.0))
                    e.sem_inc(zeroed, 1)

            @block.vector
            def _(e):
                step = Chain(e, dve_chain)
                for j in range(NBUF):
                    step(e.memset(qx[0][:, j].bitcast(fp32), 0.0))
                    e.sem_inc(zeroed, 1)
                e.wait_ge(masks_ready, 1)
                step.close()
                with e.Fori(0, G):
                    step(e.memset(state[:], 0.0))
                    e.sem_inc(state_ready, 1)
                    for c in range(KB):
                        e.wait_ge(a_ready, c + 1)
                        src = scores[c % 2][:].rearrange("p a h q -> p (a h) q")
                        e.tensor_tensor(am[:, c % 2], src, tri[:].unsqueeze(1).broadcast_to((P, F, P)), ALU.mult
                                        ).then_inc(am_ready, 1)
                        if c < KB - 1:
                            e.wait_ge(s_ready, c + 1)
                            e.tensor_tensor(state[:, :, 0:VW], s_ps[:], own[:].unsqueeze(2)
                                            .broadcast_to((P, F, VW)), ALU.mult).then_inc(state_ready, 1)
                    e.wait_ge(s_ready, KB)
                    take(e, (a_ready, KB), (s_ready, KB))
                    step.close()

            @block.scalar
            def _(e):
                e.sem_inc(ot_stored, 16)
                with e.Fori(0, 2 * G):
                    e.wait_ge(o_ready, 1)
                    e.wait_ge(ot_stored, 16)
                    e.activation(ot[:], o_ps[:], ACT.Copy).then_inc(ot_ready, 1)
                    take(e, (o_ready, 1), (ot_stored, 16))
                e.wait_ge(ot_stored, 16)

            @block.tensor
            def _(e):
                def chunk_scores(j, c):
                    cols = slice(c * P, (c + 1) * P)
                    for s in range(2):
                        heads = slice(4 * s, 4 * s + 4)
                        i = product(e, scores[c % 2][:, s],
                                    (lambda _: kk[0][:, j, cols], lambda _: kk[1][:, j, cols]),
                                    (lambda _: qx[0][:, j, heads, cols], lambda _: qx[1][:, j, heads, cols]), 1)
                    i.then_inc(a_ready, 1)

                def chunk_outputs(j, c):
                    cols = slice(c * P, (c + 1) * P)
                    oc = slice((c % TPB) * P, (c % TPB + 1) * P)
                    if c % TPB == 0:
                        e.wait_ge(o_free, 1)
                        take(e, (o_free, 1))
                    e.wait_ge(state_ready, c + 1)
                    for s in range(2):
                        e.matmul(o_ps[:, s, oc], state[:, 4 * s:4 * s + 4].rearrange("p h d -> p (h d)"),
                                 fq[:, j, cols], start=True, stop=False, skip_group_check=True)
                    e.matmul(s_ps[:].rearrange("p h d -> p (h d)"), kt[:, j, c], vs[:, j, c], start=c == 0,
                             stop=True, skip_group_check=True).then_inc(s_ready, 1)
                    e.wait_ge(am_ready, c + 1)
                    for s in range(2):
                        for h in range(4):
                            i = e.matmul(o_ps[32 * h:32 * h + VW, s, oc],
                                         vs[:, j, c, (4 * s + h) * VW:(4 * s + h + 1) * VW],
                                         am[:, c % 2, 4 * s + h], start=False, stop=True, skip_group_check=True)
                    if c % TPB == TPB - 1:
                        i.then_inc(o_ready, 1)

                e.sem_inc(o_free, 1)
                with e.Fori(0, G // NBUF):
                    for j in range(NBUF):
                        e.wait_ge(loaded[j], LOADS)
                        chunk_scores(j, 0)
                        for c in range(KB):
                            if c < KB - 1:
                                chunk_scores(j, c + 1)
                            chunk_outputs(j, c)
                        take(e, (loaded[j], LOADS), (am_ready, KB), (state_ready, KB))


def phase_gated_ffn(nc, xh_d, xl_d, x3_d, wt_d, weights, out_d):
    NCH = E1 + SF1 // P
    gw_d, sgw_d, uw_d, suw_d, dw_d, sdw_d = weights
    with Phase(nc, "ffn") as ph:
        raw = [ph.sb(f"raw{n}", [P, KC, NCH * P]) for n in ("g", "u", "d")]
        wh = [ph.sb(f"wh{n}", [P, KC, NCH * P], f32r) for n in ("g", "u", "d")]
        wl = [ph.sb(f"wl{n}", [P, KC, NCH * P], f32r) for n in ("g", "u", "d")]
        mhalf = ph.sb("mhalf", [P, TPB])
        xh = ph.sb("xh", [P, 2, KC, BLK], f32r)
        xl = ph.sb("xl", [P, 2, KC, BLK], f32r)
        wt = ph.sb("wt", [P, 2, E1, BLK])
        x3 = ph.sb("x3", [P, 2, TPB, C])
        gate = ph.sb("gate", [P, 2, BLK])
        hid = ph.sb("hid", [P, 2, BLK])
        hh = ph.sb("hh", [P, 3, BLK], f32r)
        hl = ph.sb("hl", [P, 3, BLK], f32r)
        st = ph.sb("st", [P, TPB, 6])
        mv = ph.sb("mv", [P, TPB, 2])
        ve = ph.sb("ve", [P, TPB])
        rs = ph.sb("rs", [P, TPB])
        nmr = ph.sb("nmr", [P, TPB])
        yn = ph.sb("yn", [P, 2, TPB, C])
        g_ps = ph.ps("g_ps", [P, 2, BLK])
        u_ps = ph.ps("u_ps", [P, 2, BLK])
        y_ps = ph.ps("y_ps", [P, 2, TPB, C])

        raw_loaded = [ph.sem(f"raw_loaded{n}") for n in range(3)]
        high_ready = ph.sem("high_ready")
        low_ready = ph.sem("low_ready")
        dve_chain = ph.sem("dve_chain")
        pow_ready = ph.sem("pow_ready")
        x_loaded = [ph.sem(f"x_loaded{j}") for j in range(2)]
        w_loaded = [ph.sem(f"w_loaded{j}") for j in range(2)]
        g_ready = ph.sem("g_ready")
        u_ready = ph.sem("u_ready")
        gate_ready = ph.sem("gate_ready")
        hid_ready = ph.sem("hid_ready")
        hh_ready = ph.sem("hh_ready")
        hl_ready = ph.sem("hl_ready")
        gu_free = ph.sem("gu_free")
        y_ready = ph.sem("y_ready")
        var_ready = ph.sem("var_ready")
        rstd_ready = ph.sem("rstd_ready")
        scale_ready = ph.sem("scale_ready")
        yn_ready = ph.sem("yn_ready")
        out_ready = ph.sem("out_ready")
        stored = [ph.sem(f"stored{j}") for j in range(2)]

        def tiles(d):
            return d.rearrange("(b j t p) c -> b j p t c", j=2, t=TPB, p=P)

        def turned(d):
            return d.rearrange("(b c p) (j t) -> b j p c t", b=B, p=P, j=2)

        wt_rows = wt_d.rearrange("e (b j t) -> b j e t", b=B, j=2)

        def down(a):
            return a[:].rearrange("p k (c f) -> p (k c f)", f=P).rearrange("p (c h) -> p c h", h=C)

        with nc.Block() as block:
            @block.sync
            def _(e):
                def load(b, j):
                    e.dma_start(xh[:, j].bitcast(fp32), turned(xh_d)[b, j]).then_inc(x_loaded[j], 16)
                    e.dma_start(xl[:, j].bitcast(fp32), turned(xl_d)[b, j]).then_inc(x_loaded[j], 16)
                    e.dma_start(wt[:, j], wt_rows[b, j].unsqueeze(0).broadcast_to((P, E1, BLK))
                                ).then_inc(w_loaded[j], 16)
                    e.dma_start(x3[:, j], tiles(x3_d)[b, j]).then_inc(w_loaded[j], 16)

                def store(b, j):
                    e.wait_ge(out_ready, 1)
                    e.dma_start(tiles(out_d)[b, j], yn[:, j]).then_inc(stored[j], 16)
                    take(e, (out_ready, 1))

                for n, (routed, shared) in enumerate(((gw_d, sgw_d), (uw_d, suw_d))):
                    e.dma_start(raw[n][:, :, 0:E1 * P], routed).then_inc(raw_loaded[n], 16)
                    e.dma_start(raw[n][:, :, E1 * P:], shared).then_inc(raw_loaded[n], 16)
                e.dma_start(down(raw[2])[:, 0:E1], dw_d).then_inc(raw_loaded[2], 16)
                e.dma_start(down(raw[2])[:, E1:], sdw_d).then_inc(raw_loaded[2], 16)
                for j in range(2):
                    load(0, j)
                with e.Fori(0, B - 1) as b:
                    for j in range(2):
                        store(b, j)
                        load(b + 1, j)
                for j in range(2):
                    store(B - 1, j)

            @block.gpsimd
            def _(e):
                e.memset(mhalf[:], -0.5).then_inc(pow_ready, 1)
                e.wait_ge(pow_ready, 1)
                with e.Fori(0, 2 * B):
                    e.wait_ge(var_ready, 1)
                    e.tensor_tensor(rs[:], ve[:], mhalf[:], ALU.pow).then_inc(rstd_ready, 1)
                    take(e, (var_ready, 1))

            @block.vector
            def _(e):
                step = Chain(e, dve_chain)
                for n in range(3):
                    e.wait_ge(high_ready, n + 1)
                    step(e.tensor_tensor(wl[n][:], raw[n][:], wh[n][:].bitcast(fp32), ALU.subtract))
                    e.sem_inc(low_ready, 1)
                step.close()

                def result(j, part):
                    if part == 0:
                        e.wait_ge(y_ready, 1)
                        variance(e, step, y_ps[:, j], st, mv, ve, var_ready)
                        take(e, (y_ready, 1))
                    elif part == 1:
                        scaling(e, mv, rs, nmr, rstd_ready, scale_ready)
                    else:
                        e.wait_ge(yn_ready, 1)
                        e.tensor_tensor(yn[:, j], yn[:, j], x3[:, j], ALU.add).then_inc(out_ready, 1)
                        take(e, (yn_ready, 1))

                def hidden(j, prev):
                    e.wait_ge(w_loaded[j], 32)
                    for c in range(NCH):
                        e.wait_ge(gate_ready, c + 1)
                        e.wait_ge(u_ready, c + 1)
                        product_ = e.tensor_tensor(hid[:, c % 2], gate[:, c % 2], u_ps[:, c % 2], ALU.mult)
                        if c < E1:
                            step(product_)
                            e.sem_inc(gu_free, 1)
                            e.tensor_tensor(hid[:, c % 2], hid[:, c % 2], wt[:, j, c], ALU.mult).then_inc(hid_ready, 1)
                        else:
                            product_.then_inc(hid_ready, 1)
                        e.wait_ge(hh_ready, c + 1)
                        if c >= E1:
                            e.sem_inc(gu_free, 1)
                        e.tensor_tensor(hl[:, c % 3], hid[:, c % 2], hh[:, c % 3].bitcast(fp32), ALU.subtract
                                        ).then_inc(hl_ready, 1)
                        if prev and c in (2, 3, 6):
                            result(1 - j, (2, 3, 6).index(c))
                    take(e, (w_loaded[j], 32), (gate_ready, NCH), (u_ready, NCH), (hh_ready, NCH))
                    step.close()

                hidden(0, False)
                hidden(1, True)
                with e.Fori(1, B):
                    for j in range(2):
                        hidden(j, True)
                for part in range(3):
                    result(1, part)
                step.close()

            @block.scalar
            def _(e):
                for n in range(3):
                    e.wait_ge(raw_loaded[n], 32)
                    e.activation(wh[n][:], raw[n][:], ACT.Copy).then_inc(high_ready, 1)
                for j in range(2):
                    e.sem_inc(stored[j], 16)

                def normalise(j):
                    e.wait_ge(stored[j], 16)
                    e.wait_ge(scale_ready, 1)
                    for t in range(TPB):
                        i = e.activation(yn[:, j, t], y_ps[:, j, t], ACT.Identity, bias=nmr[:, t:t + 1],
                                         scale=rs[:, t:t + 1])
                    i.then_inc(yn_ready, 1)
                    take(e, (stored[j], 16), (scale_ready, 1))

                def hidden(j, prev):
                    for c in range(NCH):
                        e.wait_ge(g_ready, c + 1)
                        e.activation(gate[:, c % 2], g_ps[:, c % 2], ACT.Silu).then_inc(gate_ready, 1)
                        e.wait_ge(hid_ready, c + 1)
                        e.activation(hh[:, c % 3], hid[:, c % 2], ACT.Copy).then_inc(hh_ready, 1)
                        if prev and c == 4:
                            normalise(1 - j)
                    take(e, (g_ready, NCH), (hid_ready, NCH))

                hidden(0, False)
                hidden(1, True)
                with e.Fori(1, B):
                    for j in range(2):
                        hidden(j, True)
                normalise(1)
                for j in range(2):
                    e.wait_ge(stored[j], 16)

            @block.tensor
            def _(e):
                def gate_up(j, c):
                    e.wait_ge(gu_free, c + 1)
                    cols = slice(c * P, (c + 1) * P)
                    for ps, n, ready in ((g_ps, 0, g_ready), (u_ps, 1, u_ready)):
                        product(e, ps[:, c % 2], (lambda k: wh[n][:, k, cols], lambda k: wl[n][:, k, cols]),
                                (lambda k: xh[:, j, k], lambda k: xl[:, j, k]), KC).then_inc(ready, 1)

                def down_product(j, c, wait):
                    e.wait_ge(hl_ready, wait)
                    for t in range(TPB):
                        cols = slice(t * P, (t + 1) * P)
                        i = product(e, y_ps[:, j, t], (lambda _: hh[:, c % 3, cols], lambda _: hl[:, c % 3, cols]),
                                    (lambda _: down(wh[2])[:, c], lambda _: down(wl[2])[:, c]), 1,
                                    first=c == 0 and t % 2 == 0, last=c == NCH - 1, skip_group_check=True)
                    return i

                def chunks(j, prev):
                    e.wait_ge(x_loaded[j], 32)
                    for c in range(NCH):
                        gate_up(j, c)
                        if c >= 2:
                            down_product(j, c - 2, c + 1)
                        elif prev:
                            i = down_product(1 - j, NCH - 2 + c, c + 1)
                            if c == 1:
                                i.then_inc(y_ready, 1)
                    take(e, (x_loaded[j], 32), (gu_free, NCH), (hl_ready, NCH))

                e.wait_ge(low_ready, 3)
                e.sem_inc(gu_free, 2)
                e.sem_inc(hl_ready, 2)
                chunks(0, False)
                chunks(1, True)
                with e.Fori(1, B):
                    for j in range(2):
                        chunks(j, True)
                down_product(1, NCH - 2, 1)
                down_product(1, NCH - 1, 2).then_inc(y_ready, 1)


def build(nc, x, w_attn, w_proj, router0, bias0, w1, w2, sw1, sw2, w_qkv, bqk, bv, w_out, b_out, router1, bias1,
          gate, up, down, s_gate, s_up, s_down, out):
    def dram(name, *shape):
        return nc.dram_tensor(name, shape, fp32, kind="Internal").ap()

    features = (B * C, T)
    heads = (B * NG * P, T)
    qh, ql, kh, kl = (dram(n, *features) for n in ("q_high", "q_low", "k_high", "k_low"))
    v = dram("values", B * NG * T, GH * VW)
    o = dram("attended", *heads)
    x1 = dram("x1", N, C)
    x1h, x1l = dram("x1_high", *features), dram("x1_low", *features)
    rows = dram("expert_rows", N + DUMMY, XW)
    chosen = dram("chosen", E0, N)
    acc0, acc1 = dram("acc0", N + DUMMY, C), dram("acc1", N + DUMMY, C)
    x2 = dram("x2", N, C)
    fq = dram("phi_q", *features)
    fqh, fql, fkh, fkl = (dram(n, *features) for n in ("phi_q_high", "phi_q_low", "phi_k_high", "phi_k_low"))
    fkt = dram("phi_k_rows", 2 * N, P)
    v1 = dram("values1", 2 * N, P + 8)
    o1 = dram("attended1", *heads)
    x3 = dram("x3", N, C)
    x3h, x3l = dram("x3_high", *features), dram("x3_low", *features)
    weights = dram("weights", E1, N)

    phase_qkv(nc, x, w_attn, qh, ql, kh, kl, v)
    phase_softmax_attention(nc, qh, ql, kh, kl, v, o)
    phase_project_route(nc, 0, o, x, w_proj, router0, bias0, None, x1, x1h, x1l, rows, chosen)
    with nc.sbuf_tensor("slots", [CAP, E0], i32) as slots:
        phase_shared_and_slots(nc, x1h, x1l, sw1, sw2, chosen, acc0, acc1, rows, slots)
        phase_experts(nc, slots, rows, w1, w2, acc0, acc1)
    phase_linear_qkv(nc, x1, acc0, acc1, w_qkv, bqk, bv, x2, fq, fqh, fql, fkh, fkl, fkt, v1)
    phase_linear_attention(nc, fq, fqh, fql, fkh, fkl, fkt, v1, o1)
    phase_project_route(nc, 1, o1, x2, w_out, router1, bias1, b_out, x3, x3h, x3l, None, weights)
    phase_gated_ffn(nc, x3h, x3l, x3, weights, (gate, s_gate, up, s_up, down, s_down), out)


def kernel(**inputs):
    import numpy as np
    import concourse.bacc as bacc
    from concourse.bass_utils import run_bass_kernel_spmd

    def chunked(w):
        return w.reshape(-1, P, w.shape[-1]).transpose(1, 0, 2)

    def gated(w):
        return w.reshape(E1, KC, P, F1).transpose(2, 1, 0, 3).reshape(P, KC, E1 * F1)

    get = {n: np.asarray(a) for n, a in inputs.items()}
    laid = {
        "x": get["L0_attn_x"].reshape(N, C),
        "w_attn": chunked(get["L0_attn_w_attn"]),
        "w_proj": chunked(get["L0_attn_w_proj"]),
        "router0": chunked(get["L0_ffn_router_weight"].T),
        "bias0": get["L0_ffn_expert_bias"],
        "w1": get["L0_ffn_w1"],
        "w2": get["L0_ffn_w2"],
        "sw1": chunked(get["L0_ffn_sw1"].T),
        "sw2": chunked(get["L0_ffn_sw2"].T),
        "w_qkv": chunked(get["L1_attn_W_qkv"]),
        "bqk": get["L1_attn_b_qkv"][:2 * C].reshape(4, P).T,
        "bv": get["L1_attn_b_qkv"][2 * C:],
        "w_out": chunked(get["L1_attn_W_out"]),
        "b_out": get["L1_attn_b_out"],
        "router1": chunked(get["L1_ffn_router_w"]),
        "bias1": get["L1_ffn_router_bias"].reshape(1),
        "gate": gated(get["L1_ffn_gate_w"]),
        "up": gated(get["L1_ffn_up_w"]),
        "down": get["L1_ffn_down_w"].transpose(1, 0, 2),
        "s_gate": chunked(get["L1_ffn_s_gate_w"]),
        "s_up": chunked(get["L1_ffn_s_up_w"]),
        "s_down": chunked(get["L1_ffn_s_down_w"]),
    }
    laid = {n: np.ascontiguousarray(a) for n, a in laid.items()}
    nc = bacc.Bacc("TRN2", target_bir_lowering=False, num_devices=1)
    args = {n: nc.dram_tensor(n, a.shape, mybir.dt.from_np(a.dtype), kind="ExternalInput").ap()
            for n, a in laid.items()}
    out = nc.dram_tensor("out", (N, C), fp32, kind="ExternalOutput").ap()
    build(nc, *args.values(), out)
    r = run_bass_kernel_spmd(nc, [laid], core_ids=[0])
    return r.results[0]["out"].reshape(B, T, C)
```

```python
import concourse.bass as bass
from concourse import mybir
from contextlib import ExitStack

fp32 = mybir.dt.float32
f32r = mybir.dt.float32r
bf16 = mybir.dt.bfloat16
i32 = mybir.dt.int32
ALU = mybir.AluOpType
ACT = mybir.ActivationFunctionType
AX = mybir.AxisListType

B, T, C = 8, 1024, 256
N = B * T
NH, HD = 16, 16
P = 128
KC = C // P
BLK = 512
TPB = BLK // P
GH = 4
NG = NH // GH
VW = HD + 1
KB = T // P
E0, K0, F0, SF0 = 64, 6, 128, 512
CAP = 2 * ((512 * K0 + E0 - 1) // E0)
E1, K1, F1, SF1 = 8, 4, 128, 512
XW = C + E0
EPS = 1e-5



def take(eng, *pairs):
    for sem, n in pairs:
        eng.sem_inc(sem, -n)


class Phase:

    def __init__(self, nc, name):
        self.nc, self.name, self.ctx, self.sems = nc, name, ExitStack(), []

    def sb(self, name, shape, dt=fp32):
        return self.ctx.enter_context(self.nc.sbuf_tensor(f"{self.name}_{name}", shape, dt))

    def ps(self, name, shape, dt=fp32):
        return self.ctx.enter_context(self.nc.psum_tensor(f"{self.name}_{name}", shape, dt))

    def sem(self, name):
        self.sems.append(self.nc.alloc_semaphore(f"{self.name}_{name}"))
        return self.sems[-1]

    def __enter__(self):
        return self

    def __exit__(self, *a):
        self.nc.clear_and_free_semaphores(self.sems)
        self.nc.all_engine_barrier()
        return self.ctx.__exit__(*a)


def pipeline(e, stages, depth, peeled=0):
    start, last = depth // 2, 2 * B - 1

    def blocks(n):
        return [((n - s) // 2, (n - s) % 2) if 0 <= n - s <= last else None for s in range(depth)]

    for n in range(2 * start):
        stages(*blocks(n))
    with e.Fori(start, B - peeled) as i:
        for half in range(2):
            stages(*((i - (s + 1 - half) // 2, (half - s) % 2) for s in range(depth)))
    for n in range(2 * (B - peeled), last + depth):
        stages(*blocks(n))


def final(block):
    return isinstance(block[0], int) and block[0] == B - 1


def phase_qkv(nc, x_d, w_d, qh_d, ql_d, kh_d, kl_d, v_d):
    with Phase(nc, "qkv") as ph:
        wf = ph.sb("wf", [P, KC, 3 * C])
        wh = ph.sb("wh", [P, KC, 3 * C], f32r)
        wl = ph.sb("wl", [P, KC, 3 * C], f32r)
        ident = ph.sb("ident", [P, P])
        mhalf = ph.sb("mhalf", [P, TPB])
        x = ph.sb("x", [P, 2, TPB, C])
        st = ph.sb("st", [P, TPB, 6])
        mv = ph.sb("mv", [P, TPB, 2])
        ve = ph.sb("ve", [P, TPB])
        rs = ph.sb("rs", [P, TPB])
        xn = ph.sb("xn", [P, TPB, C])
        xh = ph.sb("xh", [P, 2, KC, BLK], f32r)
        xl = ph.sb("xl", [P, 2, KC, BLK], f32r)
        oh = ph.sb("oh", [P, 2, 4, BLK], f32r)
        ol = ph.sb("ol", [P, 2, 4, BLK], f32r)
        vo = ph.sb("vo", [P, 2, TPB, NH, VW])
        t_ps = ph.ps("t_ps", [P, KC, BLK])
        qk = ph.ps("qk", [P, 4, BLK])
        vp = ph.ps("vp", [P, TPB, C])

        w_loaded = ph.sem("w_loaded")
        pe_consts = ph.sem("pe_consts")
        ones_ready = ph.sem("ones_ready")
        pool_chain = ph.sem("pool_chain")
        dve_chain = ph.sem("dve_chain")
        x_loaded = [ph.sem(f"x_loaded{j}") for j in range(2)]
        x_free = ph.sem("x_free")
        var_ready = ph.sem("var_ready")
        rstd_ready = ph.sem("rstd_ready")
        xn_ready = ph.sem("xn_ready")
        xn_turned = ph.sem("xn_turned")
        xh_ready = ph.sem("xh_ready")
        xl_ready = ph.sem("xl_ready")
        qk_ready = ph.sem("qk_ready")
        oh_ready = ph.sem("oh_ready")
        ol_ready = ph.sem("ol_ready")
        v_ready = ph.sem("v_ready")
        vo_ready = ph.sem("vo_ready")
        qk_read = ph.sem("qk_read")
        v_read = ph.sem("v_read")
        stored = [ph.sem(f"stored{j}") for j in range(2)]
        STORES = 16 * (4 + TPB)

        x_v = x_d.rearrange("(b j t p) c -> b j p t c", j=2, t=TPB, p=P)
        v_v = v_d.rearrange("(b g j t p) c -> b j t p g c", b=B, g=NG, j=2, t=TPB, p=P)

        def rows(d):
            return d.rearrange("(b c p) (j t) -> b j p c t", b=B, p=P, j=2)

        with nc.Block() as block:
            @block.sync
            def _(e):
                def load(b, j):
                    e.dma_start(x[:, j], x_v[b, j]).then_inc(x_loaded[j], 16)

                def stages(a, b):
                    if a is not None and not final(a):
                        e.wait_ge(x_free, 1)
                        load(a[0] + 1, a[1])
                        take(e, (x_free, 1))
                    if b is not None:
                        j = b[1]
                        e.wait_ge(ol_ready, 4)
                        for d, s, c in ((qh_d, oh, 0), (kh_d, oh, 2), (ql_d, ol, 0), (kl_d, ol, 2)):
                            e.dma_start(rows(d)[b[0], j], s[:, j, c:c + 2].bitcast(fp32)).then_inc(stored[j], 16)
                        e.sem_inc(qk_read, 1)
                        e.wait_ge(vo_ready, 1)
                        e.sem_inc(v_read, 1)
                        for t in range(TPB):
                            e.dma_start(v_v[b[0], j, t], vo[:, j, t].rearrange("p (g h) d -> p g (h d)", g=NG)
                                        ).then_inc(stored[j], 16)
                        take(e, (ol_ready, 4), (vo_ready, 1))

                e.dma_start(wf[:], w_d).then_inc(w_loaded, 16)
                for j in range(2):
                    load(0, j)
                pipeline(e, stages, 2, peeled=1)

            @block.gpsimd
            def _(e):
                step = Chain(e, pool_chain)
                identity(e, step, ident)
                step(e.memset(mhalf[:], -0.5))
                e.sem_inc(pe_consts, 1)
                step(e.memset(vo[:].rearrange("p j t h d -> p (j t h) d")[:, :, HD:VW], 1.0))
                e.sem_inc(ones_ready, 1)
                step.close()
                with e.Fori(0, 2 * B):
                    e.wait_ge(var_ready, 1)
                    e.tensor_tensor(rs[:], ve[:], mhalf[:], ALU.pow).then_inc(rstd_ready, 1)
                    take(e, (var_ready, 1))

            @block.vector
            def _(e):
                step = Chain(e, dve_chain)
                e.wait_ge(w_loaded, 16)
                step(e.tensor_scalar(wf[:, :, 0:C], wf[:, :, 0:C], HD ** -0.5, None, ALU.mult))
                split_weights(e, step, wf, wh, wl)
                e.sem_inc(pe_consts, 1)
                step.close()

                def stages(a, b):
                    if a is not None:
                        j = a[1]
                        e.wait_ge(x_loaded[j], 16)
                        variance(e, step, x[:, j], st, mv, ve, var_ready)
                        e.wait_ge(rstd_ready, 1)
                        for t in range(TPB):
                            e.tensor_scalar(xn[:, t], x[:, j, t], mv[:, t, 0:1], rs[:, t:t + 1],
                                            ALU.subtract, ALU.mult).then_inc(xn_ready, 1)
                        take(e, (x_loaded[j], 16), (rstd_ready, 1))
                    if b is not None:
                        j = b[1]
                        for c in range(4):
                            e.wait_ge(oh_ready, c + 1)
                            e.tensor_tensor(ol[:, j, c], qk[:, c], oh[:, j, c].bitcast(fp32),
                                            ALU.subtract).then_inc(ol_ready, 1)
                        take(e, (oh_ready, 4))
                    if a is not None:
                        e.wait_ge(xh_ready, 1)
                        if not final(a):
                            e.sem_inc(x_free, 1)
                        e.tensor_tensor(xl[:, a[1]], t_ps[:], xh[:, a[1]].bitcast(fp32), ALU.subtract
                                        ).then_inc(xl_ready, 1)
                        take(e, (xh_ready, 1))
                    step.close()

                pipeline(e, stages, 2, peeled=1)

            @block.scalar
            def _(e):
                for j in range(2):
                    e.sem_inc(stored[j], STORES)
                e.wait_ge(ones_ready, 1)

                def stages(a, b):
                    if b is not None:
                        j = b[1]
                        e.wait_ge(stored[j], STORES)
                        for c in range(4):
                            e.wait_ge(qk_ready, c + 1)
                            e.activation(oh[:, j, c], qk[:, c], ACT.Copy).then_inc(oh_ready, 1)
                    if a is not None:
                        e.wait_ge(xn_turned, 1)
                        e.activation(xh[:, a[1]], t_ps[:], ACT.Copy).then_inc(xh_ready, 1)
                        take(e, (xn_turned, 1))
                    if b is not None:
                        e.wait_ge(v_ready, 1)
                        e.activation(vo[:, j, :, :, 0:HD], vp[:].rearrange("p t (h d) -> p t h d", d=HD), ACT.Copy
                                     ).then_inc(vo_ready, 1)
                        take(e, (stored[j], STORES), (qk_ready, 4), (v_ready, 1))

                pipeline(e, stages, 2)
                for j in range(2):
                    e.wait_ge(stored[j], STORES)

            @block.tensor
            def _(e):
                e.sem_inc(qk_read, 1)
                e.sem_inc(v_read, 1)
                e.wait_ge(pe_consts, 2)

                def stages(a, b):
                    if b is not None:
                        j = b[1]
                        e.wait_ge(xl_ready, 1)
                        e.wait_ge(qk_read, 1)
                        for c in range(4):
                            cols = slice(c * P, (c + 1) * P)
                            product(e, qk[:, c], (lambda k: wh[:, k, cols], lambda k: wl[:, k, cols]),
                                    (lambda k: xh[:, j, k], lambda k: xl[:, j, k]), KC).then_inc(qk_ready, 1)
                        take(e, (xl_ready, 1), (qk_read, 1))
                    if a is not None:
                        for t in range(TPB):
                            e.wait_ge(xn_ready, t + 1)
                            for k in range(KC):
                                i = e.transpose(t_ps[:, k, t * P:(t + 1) * P], xn[:, t, k * P:(k + 1) * P], ident[:])
                        i.then_inc(xn_turned, 1)
                        take(e, (xn_ready, TPB))
                    if b is not None:
                        e.wait_ge(v_read, 1)
                        for t in range(TPB):
                            cols = slice(t * P, (t + 1) * P)
                            i = product(e, vp[:, t], (lambda k: xh[:, j, k, cols], lambda k: xl[:, j, k, cols]),
                                        (lambda k: wh[:, k, 2 * C:3 * C], lambda k: wl[:, k, 2 * C:3 * C]), KC)
                        i.then_inc(v_ready, 1)
                        take(e, (v_read, 1))

                pipeline(e, stages, 2)


def phase_softmax_attention(nc, qh_d, ql_d, kh_d, kl_d, v_d, o_d):
    G = B * NG
    NBUF = 3
    NPR = 4
    MBUF = 3
    SR = 4 * HD
    with Phase(nc, "att") as ph:
        qs = ph.sb("qs", [P, NBUF, GH, T], f32r)
        ks = ph.sb("ks", [P, NBUF, GH, T], f32r)
        vs = ph.sb("vs", [P, NBUF, KB, GH * VW])
        pr = ph.sb("pr", [P, NPR, GH, BLK])
        ot = ph.sb("ot", [P, 2, BLK])
        zero = ph.sb("zero", [32, P])
        identf = ph.sb("identf", [P, P])
        identb = ph.sb("identb", [P, P], bf16)
        causal = ph.sb("causal", [P, P], bf16)
        mx = ph.sb("mx", [P, 2, GH, KB])
        mxs = ph.sb("mxs", [P, GH, KB])
        nmt = ph.sb("nmt", [32, P], f32r)
        e_ps = ph.ps("e_ps", [P, 2, 2, BLK])
        m_ps = ph.ps("m_ps", [P, MBUF, BLK])
        o_ps = ph.ps("o_ps", [P, BLK])

        consts = ph.sem("consts")
        consts_pe = ph.sem("consts_pe")
        later_stacks = ph.sem("later_stacks")
        first_here = ph.sem("first_here")
        const_chain = ph.sem("const_chain")
        stack_loaded = [ph.sem(f"stack_loaded{j}") for j in range(NBUF)]
        m_scores = ph.sem("m_scores")
        m_free = ph.sem("m_free")
        pieces_done = ph.sem("pieces_done")
        max_ready = ph.sem("max_ready")
        maxt_ready = ph.sem("maxt_ready")
        nmt_ready = ph.sem("nmt_ready")
        mrow_loaded = ph.sem("mrow_loaded")
        e_scores = ph.sem("e_scores")
        exp_done = ph.sem("exp_done")
        mask_due = ph.sem("mask_due")
        masked = ph.sem("masked")
        pv_done = ph.sem("pv_done")
        ot_ready = ph.sem("ot_ready")
        o_free = ph.sem("o_free")
        ot_stored = [ph.sem(f"ot_stored{j}") for j in range(2)]
        LOADS = 16 * 10
        LOOPS = (G - 4) // NBUF

        steps = [(h, k, p) for h in range(2) for k in range(4 * h + 4) for p in range(2)]
        pieces = []
        for q in range(KB):
            for h in range(q // 4 + 1):
                per = max(1, min(GH, BLK // (min(BLK, (q + 1) * P - h * BLK))))
                if (q, h) == (1, 0):
                    pieces += [(q, h, (0, 1)), (q, h, (2,)), (q, h, (3,))]
                else:
                    pieces += [(q, h, tuple(range(n, n + per))) for n in range(0, GH, per)]
        NPC, MEND, MAXIMA = len(pieces), 19, 20
        assert NPC % MBUF == 0

        def width(h, k):
            return BLK - max(0, k * P - h * BLK)

        def keys(q, h):
            return min(BLK, (q + 1) * P - h * BLK)

        def diagonal(s):
            h, k, p = steps[s]
            return k * P >= h * BLK

        def shares():
            order = list(range(MEND, len(steps))) + list(range(MEND))
            load = [keys(q, h) * len(heads) + 96 for q, h, heads in pieces]
            work = [width(*steps[s][:2]) + 160 for s in order]
            out, n, done, due = {}, 0, 0.0, 0.0
            for s, w in zip(order, work):
                due += w * sum(load) / sum(work)
                out[s] = []
                while n < NPC and done + load[n] / 2 <= due:
                    done += load[n]
                    out[s].append(n)
                    n += 1
            return out

        share = shares()
        NDIAG = sum(diagonal(s) for s in range(len(steps)))
        UNITS = len(steps) // 2
        LAG = 2

        def masks_before(u):
            return sum(diagonal(2 * (v % UNITS)) for v in range(-LAG, u + 1)) * 2

        src_rows = {n: d.rearrange("(g h d) t -> g d h t", h=GH, d=HD)
                    for n, d in (("qh", qh_d), ("ql", ql_d), ("kh", kh_d), ("kl", kl_d))}
        v_rows = v_d.rearrange("(g k p) c -> g p k c", k=KB, p=P)
        o_rows = o_d.rearrange("(g p) (h t) -> g h p t", p=P, h=2)

        with nc.Block() as block:
            @block.sync
            def _(e):
                def maxima_row(j):
                    return qs[SR:SR + 1, j].bitcast(fp32).rearrange("o h (k p) -> o (h k) p", p=P)

                def load(g, j):
                    for name, dst, parts in (("qh", qs, (0, 1)), ("ql", qs, (2, 3)),
                                             ("kh", ks, (0, 2)), ("kl", ks, (1, 3))):
                        for r in parts:
                            e.dma_start(dst[r * HD:(r + 1) * HD, j].bitcast(fp32), src_rows[name][g]
                                        ).then_inc(stack_loaded[j], 16)
                    e.dma_start(vs[:, j], v_rows[g]).then_inc(stack_loaded[j], 16)
                    e.dma_start(maxima_row(j), zero[:]).then_inc(stack_loaded[j], 16)

                def row(j):
                    e.wait_ge(nmt_ready, 1)
                    e.dma_start(maxima_row(j), nmt[:].bitcast(fp32)).then_inc(mrow_loaded, 16)
                    take(e, (nmt_ready, 1))

                def outputs(g, h):
                    e.wait_ge(ot_ready, 1)
                    e.sem_inc(o_free, 1)
                    e.dma_start(o_rows[g, h], ot[:, h]).then_inc(ot_stored[h], 16)
                    take(e, (ot_ready, 1))

                def group(g, nxt, loads, more):
                    outputs(g - 1, 1)
                    if loads:
                        load(g + 2, (nxt + 1) % NBUF)
                    outputs(g, 0)
                    if more:
                        row(nxt)

                e.wait_ge(consts, 1)
                load(0, 0)
                e.wait_ge(consts, NBUF)
                e.wait_ge(first_here, 1)
                for j in range(1, NBUF):
                    load(j, j)
                row(0)
                outputs(0, 0)
                row(1)
                with e.Fori(0, LOOPS) as i:
                    for j in range(NBUF):
                        group(NBUF * i + j + 1, (j + 2) % NBUF, True, True)
                for g in range(NBUF * LOOPS + 1, G):
                    group(g, (g + 1) % NBUF, g + 2 < G, g + 1 < G)
                outputs(G - 1, 1)

            @block.gpsimd
            def _(e):
                step = Chain(e, const_chain)
                step(e.memset(zero[:], 0.0))
                step(e.memset(qs[SR:P, 0].bitcast(fp32), 0.0))
                e.sem_inc(consts, 1)
                step(e.memset(causal[:], 0.0))
                step(e.affine_select(out=causal[:], in_=causal[:], compare_op=ALU.is_ge, fill=-1e30, base=0,
                                     pattern=[[-1, P]], channel_multiplier=1))
                identity(e, step, identf)
                step(e.tensor_copy(identb[:], identf[:]))
                e.sem_inc(consts_pe, 1)
                for j in range(1, NBUF):
                    step(e.memset(qs[SR:P, j].bitcast(fp32), 0.0))
                    e.sem_inc(consts, 1)
                for j in range(1, NBUF):
                    step(e.memset(ks[SR:P, j].bitcast(fp32), 0.0))
                    step(e.memset(ks[SR:SR + 1, j].bitcast(fp32), 1.0))
                e.sem_inc(later_stacks, 1)
                step.close()
                with e.Fori(0, G):
                    for s, (h, k, p) in enumerate(steps):
                        if diagonal(s):
                            e.wait_ge(mask_due, sum(diagonal(r) for r in range(s + 1)))
                            blk = pr[:, (s // 2) % NPR, 2 * p:2 * p + 2, 0:P]
                            e.affine_select(out=blk, in_=blk, compare_op=ALU.is_ge, fill=0.0, base=0,
                                            pattern=[[0, 2], [1, P]], channel_multiplier=-1).then_inc(masked, 1)
                    take(e, (mask_due, NDIAG))

            @block.vector
            def _(e):
                e.memset(ks[SR:P, 0].bitcast(fp32), 0.0).then_inc(pieces_done, 1)
                e.wait_ge(pieces_done, 1)
                e.memset(ks[SR:SR + 1, 0].bitcast(fp32), 1.0).then_inc(consts_pe, 1)
                e.memset(o_ps[:], 0.0).then_inc(consts_pe, 1)
                e.memset(mx[:], -3e38).then_inc(pieces_done, 1)
                e.wait_ge(pieces_done, 2)
                take(e, (pieces_done, 2))
                with e.Fori(0, G):
                    for n, (q, h, heads) in enumerate(pieces):
                        w = keys(q, h)
                        e.wait_ge(m_scores, n + 1)
                        src = m_ps[:, n % MBUF, 0:len(heads) * w].rearrange("p (n w) -> p n w", w=w)
                        e.reduce_max(mx[:, h, heads[0]:heads[-1] + 1, q], src, AX.X).then_inc(m_free, 1)
                    e.drain().then_inc(pieces_done, 1)
                    e.wait_ge(pieces_done, 1)
                    e.tensor_tensor(mxs[:], mx[:, 0], mx[:, 1], ALU.max).then_inc(pieces_done, 1)
                    e.wait_ge(pieces_done, 2)
                    e.sem_inc(max_ready, 1)
                    take(e, (m_scores, NPC), (pieces_done, 2))

            @block.scalar
            def _(e):
                def maxima():
                    e.wait_ge(maxt_ready, 1)
                    e.activation(nmt[:], e_ps[0:32, 0, 1, BLK - P:BLK], ACT.Copy, scale=-1.0).then_inc(nmt_ready, 1)
                    take(e, (maxt_ready, 1))

                def outputs(h, products_done):
                    e.wait_ge(pv_done, products_done)
                    e.wait_ge(ot_stored[h], 16)
                    e.activation(ot[:, h], o_ps[:], ACT.Copy).then_inc(ot_ready, 1)
                    take(e, (ot_stored[h], 16))

                def group(first, more):
                    for s, (h, k, p) in enumerate(steps):
                        w, u = width(h, k), s // 2
                        if s == MAXIMA and more:
                            e.wait_ge(e_scores, s + 1)
                            maxima()
                        if p == 0:
                            e.wait_ge(pv_done, u + 1)
                        e.wait_ge(e_scores, s + 1)
                        e.activation(pr[:, u % NPR, 2 * p:2 * p + 2, 0:w], e_ps[:, s % 2, :, 0:w], ACT.Exp
                                     ).then_inc(exp_done, 1)
                        if s == 2 * LAG - 1 and not first:
                            outputs(1, NPR)
                        if s == 2 * (LAG + 3) + 1:
                            outputs(0, NPR + 4)
                    take(e, (pv_done, UNITS), (e_scores, len(steps)))

                for h in range(2):
                    e.sem_inc(ot_stored[h], 16)
                e.sem_inc(pv_done, NPR)
                maxima()
                group(True, True)
                with e.Fori(0, G - 2):
                    group(False, True)
                group(False, False)
                outputs(1, NPR)
                for h in range(2):
                    e.wait_ge(ot_stored[h], 16)

            @block.tensor
            def _(e):
                def piece(j, n):
                    q, h, heads = pieces[n]
                    w = keys(q, h)
                    e.wait_ge(m_free, n + 1)
                    out = m_ps[:, n % MBUF, 0:len(heads) * w].rearrange("p (n w) -> p n w", w=w)
                    for i, hd in enumerate(heads):
                        ins = e.matmul(out[:, i], qs[:, j, hd, q * P:(q + 1) * P], ks[:, j, hd, h * BLK:h * BLK + w],
                                       start=i == 0, stop=h != q // 4, skip_group_check=True)
                    if h == q // 4:
                        ins = e.matmul(out[:, :, w - P:w], identb[:],
                                       causal[:].unsqueeze(1).broadcast_to((P, len(heads), P)), start=False,
                                       stop=True, skip_group_check=True)
                    ins.then_inc(m_scores, 1)
                    if n == NPC - 1:
                        take(e, (m_free, NPC))

                def maxima():
                    e.wait_ge(max_ready, 1)
                    e.transpose(e_ps[0:32, 0, 1, BLK - P:BLK], mxs[:].rearrange("p h k -> p (h k)"), identf[:]
                                ).then_inc(maxt_ready, 1)
                    take(e, (max_ready, 1))

                def exponentials(s, first):
                    e.wait_ge(exp_done, s + 1)
                    if diagonal(s - 2) and not (first and s < 2):
                        e.sem_inc(mask_due, 1)

                def scores(j, s):
                    h, k, p = steps[s]
                    w = width(h, k)
                    for n in range(2):
                        hd = 2 * p + n
                        i = e.matmul(e_ps[:, s % 2, n, 0:w], ks[:, j, hd, k * P:(k + 1) * P],
                                     qs[:, j, hd, (h + 1) * BLK - w:(h + 1) * BLK], start=True, stop=True)
                    i.then_inc(e_scores, 1)

                def products(j, u):
                    if u < 0:
                        j = (j - 1) % NBUF
                    h, k, _ = steps[2 * (u % UNITS)]
                    w = width(h, k)
                    if diagonal(2 * (u % UNITS)):
                        e.wait_ge(masked, masks_before(u))
                    if k == 0:
                        e.wait_ge(o_free, 1)
                        take(e, (o_free, 1))
                    for hd in range(GH):
                        i = e.matmul(o_ps[32 * hd:32 * hd + VW, BLK - w:BLK], vs[:, j, k, hd * VW:(hd + 1) * VW],
                                     pr[:, u % NPR, hd, 0:w], start=k == 0, stop=k == 4 * h + 3)
                    i.then_inc(pv_done, 1)

                def group(j, first, more, more2):
                    e.wait_ge(mrow_loaded, 16)
                    take(e, (mrow_loaded, 16))
                    nxt, nxt2 = (j + 1) % NBUF, (j + 2) % NBUF
                    for s in range(len(steps)):
                        exponentials(s, first)
                        if s == MAXIMA and more:
                            maxima()
                        scores(j, s)
                        if s == MEND and more2:
                            e.wait_ge(stack_loaded[nxt2], LOADS)
                            take(e, (stack_loaded[nxt2], LOADS))
                        if more2 if s >= MEND else more:
                            for n in share[s]:
                                piece(nxt2 if s >= MEND else nxt, n)
                        if s % 2 and not (first and s < 2 * LAG):
                            products(j, s // 2 - LAG)
                    take(e, (exp_done, len(steps)), (masked, NDIAG))

                e.sem_inc(o_free, 1)
                e.sem_inc(m_free, MBUF)
                e.sem_inc(exp_done, 2)
                e.sem_inc(masked, masks_before(-1))
                e.wait_ge(consts_pe, 3)
                e.wait_ge(stack_loaded[0], LOADS)
                take(e, (stack_loaded[0], LOADS))
                e.sem_inc(first_here, 1)
                for n in range(NPC):
                    piece(0, n)
                maxima()
                e.wait_ge(later_stacks, 1)
                e.wait_ge(stack_loaded[1], LOADS)
                take(e, (stack_loaded[1], LOADS))
                for s in range(MEND, len(steps)):
                    for n in share[s]:
                        piece(1, n)
                group(0, True, True, True)
                with e.Fori(0, LOOPS):
                    for j in range(NBUF):
                        group((j + 1) % NBUF, False, True, True)
                for g in range(NBUF * LOOPS + 1, G):
                    group(g % NBUF, False, g + 1 < G, g + 2 < G)
                for s in range(2):
                    exponentials(s, False)
                for u in range(-LAG, 0):
                    products(G % NBUF, u)


class Chain:

    def __init__(self, eng, sem):
        self.eng, self.sem, self.n = eng, sem, 0

    def __call__(self, ins):
        ins.then_inc(self.sem, 1)
        self.n += 1
        self.eng.wait_ge(self.sem, self.n)

    def begin(self, ins):
        ins.then_inc(self.sem, 1)
        self.n += 1
        return self.n

    def done(self, n):
        self.eng.wait_ge(self.sem, n)

    def settle(self):
        self(self.eng.drain())

    def close(self):
        if self.n:
            take(self.eng, (self.sem, self.n))
        self.n = 0


def identity(e, step, ident):
    step(e.memset(ident[:], 0.0))
    step(e.affine_select(out=ident[:], in_=ident[:], compare_op=ALU.not_equal, fill=1.0, base=0,
                         pattern=[[-1, ident.shape[0]]], channel_multiplier=1))


def split_weights(e, step, wf, wh, wl):
    step(e.tensor_copy(wh[:], wf[:]))
    step(e.tensor_tensor(wl[:], wf[:], wh[:].bitcast(fp32), ALU.subtract))


def parts3(ah, al, bh, bl):
    return ((ah, bh), (ah, bl), (al, bh))


def product(e, out, lhs, rhs, n_k, first=True, last=True, **kw):
    terms = [(a(k), b(k)) for k in range(n_k) for a, b in parts3(lhs[0], lhs[1], rhs[0], rhs[1])]
    for n, (a, b) in enumerate(terms):
        i = e.matmul(out, a, b, start=first and n == 0, stop=last and n == len(terms) - 1, **kw)
    return i


def variance(e, step, src, st, mv, ve, var_ready):
    for t in range(TPB):
        e.bn_stats(st[:, t], src[:, t])
    step.settle()
    for t in range(TPB):
        e.bn_aggr(mv[:, t], st[:, t])
    step.settle()
    e.tensor_scalar(ve[:], mv[:, :, 1], EPS, None, ALU.add).then_inc(var_ready, 1)


def scaling(e, mv, rs, nmr, rstd_ready, signal):
    e.wait_ge(rstd_ready, 1)
    e.scalar_tensor_tensor(nmr[:], mv[:, :, 0], -1.0, rs[:], ALU.mult, ALU.mult).then_inc(signal, 1)
    take(e, (rstd_ready, 1))


def phase_project_route(nc, layer, o_d, x_d, wp_d, rw_d, rb_d, yb_d, xo_d, xh_d, xl_d, xg_d, rt_d):
    E, K, NB = (E0, K0, E0) if layer == 0 else (E1, K1, 1)
    with Phase(nc, f"prj{layer}") as ph:
        wf = ph.sb("wf", [P, KC, C + E])
        wh = ph.sb("wh", [P, KC, C + E], f32r)
        wl = ph.sb("wl", [P, KC, C + E], f32r)
        rbias = ph.sb("rbias", [P, NB])
        ident = ph.sb("ident", [P, P])
        mhalf = ph.sb("mhalf", [P, TPB])
        o = ph.sb("o", [P, 2, NG, BLK])
        x = ph.sb("x", [P, 2, TPB, C])
        den = ph.sb("den", [P, NH])
        rden = ph.sb("rden", [P, TPB, NH])
        att = ph.sb("att", [P, TPB, C])
        ah = ph.sb("ah", [P, KC, BLK], f32r)
        al = ph.sb("al", [P, KC, BLK], f32r)
        st = ph.sb("st", [P, 2, TPB, 6])
        mv = ph.sb("mv", [P, 2, TPB, 2])
        ve = ph.sb("ve", [P, 2, TPB])
        rs = ph.sb("rs", [P, 2, TPB])
        nmr = ph.sb("nmr", [P, 2, TPB])
        yn = ph.sb("yn", [P, TPB, C])
        xo = ph.sb("xo", [P, 2, TPB, C])
        xn = ph.sb("xn", [P, 2, TPB, XW])
        xh = ph.sb("xh", [P, 2, KC, BLK], f32r)
        xl = ph.sb("xl", [P, 2, KC, BLK], f32r)
        sc = ph.sb("sc", [P, TPB, E])
        sb = ph.sb("sb", [P, TPB, E + 8 - K])
        rep = ph.sb("rep", [P, TPB, E + 8 - K])
        top = ph.sb("top", [P, TPB, 8])
        pick = ph.sb("pick", [P, TPB, 8])
        mask = ph.sb("mask", [P, TPB, E])
        ssum = ph.sb("ssum", [P, TPB])
        rt = ph.sb("rt", [E, 2, BLK])
        o_ps = ph.ps("o_ps", [P, 2, NG, P])
        t_ps = ph.ps("t_ps", [P, KC, BLK])
        y_ps = ph.ps("y_ps", [P, TPB, C])
        l_ps = ph.ps("l_ps", [P, TPB, E])
        r_ps = ph.ps("r_ps", [E, BLK])
        if layer == 1:
            ybias = ph.sb("ybias", [P, C])
            y = ph.sb("y", [P, TPB, C])
            ls = ph.sb("ls", [P, TPB, E])
            lmax = ph.sb("lmax", [P, TPB])
            shifted = ph.sem("shifted")
        else:
            y = y_ps

        w_loaded = ph.sem("w_loaded")
        pe_consts = ph.sem("pe_consts")
        pool_chain = ph.sem("pool_chain")
        dve_chain = ph.sem("dve_chain")
        o_loaded = [ph.sem(f"o_loaded{j}") for j in range(2)]
        x_loaded = [ph.sem(f"x_loaded{j}") for j in range(2)]
        o_free = ph.sem("o_free")
        o_turned = ph.sem("o_turned")
        att_ready = ph.sem("att_ready")
        att_turned = ph.sem("att_turned")
        ah_ready = ph.sem("ah_ready")
        al_ready = ph.sem("al_ready")
        y_ready = ph.sem("y_ready")
        y_free = ph.sem("y_free")
        yvar_ready = ph.sem("yvar_ready")
        yrstd_ready = ph.sem("yrstd_ready")
        y_scale = ph.sem("y_scale")
        yn_ready = ph.sem("yn_ready")
        xo_ready = ph.sem("xo_ready")
        xvar_ready = ph.sem("xvar_ready")
        xrstd_ready = ph.sem("xrstd_ready")
        x_scale = ph.sem("x_scale")
        xn_ready = ph.sem("xn_ready")
        xn_turned = ph.sem("xn_turned")
        xh_ready = ph.sem("xh_ready")
        xl_ready = ph.sem("xl_ready")
        xhl_relayed = ph.sem("xhl_relayed")
        logits = ph.sem("logits")
        scores = ph.sem("scores")
        choice_ready = ph.sem("choice_ready")
        choice_turned = ph.sem("choice_turned")
        rt_ready = ph.sem("rt_ready")
        weights_ready = ph.sem("weights_ready")
        x_stored = [ph.sem(f"x_stored{j}") for j in range(2)]
        r_stored = [ph.sem(f"r_stored{j}") for j in range(2)]
        X_STORES = 16 * 3
        R_STORES = 16 * (2 if layer == 0 else 1)

        def tiles(d):
            return d.rearrange("(b j t p) c -> b j p t c", j=2, t=TPB, p=P)

        def turned(d):
            return d.rearrange("(b c p) (j t) -> b j p c t", b=B, p=P, j=2)

        o_rows = o_d.rearrange("(b g p) (j t) -> b j p g t", b=B, p=P, j=2)
        r_rows = rt_d.rearrange("e (b j t) -> b j e t", b=B, j=2)

        with nc.Block() as block:
            @block.sync
            def _(e):
                def load_o(b, j):
                    e.dma_start(o[:, j], o_rows[b, j]).then_inc(o_loaded[j], 16)

                def load_x(b, j):
                    e.dma_start(x[:, j], tiles(x_d)[b, j]).then_inc(x_loaded[j], 16)

                def stages(a, b, c, d):
                    if a is not None:
                        e.wait_ge(o_free, 1)
                        if not final(a):
                            load_o(a[0] + 1, a[1])
                        take(e, (o_free, 1))
                    if d is not None:
                        if layer == 0:
                            e.wait_ge(weights_ready, 1)
                            e.dma_start(tiles(xg_d[0:N])[d[0], d[1]], xn[:, d[1]]).then_inc(r_stored[d[1]], 16)
                            take(e, (weights_ready, 1))
                        e.wait_ge(rt_ready, 1)
                        e.dma_start(r_rows[d[0], d[1]], rt[:, d[1]]).then_inc(r_stored[d[1]], 16)
                        take(e, (rt_ready, 1))
                    if c is not None:
                        j = c[1]
                        e.wait_ge(xl_ready, 1)
                        e.sem_inc(xhl_relayed, 1)
                        e.dma_start(turned(xh_d)[c[0], j], xh[:, j].bitcast(fp32)).then_inc(x_stored[j], 16)
                        e.dma_start(turned(xl_d)[c[0], j], xl[:, j].bitcast(fp32)).then_inc(x_stored[j], 16)
                        e.dma_start(tiles(xo_d)[c[0], j], xo[:, j]).then_inc(x_stored[j], 16)
                        if a is not None:
                            load_x(a[0], a[1])
                        take(e, (xl_ready, 1))

                e.dma_start(wf[:, :, 0:C], wp_d).then_inc(w_loaded, 16)
                e.dma_start(wf[:, :, C:C + E], rw_d).then_inc(w_loaded, 16)
                e.dma_start(rbias[:], rb_d.rearrange("(o n) -> o n", o=1).broadcast_to((P, NB))).then_inc(w_loaded, 16)
                if layer == 1:
                    e.dma_start(ybias[:], yb_d.rearrange("(o n) -> o n", o=1).broadcast_to((P, C))
                                ).then_inc(w_loaded, 16)
                for j in range(2):
                    load_o(0, j)
                for j in range(2):
                    load_x(0, j)
                pipeline(e, stages, 4, peeled=1)

            @block.gpsimd
            def _(e):
                step = Chain(e, pool_chain)
                identity(e, step, ident)
                step(e.memset(mhalf[:], -0.5))
                e.sem_inc(pe_consts, 1)
                step.close()

                def stages(a, b, c, d):
                    if c is not None:
                        e.wait_ge(xvar_ready, 1)
                        e.tensor_tensor(rs[:, 1], ve[:, 1], mhalf[:], ALU.pow).then_inc(xrstd_ready, 1)
                        take(e, (xvar_ready, 1))
                    if b is not None:
                        e.wait_ge(yvar_ready, 1)
                        e.tensor_tensor(rs[:, 0], ve[:, 0], mhalf[:], ALU.pow).then_inc(yrstd_ready, 1)
                        j = b[1]
                        e.wait_ge(x_loaded[j], 16)
                        e.wait_ge(yn_ready, 1)
                        e.tensor_tensor(xo[:, j], x[:, j], yn[:], ALU.add).then_inc(xo_ready, 1)
                        take(e, (yvar_ready, 1), (x_loaded[j], 16), (yn_ready, 1))

                pipeline(e, stages, 4)

            @block.vector
            def _(e):
                step = Chain(e, dve_chain)
                e.wait_ge(w_loaded, 48 if layer == 0 else 64)
                split_weights(e, step, wf, wh, wl)
                step(e.memset(sb[:, :, E:E + 8 - K], 3e38))
                step(e.memset(pick[:, :, K:8], 3e38))
                e.sem_inc(pe_consts, 1)
                step.close()

                def residual(j):
                    e.wait_ge(xo_ready, 1)
                    variance(e, step, xo[:, j], st[:, 1], mv[:, 1], ve[:, 1], xvar_ready)
                    take(e, (xo_ready, 1))

                def projected():
                    e.wait_ge(y_ready, 1)
                    if layer == 1:
                        step(e.tensor_tensor(y[:], y_ps[:], ybias[:].unsqueeze(1).broadcast_to((P, TPB, C)), ALU.add))
                    variance(e, step, y, st[:, 0], mv[:, 0], ve[:, 0], yvar_ready)
                    take(e, (y_ready, 1))

                def divide():
                    for t in range(TPB):
                        e.wait_ge(o_turned, t + 1)
                        heads = o_ps[:, t % 2].rearrange("p g (h d) -> p (g h) d", d=32)
                        if layer == 0:
                            step(e.reciprocal(rden[:, t], heads[:, :, HD]))
                        else:
                            step(e.tensor_scalar(den[:], heads[:, :, HD], 1e-6, None, ALU.add))
                            step(e.reciprocal(rden[:, t], den[:]))
                        e.tensor_tensor(att[:, t].rearrange("p (h d) -> p h d", d=HD), heads[:, :, 0:HD],
                                        rden[:, t].unsqueeze(2).broadcast_to((P, NH, HD)), ALU.mult
                                        ).then_inc(att_ready, 1)
                    take(e, (o_turned, TPB))

                def softmax_shift():
                    e.wait_ge(logits, 1)
                    step(e.reduce_max(lmax[:], l_ps[:], AX.X))
                    e.tensor_tensor(ls[:], l_ps[:], lmax[:].unsqueeze(2).broadcast_to((P, TPB, E)), ALU.subtract
                                    ).then_inc(shifted, 1)
                    take(e, (logits, 1))

                def choose():
                    e.wait_ge(scores, 1)
                    if layer == 1:
                        step(e.reduce_sum(ssum[:], sc[:], AX.X))
                        step(e.reciprocal(ssum[:], ssum[:]))
                        step(e.tensor_tensor(sc[:], sc[:], ssum[:].unsqueeze(2).broadcast_to((P, TPB, E)), ALU.mult))
                    step(e.tensor_tensor(sb[:, :, 0:E], sc[:], rbias[:].unsqueeze(1).broadcast_to((P, TPB, E)),
                                         ALU.add))
                    for t in range(TPB):
                        e.max(top[:, t], sb[:, t, 0:E])
                    step.settle()
                    step(e.tensor_copy(pick[:, :, 0:K], top[:, :, 0:K]))
                    for t in range(TPB):
                        e.match_replace(rep[:, t], pick[:, t], sb[:, t], -3e38)
                    step.settle()
                    choice = e.tensor_scalar(mask[:], rep[:, :, 0:E], -1e38, None, ALU.is_lt)
                    if layer == 0:
                        choice.then_inc(choice_ready, 1)
                        step.settle()
                    else:
                        step(choice)
                    take(e, (scores, 1))

                def weigh(j):
                    step(e.tensor_tensor(sc[:], sc[:], mask[:], ALU.mult))
                    step(e.reduce_sum(ssum[:], sc[:], AX.X))
                    step(e.tensor_scalar(ssum[:], ssum[:], 1e-20, None, ALU.add))
                    step(e.reciprocal(ssum[:], ssum[:]))
                    weights = xn[:, j, :, C:XW] if layer == 0 else mask[:]
                    e.tensor_tensor(weights, sc[:], ssum[:].unsqueeze(2).broadcast_to((P, TPB, E)), ALU.mult
                                    ).then_inc(weights_ready if layer == 0 else choice_ready, 1)

                def stages(a, b, c, d):
                    if c is not None:
                        residual(c[1])
                    if b is not None:
                        projected()
                    if c is not None:
                        scaling(e, mv[:, 1], rs[:, 1], nmr[:, 1], xrstd_ready, x_scale)
                    if a is not None:
                        divide()
                    if layer == 1 and d is not None:
                        softmax_shift()
                    if b is not None:
                        scaling(e, mv[:, 0], rs[:, 0], nmr[:, 0], yrstd_ready, y_scale)
                    if d is not None:
                        choose()
                    if a is not None:
                        e.wait_ge(ah_ready, 1)
                        e.tensor_tensor(al[:], t_ps[:], ah[:].bitcast(fp32), ALU.subtract).then_inc(al_ready, 1)
                        take(e, (ah_ready, 1))
                    if d is not None:
                        weigh(d[1])
                    if c is not None:
                        e.wait_ge(xh_ready, 1)
                        e.tensor_tensor(xl[:, c[1]], t_ps[:], xh[:, c[1]].bitcast(fp32), ALU.subtract
                                        ).then_inc(xl_ready, 1)
                        take(e, (xh_ready, 1))
                    step.close()

                pipeline(e, stages, 4)

            @block.scalar
            def _(e):
                for j in range(2):
                    e.sem_inc(x_stored[j], X_STORES)
                    e.sem_inc(r_stored[j], R_STORES)

                def stages(a, b, c, d):
                    if c is not None:
                        j = c[1]
                        e.wait_ge(r_stored[j], R_STORES)
                        e.wait_ge(x_scale, 1)
                        for t in range(TPB):
                            e.activation(xn[:, j, t, 0:C], xo[:, j, t], ACT.Identity, bias=nmr[:, 1, t:t + 1],
                                         scale=rs[:, 1, t:t + 1]).then_inc(xn_ready, 1)
                        take(e, (r_stored[j], R_STORES), (x_scale, 1))
                    if d is not None:
                        if layer == 0:
                            e.wait_ge(logits, 1)
                            e.activation(sc[:], l_ps[:], ACT.Sigmoid).then_inc(scores, 1)
                            take(e, (logits, 1))
                        else:
                            e.wait_ge(shifted, 1)
                            e.activation(sc[:], ls[:], ACT.Exp).then_inc(scores, 1)
                            take(e, (shifted, 1))
                    if b is not None:
                        j = b[1]
                        e.wait_ge(x_stored[j], X_STORES)
                        e.wait_ge(y_scale, 1)
                        for t in range(TPB):
                            i = e.activation(yn[:, t], y[:, t], ACT.Identity, bias=nmr[:, 0, t:t + 1],
                                             scale=rs[:, 0, t:t + 1])
                        i.then_inc(yn_ready, 1)
                        e.drain().then_inc(y_free, 1)
                        take(e, (x_stored[j], X_STORES), (y_scale, 1))
                    if a is not None:
                        e.wait_ge(att_turned, 1)
                        e.activation(ah[:], t_ps[:], ACT.Copy).then_inc(ah_ready, 1)
                        take(e, (att_turned, 1))
                    if c is not None:
                        e.wait_ge(xn_turned, 1)
                        e.activation(xh[:, c[1]], t_ps[:], ACT.Copy).then_inc(xh_ready, 1)
                        take(e, (xn_turned, 1))
                    if d is not None:
                        e.wait_ge(choice_turned, 1)
                        e.activation(rt[:, d[1]], r_ps[:], ACT.Copy).then_inc(rt_ready, 1)
                        take(e, (choice_turned, 1))

                pipeline(e, stages, 4)
                for j in range(2):
                    e.wait_ge(x_stored[j], X_STORES)
                    e.wait_ge(r_stored[j], R_STORES)

            @block.tensor
            def _(e):
                e.wait_ge(pe_consts, 2)
                e.sem_inc(y_free, 1)

                def turn(src, ready):
                    for t in range(TPB):
                        e.wait_ge(ready, t + 1)
                        for k in range(KC):
                            i = e.transpose(t_ps[:, k, t * P:(t + 1) * P], src[:, t, k * P:(k + 1) * P], ident[:])
                    return i

                def stages(a, b, c, d):
                    if b is not None:
                        e.wait_ge(al_ready, 1)
                        e.wait_ge(y_free, 1)
                        for t in range(TPB):
                            cols = slice(t * P, (t + 1) * P)
                            i = product(e, y_ps[:, t], (lambda k: ah[:, k, cols], lambda k: al[:, k, cols]),
                                        (lambda k: wh[:, k, 0:C], lambda k: wl[:, k, 0:C]), KC)
                        i.then_inc(y_ready, 1)
                        take(e, (al_ready, 1), (y_free, 1))
                    if d is not None:
                        e.wait_ge(xhl_relayed, 1)
                        for t in range(TPB):
                            cols = slice(t * P, (t + 1) * P)
                            i = product(e, l_ps[:, t], (lambda k: xh[:, d[1], k, cols], lambda k: xl[:, d[1], k, cols]),
                                        (lambda k: wh[:, k, C:C + E], lambda k: wl[:, k, C:C + E]), KC)
                        i.then_inc(logits, 1)
                        take(e, (xhl_relayed, 1))
                    if a is not None:
                        e.wait_ge(o_loaded[a[1]], 16)
                        for t in range(TPB):
                            if t >= 2:
                                e.wait_ge(att_ready, t - 1)
                            for g in range(NG):
                                i = e.transpose(o_ps[:, t % 2, g], o[:, a[1], g, t * P:(t + 1) * P], ident[:])
                            i.then_inc(o_turned, 1)
                        take(e, (o_loaded[a[1]], 16))
                    if a is not None:
                        turn(att, att_ready).then_inc(att_turned, 1)
                        e.sem_inc(o_free, 1)
                        take(e, (att_ready, TPB))
                    if c is not None:
                        if a is not None:
                            e.wait_ge(al_ready, 1)
                        turn(xn[:, c[1]], xn_ready).then_inc(xn_turned, 1)
                        take(e, (xn_ready, TPB))
                    if d is not None:
                        e.wait_ge(choice_ready, 1)
                        for t in range(TPB):
                            i = e.transpose(r_ps[:, t * P:(t + 1) * P], mask[:, t], ident[:])
                        i.then_inc(choice_turned, 1)
                        take(e, (choice_ready, 1))

                pipeline(e, stages, 4)


DUMMY = CAP


def phase_shared_and_slots(nc, xh_d, xl_d, s1_d, s2_d, mt_d, acc0_d, acc1_d, xg_d, slots):
    HALF = N // 2
    ROUNDS = CAP // 8
    with Phase(nc, "shf") as ph:
        w1f = ph.sb("w1f", [P, KC, SF0])
        w1h = ph.sb("w1h", [P, KC, SF0], f32r)
        w1l = ph.sb("w1l", [P, KC, SF0], f32r)
        NF = SF0 // P
        w2f = ph.sb("w2f", [P, NF, C])
        w2h = ph.sb("w2h", [P, NF, C], f32r)
        w2l = ph.sb("w2l", [P, NF, C], f32r)
        xh = ph.sb("xh", [P, 2, KC, BLK], f32r)
        xl = ph.sb("xl", [P, 2, KC, BLK], f32r)
        hg = ph.sb("hg", [P, 2, NF, BLK])
        hh = ph.sb("hh", [P, 2, NF, BLK], f32r)
        hl = ph.sb("hl", [P, 2, NF, BLK], f32r)
        out = ph.sb("out", [P, 2, TPB, C])
        zero = ph.sb("zero", [P, 2048])
        key = ph.sb("key", [P, HALF])
        early = ph.sb("early", [P, HALF])
        val = ph.sb("val", [P, CAP])
        both = ph.sb("both", [E0, 2, CAP])
        first = ph.sb("first", [E0, CAP])
        slot_no = ph.sb("slot_no", [E0, CAP])
        ident = ph.sb("ident", [P, P])
        h_ps = ph.ps("h_ps", [P, NF, BLK])
        y_ps = ph.ps("y_ps", [P, TPB, C])
        i_ps = ph.ps("i_ps", [CAP, E0])

        w_loaded = ph.sem("w_loaded")
        w_split = ph.sem("w_split")
        pool_chain = ph.sem("pool_chain")
        dve_chain = ph.sem("dve_chain")
        loaded = [ph.sem(f"loaded{j}") for j in range(2)]
        zeros_ready = ph.sem("zeros_ready")
        zeros_stored = ph.sem("zeros_stored")
        iotas_ready = ph.sem("iotas_ready")
        choice_loaded = ph.sem("choice_loaded")
        moved = ph.sem("moved")
        local_ready = ph.sem("local_ready")
        list_ready = ph.sem("list_ready")
        list_turned = ph.sem("list_turned")
        h_ready = ph.sem("h_ready")
        h_free = ph.sem("h_free")
        x_free = ph.sem("x_free")
        hg_ready = ph.sem("hg_ready")
        gelu_done = ph.sem("gelu_done")
        hl_ready = ph.sem("hl_ready")
        y_ready = ph.sem("y_ready")
        out_ready = ph.sem("out_ready")
        y_free = ph.sem("y_free")
        stored = [ph.sem(f"stored{j}") for j in range(2)]

        def turned(d):
            return d.rearrange("(b c p) (j t) -> b j p c t", b=B, p=P, j=2)

        acc0_v = acc0_d[0:N].rearrange("(b j t p) c -> b j p t c", j=2, t=TPB, p=P)
        ZR = 2048 // C
        acc1_v = acc1_d[0:N].rearrange("(n p r) c -> n p (r c)", p=P, r=ZR)

        with nc.Block() as block:
            @block.sync
            def _(e):
                def load(b, j):
                    e.dma_start(xh[:, j].bitcast(fp32), turned(xh_d)[b, j]).then_inc(loaded[j], 16)
                    e.dma_start(xl[:, j].bitcast(fp32), turned(xl_d)[b, j]).then_inc(loaded[j], 16)

                def store(b, j):
                    e.wait_ge(out_ready, 1)
                    e.sem_inc(y_free, 1)
                    e.dma_start(acc0_v[b, j], out[:, j]).then_inc(stored[j], 16)
                    take(e, (out_ready, 1))

                e.dma_start(w1f[:], s1_d).then_inc(w_loaded, 16)
                e.dma_start(w2f[:], s2_d).then_inc(w_loaded, 16)
                for j in range(2):
                    load(0, j)

                def reload(b, j):
                    e.wait_ge(x_free, 1)
                    load(b + 1, j)
                    take(e, (x_free, 1))

                def blocks(first, last):
                    with e.Fori(first, last) as b:
                        reload(b, 0)
                        store(b - 1, 1)
                        reload(b, 1)
                        store(b, 0)

                MOVE = B - 2
                reload(0, 0)
                reload(0, 1)
                store(0, 0)
                blocks(1, MOVE)
                e.wait_ge(local_ready, 1)
                e.dma_start(both[:, 1], val[E0:P]).then_inc(moved, 16)
                blocks(MOVE, B - 1)
                store(B - 2, 1)
                for j in range(2):
                    store(B - 1, j)

            @block.gpsimd
            def _(e):
                step = Chain(e, pool_chain)
                identity(e, step, ident)
                step(e.memset(zero[:], 0.0))
                e.sem_inc(zeros_ready, 1)
                step(e.iota(early[:], [[-1, HALF]], base=HALF, channel_multiplier=0,
                            allow_small_or_imprecise_dtypes=True))
                e.sem_inc(iotas_ready, 1)
                step(e.iota(slot_no[:], [[1, CAP]], base=0, channel_multiplier=0,
                            allow_small_or_imprecise_dtypes=True))
                e.sem_inc(iotas_ready, 1)
                step.close()
                with e.Fori(0, B):
                    for j in range(2):
                        e.wait_ge(hg_ready, 1)
                        e.sem_inc(x_free, 1)
                        e.tensor_tensor(hl[:, j], hg[:, j], hh[:, j].bitcast(fp32), ALU.subtract
                                        ).then_inc(hl_ready, 1)
                        take(e, (hg_ready, 1))

            @block.vector
            def _(e):
                step = Chain(e, dve_chain)
                e.wait_ge(w_loaded, 32)
                split_weights(e, step, w1f, w1h, w1l)
                split_weights(e, step, w2f, w2h, w2l)
                e.sem_inc(w_split, 1)
                e.wait_ge(choice_loaded, 32)
                e.wait_ge(iotas_ready, 2)
                step(e.tensor_tensor(key[:], key[:], early[:], ALU.mult))

                def largest(dst, src):
                    for r in range(ROUNDS):
                        step(e.max(dst[:, 8 * r:8 * r + 8], src))
                        step(e.match_replace(src, dst[:, 8 * r:8 * r + 8], src, -1.0))

                largest(val[:], key[:])
                step(e.tensor_scalar(first[:], val[0:E0], 0.0, float(HALF), ALU.is_gt, ALU.mult))
                step(e.tensor_scalar(val[:], val[:], 0.0, None, ALU.max))
                step(e.tensor_tensor(both[:, 0], val[0:E0], first[:], ALU.add))
                e.sem_inc(local_ready, 1)
                e.wait_ge(moved, 16)
                largest(first[:], both[:].rearrange("e h c -> e (h c)"))
                step(e.tensor_scalar(first[:], first[:], 0.0, None, ALU.max))
                step(e.tensor_scalar(both[:, 0], first[:], 0.0, None, ALU.is_equal))
                step(e.tensor_tensor(both[:, 0], both[:, 0], slot_no[:], ALU.mult))
                step(e.tensor_scalar(first[:], first[:], -1.0, float(N), ALU.mult, ALU.add))
                e.tensor_tensor(first[:], first[:], both[:, 0], ALU.add).then_inc(list_ready, 1)
                e.wait_ge(list_turned, 1)
                step(e.tensor_copy(slots[:], i_ps[:]))

            @block.scalar
            def _(e):
                for h in range(2):
                    e.dma_start(key[h * E0:(h + 1) * E0], mt_d[:, h * HALF:(h + 1) * HALF]).then_inc(choice_loaded, 16)
                e.wait_ge(zeros_ready, 1)
                for n in range(N // (P * ZR)):
                    e.dma_start(acc1_v[n], zero[:]).then_inc(zeros_stored, 16)
                for d in (acc0_d, acc1_d):
                    e.dma_start(d[N:N + DUMMY], zero[0:DUMMY, 0:C]).then_inc(zeros_stored, 16)
                e.dma_start(xg_d[N:N + DUMMY], zero[0:DUMMY, 0:XW]).then_inc(zeros_stored, 16)
                for j in range(2):
                    e.sem_inc(stored[j], 16)

                def hidden(j):
                    for f in range(NF):
                        e.wait_ge(h_ready, f + 1)
                        e.activation(hg[:, j, f], h_ps[:, f], ACT.Gelu_apprx_tanh).then_inc(h_free, 1)
                    e.drain().then_inc(gelu_done, 1)
                    e.wait_ge(gelu_done, 1)
                    e.activation(hh[:, j], hg[:, j], ACT.Copy).then_inc(hg_ready, 1)
                    take(e, (h_ready, NF), (gelu_done, 1))

                def output(j):
                    e.wait_ge(stored[j], 16)
                    e.wait_ge(y_ready, 1)
                    e.activation(out[:, j], y_ps[:], ACT.Copy).then_inc(out_ready, 1)
                    take(e, (stored[j], 16), (y_ready, 1))

                hidden(0)
                hidden(1)
                output(0)
                with e.Fori(1, B):
                    for j in range(2):
                        hidden(j)
                        output(1 - j)
                output(1)
                for j in range(2):
                    e.wait_ge(stored[j], 16)
                e.wait_ge(zeros_stored, 16 * (N // (P * ZR) + 3))

            @block.tensor
            def _(e):
                def hidden(j):
                    e.wait_ge(loaded[j], 32)
                    for f in range(NF):
                        e.wait_ge(h_free, f + 1)
                        cols = slice(f * P, (f + 1) * P)
                        product(e, h_ps[:, f], (lambda k: w1h[:, k, cols], lambda k: w1l[:, k, cols]),
                                (lambda k: xh[:, j, k], lambda k: xl[:, j, k]), KC).then_inc(h_ready, 1)
                    take(e, (loaded[j], 32), (h_free, NF))

                def output(j):
                    e.wait_ge(hl_ready, 1)
                    e.wait_ge(y_free, 1)
                    for t in range(TPB):
                        cols = slice(t * P, (t + 1) * P)
                        i = product(e, y_ps[:, t], (lambda k: hh[:, j, k, cols], lambda k: hl[:, j, k, cols]),
                                    (lambda k: w2h[:, k], lambda k: w2l[:, k]), NF)
                    i.then_inc(y_ready, 1)
                    take(e, (hl_ready, 1), (y_free, 1))

                e.sem_inc(h_free, NF)
                e.sem_inc(y_free, 1)
                e.wait_ge(w_split, 1)
                hidden(0)
                hidden(1)
                output(0)
                with e.Fori(1, B):
                    for j in range(2):
                        hidden(j)
                        output(1 - j)
                output(1)
                e.wait_ge(list_ready, 1)
                e.transpose(i_ps[:], first[:], ident[0:E0, 0:E0]).then_inc(list_turned, 1)


def phase_experts(nc, slots, xg_d, w1_d, w2_d, acc0_d, acc1_d):
    PAIRS = E0 // 2
    SETS = 3
    NW = 2 * SETS
    LOOPS = (PAIRS - 2) // SETS
    assert 1 + LOOPS * SETS + 1 == PAIRS
    with Phase(nc, "exp") as ph:
        cur = [ph.sb(f"cur{j}", [CAP, 1], i32) for j in range(NW)]
        xs = ph.sb("xs", [CAP, NW, XW])
        xt = ph.sb("xt", [P, 2, KC, CAP])
        w1 = ph.sb("w1", [P, NW, KC, F0])
        w2 = ph.sb("w2", [P, NW, C])
        h = ph.sb("h", [P, 2, CAP])
        y = ph.sb("y", [CAP, NW, C])
        ident = ph.sb("ident", [P, P])
        t_ps = ph.ps("t_ps", [P, 2, BLK])
        h_ps = ph.ps("h_ps", [P, 2, BLK])
        y_ps = ph.ps("y_ps", [CAP, 2, BLK])

        pool_chain = ph.sem("pool_chain")
        ident_ready = ph.sem("ident_ready")
        w_loaded = [ph.sem(f"w_loaded{j}") for j in range(NW)]
        w_free = ph.sem("w_free")
        gathered = [ph.sem(f"gathered{j}") for j in range(NW)]
        x_turned = ph.sem("x_turned")
        xt_ready = ph.sem("xt_ready")
        h_ready = ph.sem("h_ready")
        gelu_ready = ph.sem("gelu_ready")
        y_ready = ph.sem("y_ready")
        out_ready = ph.sem("out_ready")
        added = [ph.sem(f"added{j}") for j in range(2)]
        accs = (acc0_d, acc1_d)

        def pairs(e, pair):
            pair(0, 0, 0)
            with e.Fori(0, LOOPS) as i:
                for n in range(1, SETS + 1):
                    pair(i * SETS + n, n % SETS, i + n // SETS)
            pair(PAIRS - 1, (PAIRS - 1) % SETS, (PAIRS - 1) // SETS)

        with nc.Block() as block:
            @block.sync
            def _(e):
                def load(expert, buf):
                    e.wait_ge(w_free, 1)
                    e.dma_start(w1[:, buf], w1_d.rearrange("e (k p) f -> e p k f", p=P)[expert]
                                ).then_inc(w_loaded[buf], 16)
                    e.dma_start(w2[:, buf], w2_d[expert]).then_inc(w_loaded[buf], 16)
                    take(e, (w_free, 1))

                e.sem_inc(w_free, NW)
                with e.Fori(0, E0 // NW) as i:
                    for j in range(NW):
                        load(i * NW + j, j)
                for j in range(E0 % NW):
                    load(E0 // NW * NW + j, j)

            @block.gpsimd
            def _(e):
                step = Chain(e, pool_chain)
                identity(e, step, ident)
                e.sem_inc(ident_ready, 1)

                def gather(n, s):
                    for j in range(2):
                        step(e.tensor_copy(cur[2 * s + j][:], slots[:, bass.ds(n * 2 + j, 1)]))
                    for j in range(2):
                        b = 2 * s + j
                        e.indirect_dma_start(xs[:, b], None, xg_d, bass.IndirectOffsetOnAxis(ap=cur[b][:], axis=0)
                                             ).then_inc(gathered[b], 16)

                def pair(n, s, turn):
                    if not (isinstance(n, int) and n == PAIRS - 1):
                        gather(n + 1, (s + 1) % SETS)
                    for j in range(2):
                        b = 2 * s + j
                        e.wait_ge(out_ready, 1)
                        if not (isinstance(n, int) and n == 0):
                            e.wait_ge(added[j], n * 16)
                        take(e, (out_ready, 1))
                        e.indirect_dma_start(accs[j], bass.IndirectOffsetOnAxis(ap=cur[b][:], axis=0), y[:, b], None,
                                             compute_op=ALU.add).then_inc(added[j], 16)
                    step.close()

                gather(0, 0)
                pairs(e, pair)
                for j in range(2):
                    e.wait_ge(added[j], 16 * PAIRS)

            @block.vector
            def _(e):
                def pair(n, s, turn):
                    for j in range(2):
                        e.wait_ge(x_turned, j + 1)
                        e.tensor_copy(xt[:, j], t_ps[:, j, 0:KC * CAP].rearrange("p (k c) -> p k c", k=KC)
                                      ).then_inc(xt_ready, 1)
                    for j in range(2):
                        e.wait_ge(y_ready, j + 1)
                        e.tensor_scalar(y[:, 2 * s + j], y_ps[:, j, 0:C], xs[:, 2 * s + j, bass.ds(n * 2 + j + C, 1)],
                                        None, ALU.mult).then_inc(out_ready, 1)
                    take(e, (x_turned, 2), (y_ready, 2))

                pairs(e, pair)

            @block.scalar
            def _(e):
                def pair(n, s, turn):
                    for j in range(2):
                        e.wait_ge(h_ready, j + 1)
                        e.activation(h[:, j], h_ps[:, j, 0:CAP], ACT.Gelu_apprx_tanh).then_inc(gelu_ready, 1)
                    take(e, (h_ready, 2))

                pairs(e, pair)

            @block.tensor
            def _(e):
                def pair(n, s, turn):
                    for j in range(2):
                        e.wait_ge(gathered[2 * s + j], turn * 16 + 16)
                        for k in range(KC):
                            i = e.transpose(t_ps[:, j, k * CAP:(k + 1) * CAP], xs[:, 2 * s + j, k * P:(k + 1) * P],
                                            ident[0:CAP, 0:CAP])
                        i.then_inc(x_turned, 1)
                    for j in range(2):
                        b = 2 * s + j
                        e.wait_ge(xt_ready, j + 1)
                        e.wait_ge(w_loaded[b], 32)
                        for k in range(KC):
                            i = e.matmul(h_ps[:, j, 0:CAP], w1[:, b, k], xt[:, j, k], start=k == 0, stop=k == KC - 1)
                        i.then_inc(h_ready, 1)
                    for j in range(2):
                        b = 2 * s + j
                        e.wait_ge(gelu_ready, j + 1)
                        e.matmul(y_ps[:, j, 0:C], h[:, j], w2[:, b], start=True, stop=True).then_inc(y_ready, 1)
                        take(e, (w_loaded[b], 32))
                    take(e, (xt_ready, 2), (gelu_ready, 2))
                    e.drain().then_inc(w_free, 2)

                e.wait_ge(ident_ready, 1)
                pairs(e, pair)


def phase_linear_qkv(nc, x1_d, acc0_d, acc1_d, w_d, bqk_d, bv_d, x2_d, fq_d, fqh_d, fql_d, fkh_d, fkl_d, fkt_d, v_d):
    FE = 1e-4
    with Phase(nc, "lqk") as ph:
        wf = ph.sb("wf", [P, KC, 3 * C])
        wh = ph.sb("wh", [P, KC, 3 * C], f32r)
        wl = ph.sb("wl", [P, KC, 3 * C], f32r)
        bqk = ph.sb("bqk", [P, 4])
        bqke = ph.sb("bqke", [P, 4])
        bv = ph.sb("bv", [P, C])
        ident = ph.sb("ident", [P, P])
        mhalf = ph.sb("mhalf", [P, TPB])
        x1 = ph.sb("x1", [P, 2, TPB, C])
        a0 = ph.sb("a0", [P, 2, TPB, C])
        a1 = ph.sb("a1", [P, 2, TPB, C])
        x2 = ph.sb("x2", [P, 2, TPB, C])
        yn = ph.sb("yn", [P, TPB, C])
        st = ph.sb("st", [P, 2, TPB, 6])
        mv = ph.sb("mv", [P, 2, TPB, 2])
        ve = ph.sb("ve", [P, 2, TPB])
        rs = ph.sb("rs", [P, 2, TPB])
        nmr = ph.sb("nmr", [P, 2, TPB])
        xn = ph.sb("xn", [P, TPB, C])
        xh = ph.sb("xh", [P, 2, KC, BLK], f32r)
        xl = ph.sb("xl", [P, 2, KC, BLK], f32r)
        ex = ph.sb("ex", [P, 4, BLK])
        re = ph.sb("re", [P, 4, BLK])
        phi = ph.sb("phi", [P, 2, 4, BLK])
        oh = ph.sb("oh", [P, 2, 4, BLK], f32r)
        ol = ph.sb("ol", [P, 2, 4, BLK], f32r)
        kt = ph.sb("kt", [P, 2, 2, TPB, P])
        vo = ph.sb("vo", [P, 2, TPB, NH, VW])
        t_ps = ph.ps("t_ps", [P, 2, BLK])
        qk = ph.ps("qk", [P, 4, BLK])
        vp = ph.ps("vp", [P, TPB, C])

        w_loaded = ph.sem("w_loaded")
        pe_consts = ph.sem("pe_consts")
        ones_ready = ph.sem("ones_ready")
        bias_ready = ph.sem("bias_ready")
        pool_chain = ph.sem("pool_chain")
        dve_chain = ph.sem("dve_chain")
        a_loaded = [ph.sem(f"a_loaded{j}") for j in range(2)]
        x_loaded = [ph.sem(f"x_loaded{j}") for j in range(2)]
        inputs_used = ph.sem("inputs_used")
        sum_ready = ph.sem("sum_ready")
        yvar_ready = ph.sem("yvar_ready")
        yrstd_ready = ph.sem("yrstd_ready")
        y_scale = ph.sem("y_scale")
        yn_ready = ph.sem("yn_ready")
        xvar_ready = ph.sem("xvar_ready")
        xrstd_ready = ph.sem("xrstd_ready")
        x_scale = ph.sem("x_scale")
        xn_ready = ph.sem("xn_ready")
        xn_turned = ph.sem("xn_turned")
        xh_ready = ph.sem("xh_ready")
        xl_ready = ph.sem("xl_ready")
        qk_ready = ph.sem("qk_ready")
        exp_ready = ph.sem("exp_ready")
        phi_done = ph.sem("phi_done")
        oh_ready = ph.sem("oh_ready")
        ol_ready = ph.sem("ol_ready")
        phi_relayed = ph.sem("phi_relayed")
        k_turned = ph.sem("k_turned")
        kt_ready = ph.sem("kt_ready")
        v_ready = ph.sem("v_ready")
        vo_ready = ph.sem("vo_ready")
        x2_stored = [ph.sem(f"x2_stored{j}") for j in range(2)]
        stored = [ph.sem(f"stored{j}") for j in range(2)]
        STORES = 16 * (1 + 2 + 4 + 2)

        def tiles(d):
            return d.rearrange("(b j t p) c -> b j p t c", j=2, t=TPB, p=P)

        def turned(d):
            return d.rearrange("(b c p) (j t) -> b j p c t", b=B, p=P, j=2)

        kt_v = fkt_d.rearrange("(b f j t p) c -> b j f p t c", b=B, f=2, j=2, t=TPB)
        v_v = v_d.rearrange("(b f j t p) c -> b j f p t c", b=B, f=2, j=2, t=TPB)

        with nc.Block() as block:
            @block.sync
            def _(e):
                def load(b, j):
                    e.dma_start(a0[:, j], tiles(acc0_d[0:N])[b, j]).then_inc(a_loaded[j], 16)
                    e.dma_start(a1[:, j], tiles(acc1_d[0:N])[b, j]).then_inc(a_loaded[j], 16)
                    e.dma_start(x1[:, j], tiles(x1_d)[b, j]).then_inc(x_loaded[j], 16)

                def stages(a, b, c):
                    if b is not None:
                        j = b[1]
                        e.wait_ge(inputs_used, 1)
                        e.dma_start(tiles(x2_d)[b[0], j], x2[:, j]).then_inc(x2_stored[j], 16)
                        if not final(b):
                            load(b[0] + 1, j)
                        take(e, (inputs_used, 1))
                    if c is not None:
                        j = c[1]
                        e.wait_ge(vo_ready, 1)
                        for f in range(2):
                            e.dma_start(v_v[c[0], j, f], vo[:, j, :, 8 * f:8 * f + 8].rearrange("p t h d -> p t (h d)")
                                        ).then_inc(stored[j], 16)
                        e.wait_ge(ol_ready, 4)
                        e.dma_start(turned(fq_d)[c[0], j], phi[:, j, 0:2]).then_inc(stored[j], 16)
                        for d, s, k in ((fqh_d, oh, 0), (fkh_d, oh, 2), (fql_d, ol, 0), (fkl_d, ol, 2)):
                            e.dma_start(turned(d)[c[0], j], s[:, j, k:k + 2].bitcast(fp32)).then_inc(stored[j], 16)
                        e.wait_ge(kt_ready, 1)
                        for f in range(2):
                            e.dma_start(kt_v[c[0], j, f], kt[:, j, f]).then_inc(stored[j], 16)
                        take(e, (vo_ready, 1), (ol_ready, 4), (kt_ready, 1))

                e.dma_start(wf[:], w_d).then_inc(w_loaded, 16)
                e.dma_start(bqk[:], bqk_d).then_inc(w_loaded, 16)
                e.dma_start(bv[:], bv_d.rearrange("(o n) -> o n", o=1).broadcast_to((P, C))).then_inc(w_loaded, 16)
                for j in range(2):
                    load(0, j)
                pipeline(e, stages, 3, peeled=1)

            @block.gpsimd
            def _(e):
                step = Chain(e, pool_chain)
                identity(e, step, ident)
                step(e.memset(mhalf[:], -0.5))
                e.sem_inc(pe_consts, 1)
                step(e.memset(vo[:].rearrange("p j t h d -> p (j t h) d")[:, :, HD:VW], 1.0))
                e.sem_inc(ones_ready, 1)
                step.close()

                def stages(a, b, c):
                    if a is not None:
                        j = a[1]
                        e.wait_ge(a_loaded[j], 32)
                        e.tensor_tensor(a0[:, j], a0[:, j], a1[:, j], ALU.add).then_inc(sum_ready, 1)
                        take(e, (a_loaded[j], 32))
                    if b is not None:
                        e.wait_ge(xvar_ready, 1)
                        e.tensor_tensor(rs[:, 1], ve[:, 1], mhalf[:], ALU.pow).then_inc(xrstd_ready, 1)
                        take(e, (xvar_ready, 1))
                    if a is not None:
                        e.wait_ge(yvar_ready, 1)
                        e.tensor_tensor(rs[:, 0], ve[:, 0], mhalf[:], ALU.pow).then_inc(yrstd_ready, 1)
                        take(e, (yvar_ready, 1))
                    if c is not None:
                        j = c[1]
                        for k in range(4):
                            e.wait_ge(oh_ready, k + 1)
                            e.tensor_tensor(ol[:, j, k], phi[:, j, k], oh[:, j, k].bitcast(fp32), ALU.subtract
                                            ).then_inc(ol_ready, 1)
                        take(e, (oh_ready, 4))

                pipeline(e, stages, 3)

            @block.vector
            def _(e):
                step = Chain(e, dve_chain)
                e.wait_ge(w_loaded, 48)
                step(e.tensor_scalar(wf[:, :, 0:C], wf[:, :, 0:C], HD ** -0.5, None, ALU.mult))
                step(e.tensor_scalar(bqk[:, 0:2], bqk[:, 0:2], HD ** -0.5, None, ALU.mult))
                step(e.tensor_scalar(bqke[:], bqk[:], FE, None, ALU.add))
                e.sem_inc(bias_ready, 1)
                split_weights(e, step, wf, wh, wl)
                e.sem_inc(pe_consts, 1)
                e.wait_ge(ones_ready, 1)
                step.close()

                def stages(a, b, c):
                    if b is not None:
                        j = b[1]
                        e.wait_ge(x_loaded[j], 16)
                        e.wait_ge(yn_ready, 1)
                        step(e.tensor_tensor(x2[:, j], x1[:, j], yn[:], ALU.add))
                        e.sem_inc(inputs_used, 1)
                        variance(e, step, x2[:, j], st[:, 1], mv[:, 1], ve[:, 1], xvar_ready)
                        take(e, (x_loaded[j], 16), (yn_ready, 1))
                    if a is not None:
                        e.wait_ge(sum_ready, 1)
                        variance(e, step, a0[:, a[1]], st[:, 0], mv[:, 0], ve[:, 0], yvar_ready)
                        take(e, (sum_ready, 1))
                    if b is not None:
                        scaling(e, mv[:, 1], rs[:, 1], nmr[:, 1], xrstd_ready, x_scale)
                    if a is not None:
                        scaling(e, mv[:, 0], rs[:, 0], nmr[:, 0], yrstd_ready, y_scale)
                    if c is not None:
                        j = c[1]
                        begun = []
                        for k in range(5):
                            if k < 4:
                                e.wait_ge(exp_ready, k + 1)
                                begun.append(step.begin(e.tensor_scalar(re[:, k], qk[:, k], bqke[:, k:k + 1], FE,
                                                                        ALU.add, ALU.max)))
                            if k:
                                step.done(begun[k - 1])
                                e.scalar_tensor_tensor(phi[:, j, k - 1], ex[:, k - 1], 1.0, re[:, k - 1], ALU.min,
                                                       ALU.add).then_inc(phi_done, 1)
                        e.wait_ge(v_ready, 1)
                        e.tensor_tensor(vo[:, j, :, :, 0:HD], vp[:].rearrange("p t (h d) -> p t h d", d=HD),
                                        bv[:].rearrange("p (h d) -> p h d", d=HD).unsqueeze(1)
                                        .broadcast_to((P, TPB, NH, HD)), ALU.add).then_inc(vo_ready, 1)
                        take(e, (exp_ready, 4), (v_ready, 1))
                    if b is not None:
                        e.wait_ge(xh_ready, 1)
                        e.tensor_tensor(xl[:, b[1]], t_ps[:], xh[:, b[1]].bitcast(fp32), ALU.subtract
                                        ).then_inc(xl_ready, 1)
                        take(e, (xh_ready, 1))
                    step.close()

                pipeline(e, stages, 3)

            @block.scalar
            def _(e):
                e.wait_ge(bias_ready, 1)
                for j in range(2):
                    e.sem_inc(x2_stored[j], 16)
                    e.sem_inc(stored[j], STORES)

                def exponential(k):
                    e.wait_ge(qk_ready, k + 1)
                    e.activation(ex[:, k], qk[:, k], ACT.Exp, bias=bqk[:, k:k + 1]).then_inc(exp_ready, 1)

                def high(j, k):
                    e.wait_ge(phi_done, k + 1)
                    e.activation(oh[:, j, k], phi[:, j, k], ACT.Copy).then_inc(oh_ready, 1)

                def stages(a, b, c):
                    if c is not None:
                        e.wait_ge(stored[c[1]], STORES)
                        take(e, (stored[c[1]], STORES))
                        for k in range(2):
                            exponential(k)
                    if b is not None:
                        e.wait_ge(x_scale, 1)
                        for t in range(TPB):
                            e.activation(xn[:, t], x2[:, b[1], t], ACT.Identity, bias=nmr[:, 1, t:t + 1],
                                         scale=rs[:, 1, t:t + 1]).then_inc(xn_ready, 1)
                        take(e, (x_scale, 1))
                    if c is not None:
                        exponential(2)
                        exponential(3)
                    if a is not None:
                        j = a[1]
                        e.wait_ge(x2_stored[j], 16)
                        e.wait_ge(y_scale, 1)
                        for t in range(TPB):
                            i = e.activation(yn[:, t], a0[:, j, t], ACT.Identity, bias=nmr[:, 0, t:t + 1],
                                             scale=rs[:, 0, t:t + 1])
                        i.then_inc(yn_ready, 1)
                        take(e, (x2_stored[j], 16), (y_scale, 1))
                    if c is not None:
                        high(c[1], 0)
                        high(c[1], 1)
                    if b is not None:
                        e.wait_ge(xn_turned, 1)
                        e.activation(xh[:, b[1]], t_ps[:], ACT.Copy).then_inc(xh_ready, 1)
                        take(e, (xn_turned, 1))
                    if c is not None:
                        high(c[1], 2)
                        high(c[1], 3)
                        e.sem_inc(phi_relayed, 1)
                        e.wait_ge(k_turned, 1)
                        e.activation(kt[:, c[1]], t_ps[:].rearrange("p f (t c) -> p f t c", t=TPB), ACT.Copy
                                     ).then_inc(kt_ready, 1)
                        take(e, (qk_ready, 4), (phi_done, 4), (k_turned, 1))

                pipeline(e, stages, 3)
                for j in range(2):
                    e.wait_ge(x2_stored[j], 16)
                    e.wait_ge(stored[j], STORES)

            @block.tensor
            def _(e):
                e.wait_ge(pe_consts, 2)

                def stages(a, b, c):
                    if c is not None:
                        j = c[1]
                        e.wait_ge(xl_ready, 1)
                        for k in range(4):
                            cols = slice(k * P, (k + 1) * P)
                            product(e, qk[:, k], (lambda k: wh[:, k, cols], lambda k: wl[:, k, cols]),
                                    (lambda k: xh[:, j, k], lambda k: xl[:, j, k]), KC).then_inc(qk_ready, 1)
                        take(e, (xl_ready, 1))
                    if b is not None:
                        for t in range(TPB):
                            e.wait_ge(xn_ready, t + 1)
                            for k in range(KC):
                                i = e.transpose(t_ps[:, k, t * P:(t + 1) * P], xn[:, t, k * P:(k + 1) * P], ident[:])
                        i.then_inc(xn_turned, 1)
                        take(e, (xn_ready, TPB))
                    if c is not None:
                        for t in range(TPB):
                            cols = slice(t * P, (t + 1) * P)
                            i = product(e, vp[:, t], (lambda k: xh[:, j, k, cols], lambda k: xl[:, j, k, cols]),
                                        (lambda k: wh[:, k, 2 * C:3 * C], lambda k: wl[:, k, 2 * C:3 * C]), KC)
                        i.then_inc(v_ready, 1)
                    if c is not None:
                        if b is not None:
                            e.wait_ge(xl_ready, 1)
                        e.wait_ge(phi_relayed, 1)
                        for f in range(2):
                            for t in range(TPB):
                                i = e.transpose(t_ps[:, f, t * P:(t + 1) * P],
                                                phi[:, c[1], 2 + f, t * P:(t + 1) * P], ident[:])
                        i.then_inc(k_turned, 1)
                        take(e, (phi_relayed, 1))

                pipeline(e, stages, 3)


def phase_linear_attention(nc, fq_d, fqh_d, fql_d, fkh_d, fkl_d, fkt_d, v_d, o_d):
    G, F = 2 * B, 8
    NBUF = 2
    with Phase(nc, "lin") as ph:
        qx = [ph.sb(f"qx{n}", [P, NBUF, F, T], f32r) for n in ("h", "l")]
        kk = [ph.sb(f"kk{n}", [P, NBUF, T], f32r) for n in ("h", "l")]
        fq = ph.sb("fq", [P, NBUF, T])
        kt = ph.sb("kt", [P, NBUF, KB, P])
        vs = ph.sb("vs", [P, NBUF, KB, F * VW])
        am = ph.sb("am", [P, 2, F, P])
        tri = ph.sb("tri", [P, P])
        own = ph.sb("own", [P, F])
        state = ph.sb("state", [P, F, 32])
        ot = ph.sb("ot", [P, 2, BLK])
        a_ps = ph.ps("a_ps", [P, 2, F // 2, P])
        b_ps = ph.ps("b_ps", [P, 2, F // 2, P])
        o_ps = ph.ps("o_ps", [P, 2, BLK])
        s_ps = ph.ps("s_ps", [P, F, VW])

        zeroed = [ph.sem(f"zeroed{j}") for j in range(NBUF)]
        pool_chain = ph.sem("pool_chain")
        dve_chain = ph.sem("dve_chain")
        masks_ready = ph.sem("masks_ready")
        loaded = [ph.sem(f"loaded{j}") for j in range(NBUF)]
        a_ready = ph.sem("a_ready")
        am_ready = ph.sem("am_ready")
        s_ready = ph.sem("s_ready")
        state_ready = ph.sem("state_ready")
        o_ready = ph.sem("o_ready")
        ot_ready = ph.sem("ot_ready")
        o_free = ph.sem("o_free")
        ot_stored = ph.sem("ot_stored")
        LOADS = 16 * (2 * F + 5)
        scores = (a_ps, b_ps)

        rows = {n: d.rearrange("(g p) t -> g p t", p=P) for n, d in
                (("fq", fq_d), ("fqh", fqh_d), ("fql", fql_d), ("fkh", fkh_d), ("fkl", fkl_d))}
        kt_rows = fkt_d.rearrange("(g k p) c -> g p k c", k=KB, p=P)
        v_rows = v_d.rearrange("(g k p) c -> g p k c", k=KB, p=P)
        o_rows = o_d.rearrange("(g s p) (h t) -> g h p s t", s=2, p=P, h=2)

        with nc.Block() as block:
            @block.sync
            def _(e):
                def load_queries(g, j):
                    for dst, name in ((qx[0], "fqh"), (qx[1], "fql")):
                        for h in range(F):
                            e.dma_start(dst[h * HD:(h + 1) * HD, j, h].bitcast(fp32),
                                        rows[name][g, h * HD:(h + 1) * HD]).then_inc(loaded[j], 16)

                def load(g, j):
                    e.dma_start(kk[0][:, j].bitcast(fp32), rows["fkh"][g]).then_inc(loaded[j], 16)
                    e.dma_start(kk[1][:, j].bitcast(fp32), rows["fkl"][g]).then_inc(loaded[j], 16)
                    e.dma_start(fq[:, j], rows["fq"][g]).then_inc(loaded[j], 16)
                    e.dma_start(kt[:, j], kt_rows[g]).then_inc(loaded[j], 16)
                    e.dma_start(vs[:, j], v_rows[g]).then_inc(loaded[j], 16)

                def outputs(g):
                    for h in range(2):
                        e.wait_ge(ot_ready, h + 1)
                        e.sem_inc(o_free, 1)
                        e.dma_start(o_rows[g, h], ot[:]).then_inc(ot_stored, 16)
                    take(e, (ot_ready, 2))

                load(0, 0)
                for j in range(NBUF):
                    e.wait_ge(zeroed[j], 2)
                    load_queries(j, j)
                    if j + 1 < NBUF:
                        load(j + 1, j + 1)
                with e.Fori(0, G // NBUF - 1) as i:
                    for j in range(NBUF):
                        outputs(NBUF * i + j)
                        load_queries(NBUF * i + j + NBUF, j)
                        load(NBUF * i + j + NBUF, j)
                outputs(G - 2)
                outputs(G - 1)

            @block.gpsimd
            def _(e):
                step = Chain(e, pool_chain)
                step(e.memset(qx[1][:, 0].bitcast(fp32), 0.0))
                e.sem_inc(zeroed[0], 1)
                step(e.memset(tri[:], 1.0))
                step(e.affine_select(out=tri[:], in_=tri[:], compare_op=ALU.is_ge, fill=0.0, base=0,
                                     pattern=[[1, P]], channel_multiplier=-1))
                step(e.memset(own[:], 1.0))
                step(e.affine_select(out=own[:], in_=own[:], compare_op=ALU.is_ge, fill=0.0, base=0,
                                     pattern=[[-HD, F]], channel_multiplier=1))
                step(e.affine_select(out=own[:], in_=own[:], compare_op=ALU.is_ge, fill=0.0, base=HD - 1,
                                     pattern=[[HD, F]], channel_multiplier=-1))
                e.sem_inc(masks_ready, 1)
                step(e.memset(qx[1][:, 1].bitcast(fp32), 0.0))
                e.sem_inc(zeroed[1], 1)

            @block.vector
            def _(e):
                step = Chain(e, dve_chain)
                for j in range(NBUF):
                    step(e.memset(qx[0][:, j].bitcast(fp32), 0.0))
                    e.sem_inc(zeroed[j], 1)
                e.wait_ge(masks_ready, 1)
                step.close()
                with e.Fori(0, G):
                    step(e.memset(state[:], 0.0))
                    e.sem_inc(state_ready, 1)
                    for c in range(KB):
                        e.wait_ge(a_ready, c + 1)
                        src = scores[c % 2][:].rearrange("p a h q -> p (a h) q")
                        e.tensor_tensor(am[:, c % 2], src, tri[:].unsqueeze(1).broadcast_to((P, F, P)), ALU.mult
                                        ).then_inc(am_ready, 1)
                        if c < KB - 1:
                            e.wait_ge(s_ready, c + 1)
                            e.tensor_tensor(state[:, :, 0:VW], s_ps[:], own[:].unsqueeze(2)
                                            .broadcast_to((P, F, VW)), ALU.mult).then_inc(state_ready, 1)
                    e.wait_ge(s_ready, KB)
                    take(e, (a_ready, KB), (s_ready, KB))
                    step.close()

            @block.scalar
            def _(e):
                e.sem_inc(ot_stored, 16)
                with e.Fori(0, 2 * G):
                    e.wait_ge(o_ready, 1)
                    e.wait_ge(ot_stored, 16)
                    e.activation(ot[:], o_ps[:], ACT.Copy).then_inc(ot_ready, 1)
                    take(e, (o_ready, 1), (ot_stored, 16))
                e.wait_ge(ot_stored, 16)

            @block.tensor
            def _(e):
                def chunk_scores(j, c):
                    cols = slice(c * P, (c + 1) * P)
                    for s in range(2):
                        heads = slice(4 * s, 4 * s + 4)
                        i = product(e, scores[c % 2][:, s],
                                    (lambda _: kk[0][:, j, cols], lambda _: kk[1][:, j, cols]),
                                    (lambda _: qx[0][:, j, heads, cols], lambda _: qx[1][:, j, heads, cols]), 1)
                    i.then_inc(a_ready, 1)

                def chunk_outputs(j, c):
                    cols = slice(c * P, (c + 1) * P)
                    oc = slice((c % TPB) * P, (c % TPB + 1) * P)
                    if c % TPB == 0:
                        e.wait_ge(o_free, 1)
                        take(e, (o_free, 1))
                    e.wait_ge(state_ready, c + 1)
                    for s in range(2):
                        e.matmul(o_ps[:, s, oc], state[:, 4 * s:4 * s + 4].rearrange("p h d -> p (h d)"),
                                 fq[:, j, cols], start=True, stop=False, skip_group_check=True)
                    e.matmul(s_ps[:].rearrange("p h d -> p (h d)"), kt[:, j, c], vs[:, j, c], start=c == 0,
                             stop=True, skip_group_check=True).then_inc(s_ready, 1)
                    e.wait_ge(am_ready, c + 1)
                    for s in range(2):
                        for h in range(4):
                            i = e.matmul(o_ps[32 * h:32 * h + VW, s, oc],
                                         vs[:, j, c, (4 * s + h) * VW:(4 * s + h + 1) * VW],
                                         am[:, c % 2, 4 * s + h], start=False, stop=True, skip_group_check=True)
                    if c % TPB == TPB - 1:
                        i.then_inc(o_ready, 1)

                e.sem_inc(o_free, 1)
                with e.Fori(0, G // NBUF):
                    for j in range(NBUF):
                        e.wait_ge(loaded[j], LOADS)
                        chunk_scores(j, 0)
                        for c in range(KB):
                            if c < KB - 1:
                                chunk_scores(j, c + 1)
                            chunk_outputs(j, c)
                        take(e, (loaded[j], LOADS), (am_ready, KB), (state_ready, KB))


def phase_gated_ffn(nc, xh_d, xl_d, x3_d, wt_d, weights, out_d):
    NCH = E1 + SF1 // P
    gw_d, sgw_d, uw_d, suw_d, dw_d, sdw_d = weights
    with Phase(nc, "ffn") as ph:
        raw = [ph.sb(f"raw{n}", [P, KC, NCH * P]) for n in ("g", "u", "d")]
        wh = [ph.sb(f"wh{n}", [P, KC, NCH * P], f32r) for n in ("g", "u", "d")]
        wl = [ph.sb(f"wl{n}", [P, KC, NCH * P], f32r) for n in ("g", "u", "d")]
        mhalf = ph.sb("mhalf", [P, TPB])
        xh = ph.sb("xh", [P, 2, KC, BLK], f32r)
        xl = ph.sb("xl", [P, 2, KC, BLK], f32r)
        wt = ph.sb("wt", [P, 2, E1, BLK])
        x3 = ph.sb("x3", [P, 2, TPB, C])
        gate = ph.sb("gate", [P, 2, BLK])
        hid = ph.sb("hid", [P, 2, BLK])
        hh = ph.sb("hh", [P, 3, BLK], f32r)
        hl = ph.sb("hl", [P, 3, BLK], f32r)
        st = ph.sb("st", [P, TPB, 6])
        mv = ph.sb("mv", [P, TPB, 2])
        ve = ph.sb("ve", [P, TPB])
        rs = ph.sb("rs", [P, TPB])
        nmr = ph.sb("nmr", [P, TPB])
        yn = ph.sb("yn", [P, 2, TPB, C])
        g_ps = ph.ps("g_ps", [P, 2, BLK])
        u_ps = ph.ps("u_ps", [P, 2, BLK])
        y_ps = ph.ps("y_ps", [P, 2, TPB, C])

        raw_loaded = [ph.sem(f"raw_loaded{n}") for n in range(3)]
        high_ready = ph.sem("high_ready")
        low_ready = ph.sem("low_ready")
        dve_chain = ph.sem("dve_chain")
        pow_ready = ph.sem("pow_ready")
        x_loaded = [ph.sem(f"x_loaded{j}") for j in range(2)]
        w_loaded = [ph.sem(f"w_loaded{j}") for j in range(2)]
        g_ready = ph.sem("g_ready")
        u_ready = ph.sem("u_ready")
        gate_ready = ph.sem("gate_ready")
        hid_ready = ph.sem("hid_ready")
        hh_ready = ph.sem("hh_ready")
        hl_ready = ph.sem("hl_ready")
        gu_free = ph.sem("gu_free")
        y_ready = ph.sem("y_ready")
        var_ready = ph.sem("var_ready")
        rstd_ready = ph.sem("rstd_ready")
        scale_ready = ph.sem("scale_ready")
        yn_ready = ph.sem("yn_ready")
        out_ready = ph.sem("out_ready")
        stored = [ph.sem(f"stored{j}") for j in range(2)]

        def tiles(d):
            return d.rearrange("(b j t p) c -> b j p t c", j=2, t=TPB, p=P)

        def turned(d):
            return d.rearrange("(b c p) (j t) -> b j p c t", b=B, p=P, j=2)

        wt_rows = wt_d.rearrange("e (b j t) -> b j e t", b=B, j=2)

        def down(a):
            return a[:].rearrange("p k (c f) -> p (k c f)", f=P).rearrange("p (c h) -> p c h", h=C)

        with nc.Block() as block:
            @block.sync
            def _(e):
                def load(b, j):
                    e.dma_start(xh[:, j].bitcast(fp32), turned(xh_d)[b, j]).then_inc(x_loaded[j], 16)
                    e.dma_start(xl[:, j].bitcast(fp32), turned(xl_d)[b, j]).then_inc(x_loaded[j], 16)
                    e.dma_start(wt[:, j], wt_rows[b, j].unsqueeze(0).broadcast_to((P, E1, BLK))
                                ).then_inc(w_loaded[j], 16)
                    e.dma_start(x3[:, j], tiles(x3_d)[b, j]).then_inc(w_loaded[j], 16)

                def store(b, j):
                    e.wait_ge(out_ready, 1)
                    e.dma_start(tiles(out_d)[b, j], yn[:, j]).then_inc(stored[j], 16)
                    take(e, (out_ready, 1))

                for n, (routed, shared) in enumerate(((gw_d, sgw_d), (uw_d, suw_d))):
                    e.dma_start(raw[n][:, :, 0:E1 * P], routed).then_inc(raw_loaded[n], 16)
                    e.dma_start(raw[n][:, :, E1 * P:], shared).then_inc(raw_loaded[n], 16)
                e.dma_start(down(raw[2])[:, 0:E1], dw_d).then_inc(raw_loaded[2], 16)
                e.dma_start(down(raw[2])[:, E1:], sdw_d).then_inc(raw_loaded[2], 16)
                for j in range(2):
                    load(0, j)
                with e.Fori(0, B - 1) as b:
                    for j in range(2):
                        store(b, j)
                        load(b + 1, j)
                for j in range(2):
                    store(B - 1, j)

            @block.gpsimd
            def _(e):
                e.memset(mhalf[:], -0.5).then_inc(pow_ready, 1)
                e.wait_ge(pow_ready, 1)
                with e.Fori(0, 2 * B):
                    e.wait_ge(var_ready, 1)
                    e.tensor_tensor(rs[:], ve[:], mhalf[:], ALU.pow).then_inc(rstd_ready, 1)
                    take(e, (var_ready, 1))

            @block.vector
            def _(e):
                step = Chain(e, dve_chain)
                for n in range(3):
                    e.wait_ge(high_ready, n + 1)
                    step(e.tensor_tensor(wl[n][:], raw[n][:], wh[n][:].bitcast(fp32), ALU.subtract))
                    e.sem_inc(low_ready, 1)
                step.close()

                def result(j, part):
                    if part == 0:
                        e.wait_ge(y_ready, 1)
                        variance(e, step, y_ps[:, j], st, mv, ve, var_ready)
                        take(e, (y_ready, 1))
                    elif part == 1:
                        scaling(e, mv, rs, nmr, rstd_ready, scale_ready)
                    else:
                        e.wait_ge(yn_ready, 1)
                        e.tensor_tensor(yn[:, j], yn[:, j], x3[:, j], ALU.add).then_inc(out_ready, 1)
                        take(e, (yn_ready, 1))

                def hidden(j, prev):
                    e.wait_ge(w_loaded[j], 32)
                    for c in range(NCH):
                        e.wait_ge(gate_ready, c + 1)
                        e.wait_ge(u_ready, c + 1)
                        product_ = e.tensor_tensor(hid[:, c % 2], gate[:, c % 2], u_ps[:, c % 2], ALU.mult)
                        if c < E1:
                            step(product_)
                            e.sem_inc(gu_free, 1)
                            e.tensor_tensor(hid[:, c % 2], hid[:, c % 2], wt[:, j, c], ALU.mult).then_inc(hid_ready, 1)
                        else:
                            product_.then_inc(hid_ready, 1)
                        e.wait_ge(hh_ready, c + 1)
                        if c >= E1:
                            e.sem_inc(gu_free, 1)
                        e.tensor_tensor(hl[:, c % 3], hid[:, c % 2], hh[:, c % 3].bitcast(fp32), ALU.subtract
                                        ).then_inc(hl_ready, 1)
                        if prev and c in (2, 3, 6):
                            result(1 - j, (2, 3, 6).index(c))
                    take(e, (w_loaded[j], 32), (gate_ready, NCH), (u_ready, NCH), (hh_ready, NCH))
                    step.close()

                hidden(0, False)
                hidden(1, True)
                with e.Fori(1, B):
                    for j in range(2):
                        hidden(j, True)
                for part in range(3):
                    result(1, part)
                step.close()

            @block.scalar
            def _(e):
                for n in range(3):
                    e.wait_ge(raw_loaded[n], 32)
                    e.activation(wh[n][:], raw[n][:], ACT.Copy).then_inc(high_ready, 1)
                for j in range(2):
                    e.sem_inc(stored[j], 16)

                def normalise(j):
                    e.wait_ge(stored[j], 16)
                    e.wait_ge(scale_ready, 1)
                    for t in range(TPB):
                        i = e.activation(yn[:, j, t], y_ps[:, j, t], ACT.Identity, bias=nmr[:, t:t + 1],
                                         scale=rs[:, t:t + 1])
                    i.then_inc(yn_ready, 1)
                    take(e, (stored[j], 16), (scale_ready, 1))

                def hidden(j, prev):
                    for c in range(NCH):
                        e.wait_ge(g_ready, c + 1)
                        e.activation(gate[:, c % 2], g_ps[:, c % 2], ACT.Silu).then_inc(gate_ready, 1)
                        e.wait_ge(hid_ready, c + 1)
                        e.activation(hh[:, c % 3], hid[:, c % 2], ACT.Copy).then_inc(hh_ready, 1)
                        if prev and c == 4:
                            normalise(1 - j)
                    take(e, (g_ready, NCH), (hid_ready, NCH))

                hidden(0, False)
                hidden(1, True)
                with e.Fori(1, B):
                    for j in range(2):
                        hidden(j, True)
                normalise(1)
                for j in range(2):
                    e.wait_ge(stored[j], 16)

            @block.tensor
            def _(e):
                def gate_up(j, c):
                    e.wait_ge(gu_free, c + 1)
                    cols = slice(c * P, (c + 1) * P)
                    for ps, n, ready in ((g_ps, 0, g_ready), (u_ps, 1, u_ready)):
                        product(e, ps[:, c % 2], (lambda k: wh[n][:, k, cols], lambda k: wl[n][:, k, cols]),
                                (lambda k: xh[:, j, k], lambda k: xl[:, j, k]), KC).then_inc(ready, 1)

                def down_product(j, c, wait):
                    e.wait_ge(hl_ready, wait)
                    for t in range(TPB):
                        cols = slice(t * P, (t + 1) * P)
                        i = product(e, y_ps[:, j, t], (lambda _: hh[:, c % 3, cols], lambda _: hl[:, c % 3, cols]),
                                    (lambda _: down(wh[2])[:, c], lambda _: down(wl[2])[:, c]), 1,
                                    first=c == 0 and t % 2 == 0, last=c == NCH - 1, skip_group_check=True)
                    return i

                def chunks(j, prev):
                    e.wait_ge(x_loaded[j], 32)
                    for c in range(NCH):
                        gate_up(j, c)
                        if c == 2 and not prev:
                            e.wait_ge(low_ready, 3)
                        if c >= 2:
                            down_product(j, c - 2, c + 1)
                        elif prev:
                            i = down_product(1 - j, NCH - 2 + c, c + 1)
                            if c == 1:
                                i.then_inc(y_ready, 1)
                    take(e, (x_loaded[j], 32), (gu_free, NCH), (hl_ready, NCH))

                e.wait_ge(low_ready, 2)
                e.sem_inc(gu_free, 2)
                e.sem_inc(hl_ready, 2)
                chunks(0, False)
                chunks(1, True)
                with e.Fori(1, B):
                    for j in range(2):
                        chunks(j, True)
                down_product(1, NCH - 2, 1)
                down_product(1, NCH - 1, 2).then_inc(y_ready, 1)


def build(nc, x, w_attn, w_proj, router0, bias0, w1, w2, sw1, sw2, w_qkv, bqk, bv, w_out, b_out, router1, bias1,
          gate, up, down, s_gate, s_up, s_down, out):
    def dram(name, *shape):
        return nc.dram_tensor(name, shape, fp32, kind="Internal").ap()

    features = (B * C, T)
    heads = (B * NG * P, T)
    qh, ql, kh, kl = (dram(n, *features) for n in ("q_high", "q_low", "k_high", "k_low"))
    v = dram("values", B * NG * T, GH * VW)
    o = dram("attended", *heads)
    x1 = dram("x1", N, C)
    x1h, x1l = dram("x1_high", *features), dram("x1_low", *features)
    rows = dram("expert_rows", N + DUMMY, XW)
    chosen = dram("chosen", E0, N)
    acc0, acc1 = dram("acc0", N + DUMMY, C), dram("acc1", N + DUMMY, C)
    x2 = dram("x2", N, C)
    fq = dram("phi_q", *features)
    fqh, fql, fkh, fkl = (dram(n, *features) for n in ("phi_q_high", "phi_q_low", "phi_k_high", "phi_k_low"))
    fkt = dram("phi_k_rows", 2 * N, P)
    v1 = dram("values1", 2 * N, P + 8)
    o1 = dram("attended1", *heads)
    x3 = dram("x3", N, C)
    x3h, x3l = dram("x3_high", *features), dram("x3_low", *features)
    weights = dram("weights", E1, N)

    phase_qkv(nc, x, w_attn, qh, ql, kh, kl, v)
    phase_softmax_attention(nc, qh, ql, kh, kl, v, o)
    phase_project_route(nc, 0, o, x, w_proj, router0, bias0, None, x1, x1h, x1l, rows, chosen)
    with nc.sbuf_tensor("slots", [CAP, E0], i32) as slots:
        phase_shared_and_slots(nc, x1h, x1l, sw1, sw2, chosen, acc0, acc1, rows, slots)
        phase_experts(nc, slots, rows, w1, w2, acc0, acc1)
    phase_linear_qkv(nc, x1, acc0, acc1, w_qkv, bqk, bv, x2, fq, fqh, fql, fkh, fkl, fkt, v1)
    phase_linear_attention(nc, fq, fqh, fql, fkh, fkl, fkt, v1, o1)
    phase_project_route(nc, 1, o1, x2, w_out, router1, bias1, b_out, x3, x3h, x3l, None, weights)
    phase_gated_ffn(nc, x3h, x3l, x3, weights, (gate, s_gate, up, s_up, down, s_down), out)


def kernel(**inputs):
    import numpy as np
    import concourse.bacc as bacc
    from concourse.bass_utils import run_bass_kernel_spmd

    def chunked(w):
        return w.reshape(-1, P, w.shape[-1]).transpose(1, 0, 2)

    def gated(w):
        return w.reshape(E1, KC, P, F1).transpose(2, 1, 0, 3).reshape(P, KC, E1 * F1)

    get = {n: np.asarray(a) for n, a in inputs.items()}
    laid = {
        "x": get["L0_attn_x"].reshape(N, C),
        "w_attn": chunked(get["L0_attn_w_attn"]),
        "w_proj": chunked(get["L0_attn_w_proj"]),
        "router0": chunked(get["L0_ffn_router_weight"].T),
        "bias0": get["L0_ffn_expert_bias"],
        "w1": get["L0_ffn_w1"],
        "w2": get["L0_ffn_w2"],
        "sw1": chunked(get["L0_ffn_sw1"].T),
        "sw2": chunked(get["L0_ffn_sw2"].T),
        "w_qkv": chunked(get["L1_attn_W_qkv"]),
        "bqk": get["L1_attn_b_qkv"][:2 * C].reshape(4, P).T,
        "bv": get["L1_attn_b_qkv"][2 * C:],
        "w_out": chunked(get["L1_attn_W_out"]),
        "b_out": get["L1_attn_b_out"],
        "router1": chunked(get["L1_ffn_router_w"]),
        "bias1": get["L1_ffn_router_bias"].reshape(1),
        "gate": gated(get["L1_ffn_gate_w"]),
        "up": gated(get["L1_ffn_up_w"]),
        "down": get["L1_ffn_down_w"].transpose(1, 0, 2),
        "s_gate": chunked(get["L1_ffn_s_gate_w"]),
        "s_up": chunked(get["L1_ffn_s_up_w"]),
        "s_down": chunked(get["L1_ffn_s_down_w"]),
    }
    laid = {n: np.ascontiguousarray(a) for n, a in laid.items()}
    nc = bacc.Bacc("TRN2", target_bir_lowering=False, num_devices=1)
    args = {n: nc.dram_tensor(n, a.shape, mybir.dt.from_np(a.dtype), kind="ExternalInput").ap()
            for n, a in laid.items()}
    out = nc.dram_tensor("out", (N, C), fp32, kind="ExternalOutput").ap()
    build(nc, *args.values(), out)
    r = run_bass_kernel_spmd(nc, [laid], core_ids=[0])
    return r.results[0]["out"].reshape(B, T, C)
```
